# Optimizing a Trainium2 kernel written in Bass

```python
import numpy as np
import jax
import jax.numpy as jnp

def _softmax(x, axis=-1):
    return jax.nn.softmax(x, axis=axis)

def _gelu(x):
    return jax.nn.gelu(x, approximate=True)

def _silu(x):
    return jax.nn.silu(x)

def _sigmoid(x):
    return jax.nn.sigmoid(x)

def _layernorm(x, axis=-1, eps=1e-05):
    m = jnp.mean(x, axis=axis, keepdims=True)
    v = jnp.var(x, axis=axis, keepdims=True)
    return (x - m) / jnp.sqrt(v + eps)

def _scatter_add(tgt, idx, src, axis=0):
    return tgt.at[idx].add(src)

def _segment_sum(src, seg, n):
    return jax.ops.segment_sum(src, seg, n)
kernel_name = 'mk_gnn_resnorm_d1_gnn_r64_6f6c1b'

def setup_inputs(seed: int=0):
    np.random.seed(seed)
    _w = jnp.asarray

    def _rec_inputs():
        import jax
        import jax.numpy as jnp
        _gk = jax.random.key(seed)
        x = -0.0002117 + 1 * jax.random.normal(jax.random.fold_in(_gk, 1), (100000, 256), jnp.float32)
        _s = jax.random.randint(jax.random.fold_in(_gk, 2), (12500,), 0, 100000, jnp.int32)
        _d = jax.random.randint(jax.random.fold_in(_gk, 3), (12500,), 0, 100000, jnp.int32)
        _loop = jnp.arange(100000, dtype=jnp.int32)
        src = jnp.concatenate([_s, _d, _loop])
        dst = jnp.concatenate([_d, _s, _loop])
        _o = jnp.argsort(dst, stable=True)
        src = src[_o]
        dst = dst[_o]
        return (x, src, dst)
    x, src, dst = _rec_inputs()

    def _L0_gnn_setup():
        import jax, jax.numpy as jnp
        import numpy as np
        N_NODES = 100000
        N_EDGES = 20000
        NNZ = 10000
        C = 256
        ATT_H = 128
        NS = 2
        EPS = 1e-05
        key = jax.random.key(seed)
        ks = jax.random.split(key, 16)
        x = jax.random.normal(ks[0], (N_NODES, C), jnp.float32)
        node_idx = jax.random.randint(ks[1], (NNZ,), 0, N_NODES, dtype=jnp.int64)
        edge_idx = jax.random.randint(ks[2], (NNZ,), 0, N_EDGES, dtype=jnp.int64)
        hyperedge_index = jnp.stack([node_idx, edge_idx])
        s = 1.0 / np.sqrt(C).astype(np.float32)
        sa = 1.0 / np.sqrt(ATT_H).astype(np.float32)
        return {'x': x, 'hyperedge_index': hyperedge_index, 'conv_W': jax.random.normal(ks[3], (NS, C, C), jnp.float32) * s, 'conv_b': jnp.zeros((NS, C), jnp.float32), 'tr_W': jax.random.normal(ks[4], (NS, C, C), jnp.float32) * s, 'tr_b': jnp.zeros((NS, C), jnp.float32), 'ln_g': jnp.ones((NS, C), jnp.float32), 'ln_b': jnp.zeros((NS, C), jnp.float32), 'scale_weights': jnp.ones((NS,), jnp.float32), 'attn_W1': jax.random.normal(ks[5], (C, ATT_H), jnp.float32) * s, 'attn_b1': jnp.zeros((ATT_H,), jnp.float32), 'attn_W2': jax.random.normal(ks[6], (ATT_H, NS), jnp.float32) * sa, 'attn_b2': jnp.zeros((NS,), jnp.float32)}
    _L0_gnn_all = _L0_gnn_setup()
    _L0_gnn_in = {k: v for k, v in _L0_gnn_all.items() if k in ('conv_W', 'conv_b', 'tr_W', 'tr_b', 'ln_g', 'ln_b', 'scale_weights', 'attn_W1', 'attn_b1', 'attn_W2', 'attn_b2')}
    del _L0_gnn_all
    return {'x': x, 'src': src, 'dst': dst, 'L0_gnn_conv_W': _L0_gnn_in['conv_W'], 'L0_gnn_conv_b': _L0_gnn_in['conv_b'], 'L0_gnn_tr_W': _L0_gnn_in['tr_W'], 'L0_gnn_tr_b': _L0_gnn_in['tr_b'], 'L0_gnn_ln_g': _L0_gnn_in['ln_g'], 'L0_gnn_ln_b': _L0_gnn_in['ln_b'], 'L0_gnn_scale_weights': _L0_gnn_in['scale_weights'], 'L0_gnn_attn_W1': _L0_gnn_in['attn_W1'], 'L0_gnn_attn_b1': _L0_gnn_in['attn_b1'], 'L0_gnn_attn_W2': _L0_gnn_in['attn_W2'], 'L0_gnn_attn_b2': _L0_gnn_in['attn_b2']}

def reference(x, src, dst, L0_gnn_conv_W, L0_gnn_conv_b, L0_gnn_tr_W, L0_gnn_tr_b, L0_gnn_ln_g, L0_gnn_ln_b, L0_gnn_scale_weights, L0_gnn_attn_W1, L0_gnn_attn_b1, L0_gnn_attn_W2, L0_gnn_attn_b2):
    import jax
    import jax.numpy as jnp

    def _L0_gnn_ref(x, hyperedge_index, conv_W, conv_b, tr_W, tr_b, ln_g, ln_b, scale_weights, attn_W1, attn_b1, attn_W2, attn_b2):
        import jax, jax.numpy as jnp
        import numpy as np
        N_NODES = 100000
        N_EDGES = 20000
        NNZ = 10000
        C = 256
        ATT_H = 128
        NS = 2
        EPS = 1e-05
        node_idx = hyperedge_index[0]
        edge_idx = hyperedge_index[1]
        ones = jnp.ones(node_idx.shape, x.dtype)
        deg_e = jax.ops.segment_sum(ones, edge_idx, num_segments=N_EDGES)
        Binv = jnp.where(deg_e > 0, 1.0 / deg_e, 0.0)
        deg_v = jax.ops.segment_sum(ones, node_idx, num_segments=N_NODES)
        Dinv = jnp.where(deg_v > 0, 1.0 / deg_v, 0.0)
        outs, trans = ([], [])
        for i in range(NS):
            xt = x @ conv_W[i]
            e_feat = jax.ops.segment_sum(xt[node_idx], edge_idx, num_segments=N_EDGES)
            e_feat = e_feat * Binv[:, None]
            out = jax.ops.segment_sum(e_feat[edge_idx], node_idx, num_segments=N_NODES)
            out = out * Dinv[:, None] + conv_b[i]
            outs.append(out)
            h = out @ tr_W[i] + tr_b[i]
            mu = jnp.mean(h, axis=-1, keepdims=True)
            var = jnp.var(h, axis=-1, keepdims=True)
            h = (h - mu) / jnp.sqrt(var + EPS) * ln_g[i] + ln_b[i]
            trans.append(jax.nn.relu(h))
        output_stack = jnp.stack(outs)
        transformed_stack = jnp.stack(trans)
        static_w = jax.nn.softmax(scale_weights, axis=0)
        node_features = jnp.mean(output_stack, axis=0)
        a = jax.nn.relu(node_features @ attn_W1 + attn_b1)
        a = jax.nn.softmax(a @ attn_W2 + attn_b2, axis=-1)
        dynamic_w = jnp.mean(a, axis=0)
        w = (static_w + dynamic_w) / 2.0
        return jnp.sum(transformed_stack * w[:, None, None], axis=0)
    edge_index = jnp.stack([src, dst])
    x = _layernorm(x + _L0_gnn_ref(x, edge_index, L0_gnn_conv_W, L0_gnn_conv_b, L0_gnn_tr_W, L0_gnn_tr_b, L0_gnn_ln_g, L0_gnn_ln_b, L0_gnn_scale_weights, L0_gnn_attn_W1, L0_gnn_attn_b1, L0_gnn_attn_W2, L0_gnn_attn_b2), axis=-1)
    return x

_drawn_inputs = setup_inputs


def setup_inputs(seed=0):
    import zlib

    import numpy as np

    out = dict(_drawn_inputs(seed))
    spreads = {'L0_gnn_conv_b': (0.0, 0.1),
     'L0_gnn_tr_b': (0.0, 0.1),
     'L0_gnn_ln_g': (1.0, 0.2),
     'L0_gnn_ln_b': (0.0, 0.1),
     'L0_gnn_scale_weights': (1.0, 0.2),
     'L0_gnn_attn_b1': (0.0, 0.1),
     'L0_gnn_attn_b2': (0.0, 0.1)}
    factors = {}
    for name, (base, spread) in spreads.items():
        noise = np.random.default_rng([zlib.crc32(name.encode()), seed]).standard_normal(out[name].shape)
        drawn = base * np.exp(spread * noise) if base else spread * noise
        out[name] = jnp.asarray(drawn.astype(out[name].dtype))
    for name, factor in factors.items():
        out[name] = (out[name] * factor).astype(out[name].dtype)
    return out
```

```python
from contextlib import ExitStack

import concourse.bass as bass
from concourse import mybir

P = 128
ALU = mybir.AluOpType
ACT = mybir.ActivationFunctionType
F32 = mybir.dt.float32
BF16 = mybir.dt.bfloat16
FP16 = mybir.dt.float16
I32 = mybir.dt.int32
AX = mybir.AxisListType.X

N_EDGES = 20000
EPS = 1e-5
ROW = 260
G = 2
UNROLL = 2
BODY = G * UNROLL


class Chain:

    def __init__(self, eng, sem, base=0):
        self.eng, self.sem, self.base, self.n = eng, sem, base, 0

    def __call__(self, instruction):
        instruction.then_inc(self.sem, 1)
        self.n += 1
        self.eng.wait_ge(self.sem, self.base + self.n)


def gnn_kernel(nc, x, src, dst, conv_W, conv_b, tr_W, tr_b, ln_g, ln_b, scale_w, attn_W1, attn_b1, attn_W2,
               attn_b2, out):
    N, C = x.shape
    E = src.shape[0]
    NS = conv_W.shape[0]
    H = attn_W1.shape[1]
    assert C == 2 * P and H == P and NS == 2
    K = C // P
    BATCHES = -(-E // P)
    TB = -(-BATCHES // P) * P
    HI = -(-N // P)
    LAST = N_EDGES - 1
    PAD = 1 << 17
    assert PAD > N and PAD // P > HI and TB >= BATCHES + 2 * BODY

    E_TRASH = N_EDGES
    E_COLS = -(-(N_EDGES + G * P) // P)
    S_TRASH = P * HI
    S_COMMON = S_TRASH + G * P
    LIST = -(-HI // 8) * 8
    TILES = LIST + 8
    T_ROWS = (1 + TILES) * P

    ZC = 23
    assert HI % ZC == 0
    FULL = N // (8 * P)
    REST = N - FULL * 8 * P
    REST_P = 112
    assert REST % REST_P == 0
    REST_R = REST // REST_P

    ctx = ExitStack()
    with ctx:
        def sb(name, shape, dt=F32):
            return ctx.enter_context(nc.sbuf_tensor(name, shape, dt))

        def sem(name):
            return ctx.enter_context(nc.semaphore(name))

        def dram(name, shape, dt=F32):
            return nc.dram_tensor(name, shape, dt, kind="Internal").ap()

        src_pad = dram("src_pad", [TB, P], I32)
        dst_pad = dram("dst_pad", [TB, P], I32)
        edge_sum = dram("edge_sum", [E_COLS * P, ROW])
        node_sum = dram("node_sum", [S_COMMON + P, ROW])
        transformed = dram("transformed", [T_ROWS, 2 * C])

        psum = [ctx.enter_context(nc.psum_tensor(f"bank{i}", [P, 512], F32)) for i in range(8)]

        ident = sb("ident", [P, P])
        ones = sb("ones", [P, P])
        ones3 = sb("ones3", [3, P], BF16)
        zeros_bf = sb("zeros_bf", [P, 512], BF16)
        iota_h = sb("iota_h", [P, HI], FP16)
        earlier = sb("earlier", [P, P])
        before = sb("before", [P, G, G, P])
        key_init = sb("key_init", [P, HI])
        part = sb("part", [P, 1])
        eps_t = sb("eps_t", [P, 1])
        own_hi = sb("own_hi", [P, TB])
        own_lo = sb("own_lo", [P, TB])
        is_live = sb("is_live", [P, TB])
        edge_row = sb("edge_row", [P, TB])
        edge_off = sb("edge_off", [P, TB])
        node_row = sb("node_row", [P, TB])
        node_off = sb("node_off", [P, TB])
        dst_key = sb("dst_key", [P, TB])
        src_key = sb("src_key", [P, TB])
        src_take = sb("src_take", [P, TB], I32)
        dst_take = sb("dst_take", [P, TB], I32)
        w_h = sb("w_h", [P, K, NS * C])
        bias3 = sb("bias3", [3, NS * C], BF16)
        w_a = sb("w_a", [P, K, H])
        b_a = sb("b_a", [P, 1])
        w2 = sb("w2", [P, NS])
        gain = sb("gain", [P, NS * C])
        shift = sb("shift", [P, NS * C])
        b2 = sb("b2", [P, NS])
        static_w = sb("static_w", [P, NS])
        common_q = sb("common_q", [P, C])
        inv_deg = sb("inv_deg", [P, HI])
        common_deg = sb("common_deg", [P, HI])
        sum_take = sb("sum_take", [P, TILES], I32)
        x_take = sb("x_take", [P, TILES], I32)
        y_put = sb("y_put", [P, TILES], I32)
        tile_weight = sb("tile_weight", [P, TILES])
        logits = sb("logits", [P, 1 + TILES, NS])
        counts_i = sb("counts_i", [1, 4], I32)
        mix = sb("mix", [P, NS])
        common_r = sb("common_r", [P, C])
        common_r3 = sb("common_r3", [3, 2 * C], BF16)

        pool_passed, dve_passed, sp_passed = sem("pool_passed"), sem("dve_passed"), sem("sp_passed")

        setup = ExitStack()
        with setup:
            def tb(name, shape, dt=F32):
                return setup.enter_context(nc.sbuf_tensor(name, shape, dt))

            raw = [tb("src_raw", [P, TB // P, P], I32), tb("dst_raw", [P, TB // P, P], I32)]
            rawf = [tb("src_rawf", [P, TB // P, P]), tb("dst_rawf", [P, TB // P, P])]
            tmp_i = tb("tmp_i", [P, TB], I32)
            tmp_j = tb("tmp_j", [P, TB], I32)
            tmp_f = tb("tmp_f", [P, TB])
            trash_i = tb("trash_i", [P, TB // G, G], I32)
            trash = tb("trash", [P, TB])
            batch_i = tb("batch_i", [P, TB], I32)
            hi_i = tb("hi_i", [P, HI], I32)
            part_i = tb("part_i", [P, 1], I32)
            cw = tb("cw", [P, NS, K, C])
            cwT = tb("cwT", [P, NS, K, C])
            tw = tb("tw", [P, NS, K, C])
            aw = tb("aw", [P, K, H])
            cb = tb("cb", [P, NS, K])
            cbB = tb("cbB", [P, NS, K, P])
            cb_sum = tb("cb_sum", [P, K])
            hb = tb("hb", [P, NS * C])
            hb_row = tb("hb_row", [P, NS * C])
            hb_part = tb("hb_part", [1, 3, NS * C], BF16)
            ab1 = tb("ab1", [P, 1])
            small = tb("small", [P, 16])
            sw = tb("sw", [P, NS])

            s_cleared, s_raw, s_padded, s_rawf, s_tr, s_tab = map(sem, (
                "s_cleared", "s_raw", "s_padded", "s_rawf", "s_tr", "s_tab"))
            s_wl, s_iota, s_wT, s_wTc, s_prod, s_dve, s_last, s_b3 = map(sem, (
                "s_wl", "s_iota", "s_wT", "s_wTc", "s_prod", "s_dve", "s_last", "s_b3"))
            s_pool, s_exp, s_parts, s_lastT = map(sem, ("s_pool", "s_exp", "s_parts", "s_lastT"))
            WHOLE = BATCHES - 1
            TAIL = E - WHOLE * P
            with nc.Block() as block:
                @block.sync
                def _(sp):
                    sp.wait_ge(s_cleared, 2)
                    n = 0
                    for t, a in zip(raw, (src, dst)):
                        chunks = WHOLE // P
                        sp.dma_start(t[:, 0:chunks, :], a[0:chunks * P * P].rearrange("(c r e) -> r c e", r=P, e=P))\
                          .then_inc(s_raw, 16)
                        more = WHOLE - chunks * P
                        sp.dma_start(t[0:more, chunks, :],
                                     a[chunks * P * P:WHOLE * P].rearrange("(r e) -> r e", e=P)).then_inc(s_raw, 16)
                        sp.dma_start(t[more:more + 1, chunks, 0:TAIL],
                                     a[WHOLE * P:E].rearrange("(r e) -> r e", r=1)).then_inc(s_raw, 16)
                        n += 3
                    sp.wait_ge(s_raw, 16 * n)
                    for t, d in zip(raw, (src_pad, dst_pad)):
                        sp.dma_start(d.rearrange("(c r) e -> r c e", r=P), t[:, :, :]).then_inc(s_padded, 16)
                    sp.wait_ge(s_parts, 1)
                    for k in range(3):
                        sp.dma_start(bias3[k:k + 1, :], hb_part[0:1, k, :]).then_inc(s_b3, 16)
                    sp.wait_ge(s_b3, 48)
                    sp.wait_ge(s_padded, 32)

                @block.scalar
                def _(act):
                    act.dma_start(cw[:, :, :, :], conv_W.rearrange("s (k p) c -> p s k c", p=P)).then_inc(s_wl, 16)
                    act.dma_start(tw[:, :, :, :], tr_W.rearrange("s (k p) c -> p s k c", p=P)).then_inc(s_wl, 16)
                    act.dma_start(aw[:, :, :], attn_W1.rearrange("(k p) h -> p k h", p=P)).then_inc(s_wl, 16)
                    act.dma_start(w2[:, :], attn_W2).then_inc(s_wl, 16)
                    with nc.allow_non_contiguous_dma(reason="small bias columns"):
                        act.dma_start(cb[:, :, :], conv_b.rearrange("s (k p) -> p s k", p=P)).then_inc(s_wl, 16)
                        act.dma_start(ab1[:, :], attn_b1.rearrange("(p a) -> p a", a=1)).then_inc(s_wl, 16)

                    def rows(t, a):
                        act.dma_start(t[:, :], a.to_broadcast([P, a.shape[1]])).then_inc(s_wl, 16)

                    flat = "s c -> (s c)"
                    rows(hb, tr_b.rearrange(flat).rearrange("(a n) -> a n", a=1))
                    rows(gain, ln_g.rearrange(flat).rearrange("(a n) -> a n", a=1))
                    rows(shift, ln_b.rearrange(flat).rearrange("(a n) -> a n", a=1))
                    rows(b2, attn_b2.rearrange("(a n) -> a n", a=1))
                    rows(sw, scale_w.rearrange("(a n) -> a n", a=1))
                    act.wait_ge(s_exp, 1)
                    nc.scalar.activation(small[:, 8:8 + NS], small[:, 4:4 + NS], ACT.Exp).then_inc(s_exp, 1)

                WL = 16 * 11

                @block.gpsimd
                def _(pool):
                    step = Chain(pool, s_pool)
                    nc.gpsimd.memset(raw[0][:, :, :], PAD).then_inc(s_cleared, 1)
                    nc.gpsimd.memset(raw[1][:, :, :], PAD).then_inc(s_cleared, 1)
                    step(nc.gpsimd.memset(ident[:, :], 0.0))
                    step(nc.gpsimd.affine_select(out=ident[:, :], in_=ident[:, :], compare_op=ALU.not_equal, fill=1.0,
                                                 base=0, pattern=[[-1, P]], channel_multiplier=1))
                    step(nc.gpsimd.memset(ones[:, :], 1.0))
                    step(nc.gpsimd.memset(ones3[:, :], 1.0))
                    step(nc.gpsimd.memset(zeros_bf[:, :], 0.0))
                    step(nc.gpsimd.affine_select(out=earlier[:, :], in_=ones[:, :], compare_op=ALU.is_gt, fill=0.0,
                                                 base=0, pattern=[[-1, P]], channel_multiplier=1))
                    step(nc.gpsimd.memset(before[:, :, :, :], 0.0))
                    for b in range(G):
                        for f in range(b + 1):
                            step(nc.gpsimd.tensor_copy(before[:, b, f, :], earlier[:, :] if f == b else ones[:, :]))
                    step(nc.gpsimd.iota(hi_i[:, :], pattern=[[1, HI]], base=0, channel_multiplier=0))
                    step(nc.gpsimd.tensor_copy(iota_h[:, :], hi_i[:, :]))
                    step(nc.gpsimd.iota(part_i[:, :], pattern=[[0, 1]], base=0, channel_multiplier=1))
                    step(nc.gpsimd.tensor_copy(part[:, :], part_i[:, :]))
                    step(nc.gpsimd.iota(batch_i[:, :], pattern=[[1, TB]], base=1, channel_multiplier=0))
                    step(nc.gpsimd.iota(trash_i[:, :, :], pattern=[[0, TB // G], [P, G]], base=0,
                                        channel_multiplier=1))
                    step(nc.gpsimd.memset(eps_t[:, :], EPS))
                    step(nc.gpsimd.memset(logits[:, :, :], 0.0))
                    nc.gpsimd.tensor_copy(trash[:, :], trash_i[:, :, :].rearrange("p a b -> p (a b)"))\
                        .then_inc(s_iota, 1)

                @block.tensor
                def _(pe):
                    pe.wait_ge(s_iota, 1)
                    for j in range(2):
                        pe.wait_ge(s_rawf, j + 1)
                        for c in range(TB // P):
                            last = nc.tensor.transpose(psum[2 * j + c // 4][:, (c % 4) * P:(c % 4 + 1) * P],
                                                       rawf[j][:, c, :], ident[:, :])
                        last.then_inc(s_tr, 1)
                    pe.wait_ge(s_wl, WL)
                    for s in range(NS):
                        for k in range(K):
                            for m in range(K):
                                last = nc.tensor.transpose(psum[4 + s][:, m * C + k * P:m * C + (k + 1) * P],
                                                           cw[:, s, k, m * P:(m + 1) * P], ident[:, :])
                    last.then_inc(s_wT, 1)
                    pe.wait_ge(s_wTc, 1)
                    pe.wait_ge(s_tab, 2)
                    for k in range(K):
                        for s in range(NS):
                            for m in range(K):
                                last = nc.tensor.matmul(psum[k][:, s * C:(s + 1) * C],
                                                        cwT[:, s, m, k * P:(k + 1) * P], tw[:, s, m, :],
                                                        start=(m == 0), stop=(m == K - 1))
                    for k in range(K):
                        for n in range(NS * K):
                            s, m = n // K, n % K
                            last = nc.tensor.matmul(psum[2][:, k * H:(k + 1) * H],
                                                    cwT[:, s, m, k * P:(k + 1) * P], aw[:, m, :],
                                                    start=(n == 0), stop=(n == NS * K - 1))
                    for s in range(NS):
                        for m in range(K):
                            last = nc.tensor.matmul(psum[3][:, s * C:(s + 1) * C], cbB[:, s, m, :], tw[:, s, m, :],
                                                    start=(m == 0), stop=(m == K - 1))
                    for m in range(K):
                        last = nc.tensor.matmul(psum[6][:, 0:1], aw[:, m, :], cb_sum[:, m:m + 1],
                                                start=(m == 0), stop=(m == K - 1))
                    last.then_inc(s_prod, 1)
                    pe.wait_ge(s_last, 1)
                    nc.tensor.matmul(psum[7][0:1, 0:P], small[:, 0:1], ident[:, :], start=True, stop=True)\
                        .then_inc(s_lastT, 1)

                @block.vector
                def _(dve):
                    v = nc.vector
                    step = Chain(dve, s_dve)
                    dve.wait_ge(s_raw, 96)
                    for j in range(2):
                        v.tensor_copy(rawf[j][:, :, :], raw[j][:, :, :]).then_inc(s_rawf, 1)
                    dve.wait_ge(s_iota, 1)
                    for j, t in enumerate((src_key, dst_key)):
                        dve.wait_ge(s_tr, j + 1)
                        for h in range(TB // 512):
                            step(v.tensor_copy(t[:, h * 512:(h + 1) * 512], psum[2 * j + h][:, :]))
                        dve.sem_inc(s_tab, 1)
                    dve.wait_ge(s_wT, 1)
                    for s in range(NS):
                        step(v.tensor_copy(cwT[:, s, :, :], psum[4 + s][:, :].rearrange("p (m c) -> p m c", c=C)))
                        for m in range(K):
                            step(v.tensor_scalar(cbB[:, s, m, :], ones[:, :], cb[:, s, m:m + 1], None, ALU.mult))
                    step(v.tensor_tensor(cb_sum[:, :], cb[:, 0, :], cb[:, 1, :], ALU.add))
                    dve.sem_inc(s_wTc, 1)
                    step(v.tensor_scalar(edge_off[:, :], trash[:, :], float(E_TRASH), None, ALU.add))
                    step(v.tensor_tensor(tmp_f[:, :], edge_off[:, :], dst_key[:, :], ALU.subtract))
                    step(v.tensor_scalar(is_live[:, :], dst_key[:, :], float(N_EDGES), None, ALU.is_lt))
                    step(v.tensor_tensor(tmp_f[:, :], tmp_f[:, :], is_live[:, :], ALU.mult))
                    step(v.tensor_tensor(edge_row[:, :], edge_off[:, :], tmp_f[:, :], ALU.subtract))
                    step(v.tensor_copy(edge_off[:, :], tmp_f[:, :]))
                    step(v.tensor_copy(tmp_f[:, :], batch_i[:, :]))
                    step(v.tensor_tensor(tmp_f[:, :], tmp_f[:, :], is_live[:, :], ALU.mult))
                    step(v.reduce_max(small[:, 0:1], tmp_f[:, :], AX))
                    dve.sem_inc(s_last, 1)
                    step(v.tensor_scalar(is_live[:, :], dst_key[:, :], float(LAST), None, ALU.is_lt))
                    step(v.tensor_copy(tmp_i[:, :], src_key[:, :]))
                    step(v.tensor_scalar(tmp_j[:, :], tmp_i[:, :], 7, None, ALU.arith_shift_right))
                    step(v.tensor_copy(own_hi[:, :], tmp_j[:, :]))
                    step(v.tensor_scalar(tmp_j[:, :], tmp_i[:, :], P - 1, None, ALU.bitwise_and))
                    step(v.tensor_copy(own_lo[:, :], tmp_j[:, :]))
                    step(v.scalar_tensor_tensor(node_row[:, :], own_lo[:, :], float(HI), own_hi[:, :],
                                                ALU.mult, ALU.add))
                    step(v.tensor_scalar(trash[:, :], trash[:, :], float(S_TRASH), None, ALU.add))
                    step(v.tensor_tensor(tmp_f[:, :], trash[:, :], node_row[:, :], ALU.subtract))
                    step(v.tensor_scalar(node_off[:, :], src_key[:, :], float(N), None, ALU.is_lt))
                    step(v.tensor_tensor(node_off[:, :], node_off[:, :], tmp_f[:, :], ALU.mult))
                    step(v.tensor_tensor(node_row[:, :], trash[:, :], node_off[:, :], ALU.subtract))
                    step(v.tensor_scalar(src_take[:, :], src_key[:, :], float(N - 1), None, ALU.min))
                    step(v.tensor_scalar(dst_take[:, :], dst_key[:, :], float(LAST), None, ALU.min))
                    dve.wait_ge(s_lastT, 1)
                    step(v.reduce_max(small[0:1, 1:2], psum[7][0:1, 0:P], AX))
                    step(v.tensor_scalar(small[0:1, 1:2], small[0:1, 1:2], 1.0, float(BODY - 1), ALU.max, ALU.add))
                    step(v.tensor_copy(counts_i[0:1, 1:2], small[0:1, 1:2]))
                    step(v.tensor_scalar(counts_i[0:1, 0:1], counts_i[0:1, 1:2], BODY.bit_length() - 1, None,
                                         ALU.arith_shift_right))
                    dve.wait_ge(s_prod, 1)
                    step(v.tensor_tensor(hb[:, :], hb[:, :], psum[3][:, :], ALU.add))
                    for s in range(NS):
                        cols = slice(s * C, (s + 1) * C)
                        for k in range(K + 1):
                            row = psum[k][:, cols] if k < K else hb[:, cols]
                            to = w_h[:, k, cols] if k < K else hb_row[:, cols]
                            step(v.reduce_sum(small[:, 2:3], row, AX))
                            step(v.tensor_scalar(small[:, 3:4], small[:, 2:3], 1.0 / C, None, ALU.mult))
                            step(v.tensor_scalar(to, row, small[:, 3:4], None, ALU.subtract))
                    for k in range(3):
                        step(v.tensor_copy(hb_part[0:1, k, :], hb_row[0:1, :]))
                        step(v.tensor_tensor(hb_row[0:1, :], hb_row[0:1, :], hb_part[0:1, k, :], ALU.subtract))
                    dve.sem_inc(s_parts, 1)
                    step(v.tensor_scalar(w_a[:, :, :], psum[2][:, 0:K * H].rearrange("p (k h) -> p k h", h=H),
                                         1.0 / NS, None, ALU.mult))
                    step(v.scalar_tensor_tensor(b_a[:, :], psum[6][:, 0:1], 1.0 / NS, ab1[:, :], ALU.mult, ALU.add))
                    step(v.reduce_max(small[:, 2:3], sw[:, :], AX))
                    step(v.tensor_scalar(small[:, 4:4 + NS], sw[:, :], small[:, 2:3], None, ALU.subtract))
                    dve.sem_inc(s_exp, 1)
                    dve.wait_ge(s_exp, 2)
                    step(v.reduce_sum(small[:, 2:3], small[:, 8:8 + NS], AX))
                    step(v.reciprocal(small[:, 3:4], small[:, 2:3]))
                    step(v.tensor_scalar(static_w[:, :], small[:, 8:8 + NS], small[:, 3:4], None, ALU.mult))

        def count(eng, j, most):
            return eng.value_load(counts_i[0:1, j:j + 1], min_val=1, max_val=most)

        BODIES = -(-BATCHES // BODY)

        deg = ExitStack()
        with deg:
            def tb(name, shape, dt=F32):
                return deg.enter_context(nc.sbuf_tensor(name, shape, dt))

            one_hi = tb("one_hi", [P, BODY, HI], BF16)
            one_lo = tb("one_lo", [P, BODY, P], BF16)
            live_lo = tb("live_lo", [P, BODY, P], BF16)
            total = tb("total", [P, HI])
            live = tb("live", [P, HI])
            flag = tb("flag", [P, HI])
            keys = tb("keys", [P, 2, HI])
            listed = tb("listed", [P, TILES])
            top = tb("top", [P, 8])
            fill = tb("fill", [P, 2, ZC, ROW])
            dsm = tb("dsm", [P, 8])
            common_row = tb("common_row", [P, ROW])
            valid = tb("valid", [P, TILES])

            s_hot, s_hist, s_sums, s_d2, s_top, s_cnt, s_cntT, s_init, s_fill, s_fz, s_k = map(sem, (
                "s_hot", "s_hist", "s_sums", "s_d2", "s_top", "s_cnt", "s_cntT", "s_init", "s_fill", "s_fz", "s_k"))
            fill_out = [sem("fill_out0"), sem("fill_out1")]
            BANKS = [(0, 0, 512), (1, 512, HI)]
            with nc.Block() as block:
                @block.vector
                def _(dve):
                    v = nc.vector
                    n_live = count(dve, 0, BODIES)

                    def hot(i, with_live):
                        for k in range(BODY):
                            b = i * BODY + k
                            dve.wait_ge(s_hist, b + 1)
                            if with_live:
                                v.tensor_scalar(live_lo[:, k, :], iota_h[:, 0:P], own_lo[:, bass.ds(b, 1)],
                                                is_live[:, bass.ds(b, 1)], ALU.is_equal, ALU.mult)
                            v.tensor_scalar(one_lo[:, k, :], iota_h[:, 0:P], own_lo[:, bass.ds(b, 1)], None,
                                            ALU.is_equal)
                            v.tensor_scalar(one_hi[:, k, :], iota_h[:, :], own_hi[:, bass.ds(b, 1)], None,
                                            ALU.is_equal).then_inc(s_hot, 1)

                    with dve.Fori(0, n_live) as i:
                        hot(i, True)
                    with dve.Fori(n_live, BODIES) as i:
                        hot(i, False)
                    dve.wait_ge(s_sums, 1)
                    step = Chain(dve, s_d2)
                    for b, lo, hi in BANKS:
                        step(v.tensor_copy(total[:, lo:hi], psum[b][:, 0:hi - lo]))
                        step(v.tensor_copy(live[:, lo:hi], psum[2 + b][:, 0:hi - lo]))
                    step(v.tensor_tensor(common_deg[:, :], total[:, :], live[:, :], ALU.subtract))
                    step(v.tensor_scalar(inv_deg[:, :], total[:, :], 1.0, None, ALU.max))
                    step(v.reciprocal(inv_deg[:, :], inv_deg[:, :]))
                    step(v.tensor_scalar(total[:, :], total[:, :], 0.5, None, ALU.is_lt))
                    step(v.scalar_tensor_tensor(flag[:, :], live[:, :], 0.5, total[:, :], ALU.is_gt, ALU.max))
                    dve.wait_ge(s_k, 2)
                    step(v.tensor_tensor(keys[:, 0, :], flag[:, :], key_init[:, :], ALU.mult))
                    step(v.tensor_scalar(flag[:, :], keys[:, 0, :], 0.5, None, ALU.is_gt))
                    step(v.reduce_sum(dsm[:, 0:1], flag[:, :], AX))
                    dve.sem_inc(s_cnt, 1)
                    step(v.memset(listed[:, :], 0.0))
                    dve.wait_ge(s_cntT, 1)
                    step(v.reduce_max(dsm[0:1, 1:2], psum[4][0:1, 0:P], AX))
                    step(v.tensor_scalar(dsm[0:1, 2:3], dsm[0:1, 1:2], 1.0, 1.0, ALU.max, ALU.add))
                    step(v.tensor_scalar(dsm[0:1, 3:4], dsm[0:1, 1:2], 1.0, 7.0, ALU.max, ALU.add))
                    step(v.tensor_copy(counts_i[0:1, 2:4], dsm[0:1, 2:4]))
                    step(v.tensor_scalar(counts_i[0:1, 1:2], counts_i[0:1, 2:3], 1, None, ALU.arith_shift_right))
                    step(v.tensor_scalar(counts_i[0:1, 2:3], counts_i[0:1, 3:4], 3, None, ALU.arith_shift_right))
                    eights = count(dve, 2, LIST // 8)
                    with dve.Fori(0, eights) as i:
                        pick = Chain(dve, s_top, i * 4)
                        pick(v.max(top[:, :], keys[:, 0, :]))
                        dve.sem_inc(dve_passed, 1)
                        pick(v.match_replace(keys[:, 1, :], top[:, :], keys[:, 0, :], 0.0))
                        pick(v.tensor_copy(keys[:, 0, :], keys[:, 1, :]))
                        pick(v.tensor_copy(listed[:, bass.ds(i * 8 + 1, 8)], top[:, :]))
                    step(v.tensor_scalar(valid[:, :], listed[:, :], 0.5, None, ALU.is_gt))
                    step(v.tensor_scalar(listed[:, :], listed[:, :], 1.0, 0.0, ALU.subtract, ALU.max))
                    step(v.tensor_scalar(dsm[:, 4:5], part[:, :], float(HI), None, ALU.mult))
                    step(v.tensor_scalar(sum_take[:, :], listed[:, :], dsm[:, 4:5], None, ALU.add))
                    step(v.tensor_scalar(listed[:, :], listed[:, :], float(P), part[:, 0:1], ALU.mult, ALU.add))
                    step(v.tensor_copy(x_take[:, :], listed[:, :]))
                    step(v.tensor_scalar(tile_weight[:, :], valid[:, :], float(-PAD), float(PAD), ALU.mult, ALU.add))
                    step(v.tensor_tensor(y_put[:, :], listed[:, :], tile_weight[:, :], ALU.add))
                    step(v.tensor_copy(tile_weight[:, :], valid[:, :]))
                    step(v.memset(sum_take[:, 0:1], S_COMMON))
                    dve.wait_ge(s_cntT, 2)
                    step(v.tensor_scalar(tile_weight[:, 0:1], psum[5][:, 0:1], -1.0 / P, float(N) / P,
                                         ALU.mult, ALU.add))

                @block.tensor
                def _(pe):
                    n_live = count(pe, 0, BODIES)
                    for b in range(4):
                        last = nc.tensor.matmul(psum[b][:, :], zeros_bf[:, 0:P], zeros_bf[:, :], start=True,
                                                stop=False, skip_group_check=True)
                    last.then_inc(s_hist, BODY)

                    def add(i, with_live):
                        for k in range(BODY):
                            pe.wait_ge(s_hot, i * BODY + k + 1)
                            for which in range(1 + with_live):
                                for b, lo, hi in BANKS:
                                    last = nc.tensor.matmul(psum[2 * which + b][:, 0:hi - lo],
                                                            (live_lo if which else one_lo)[:, k, :],
                                                            one_hi[:, k, lo:hi], start=False, stop=False,
                                                            skip_group_check=True)
                            last.then_inc(s_hist, 1)

                    with pe.Fori(0, n_live) as i:
                        add(i, True)
                    with pe.Fori(n_live, BODIES) as i:
                        add(i, False)
                    for b in range(4):
                        last = nc.tensor.matmul(psum[b][:, :], zeros_bf[:, 0:P], zeros_bf[:, :], start=False,
                                                stop=True, skip_group_check=True)
                    last.then_inc(s_sums, 1)
                    pe.wait_ge(s_cnt, 1)
                    nc.tensor.matmul(psum[4][0:1, 0:P], dsm[:, 0:1], ident[:, :], start=True, stop=True)\
                        .then_inc(s_cntT, 1)
                    nc.tensor.matmul(psum[5][:, 0:1], ones[:, :], dsm[:, 0:1], start=True, stop=True)\
                        .then_inc(s_cntT, 1)

                @block.gpsimd
                def _(pool):
                    nc.gpsimd.iota(key_init[:, :], pattern=[[1, HI]], base=1, channel_multiplier=0,
                                   allow_small_or_imprecise_dtypes=True).then_inc(s_k, 1)
                    pool.wait_ge(s_k, 1)
                    nc.gpsimd.affine_select(out=key_init[:, :], in_=key_init[:, :], compare_op=ALU.is_gt, fill=0.0,
                                            base=N, pattern=[[-P, HI]], channel_multiplier=-1).then_inc(s_k, 1)
                    nc.gpsimd.memset(fill[:, :, :, :], 0.0).then_inc(s_fz, 1)
                    nc.gpsimd.memset(common_row[:, :], 0.0).then_inc(s_k, 1)
                    pool.wait_ge(s_k, 3)
                    nc.gpsimd.memset(common_row[:, C:C + 2], 1.0).then_inc(s_fz, 1)

                @block.scalar
                def _(act):
                    act.wait_ge(s_d2, 7)
                    act.wait_ge(s_fz, 1)
                    for c in range(HI // ZC):
                        if c < 2:
                            act.wait_ge(s_init, 16 * 9)
                        else:
                            act.wait_ge(fill_out[c % 2], 16 * (c // 2))
                        cols = slice(c * ZC, (c + 1) * ZC)
                        nc.scalar.copy(fill[:, c % 2, :, C], inv_deg[:, cols]).then_inc(s_fill, 1)
                        nc.scalar.copy(fill[:, c % 2, :, C + 1], common_deg[:, cols]).then_inc(s_fill, 1)

                @block.sync
                def _(sp):
                    sp.wait_ge(s_fz, 2)
                    edge_v = edge_sum.rearrange("(p r) c -> p r c", p=P)
                    n = 0
                    for lo in range(0, E_COLS, ZC):
                        hi = min(E_COLS, lo + ZC)
                        sp.dma_start(edge_v[:, lo:hi, :], fill[:, 0, 0:hi - lo, :]).then_inc(s_init, 16)
                        n += 1
                    for g in range(G):
                        sp.dma_start(node_sum[S_TRASH + g * P:S_TRASH + (g + 1) * P, :], fill[:, 0, 0, :])\
                          .then_inc(s_init, 16)
                        n += 1
                    assert n == 9
                    node_v = node_sum[0:S_TRASH, :].rearrange("(p r) c -> p r c", p=P)
                    for c in range(HI // ZC):
                        sp.wait_ge(s_fill, 2 * (c + 1))
                        sp.dma_start(node_v[:, c * ZC:(c + 1) * ZC, :], fill[:, c % 2, :, :])\
                          .then_inc(fill_out[c % 2], 16)
                    sp.dma_start(node_sum[S_COMMON:S_COMMON + P, :], common_row[:, :]).then_inc(s_init, 16)
                    sp.wait_ge(s_init, 16 * (n + 1))
                    for u in range(2):
                        sp.wait_ge(fill_out[u], 16 * (HI // ZC // 2))

        def segment_sums(name, keys_dram, key, table, take, row, off, target, from_edges):
            st = ExitStack()
            with st:
                def tb(nm, shape, dt=F32):
                    return st.enter_context(nc.sbuf_tensor(f"{name}_{nm}", shape, dt))

                def sm(nm):
                    return sem(f"{name}_{nm}")

                taken = tb("taken", [P, UNROLL, G, ROW])
                merged = tb("merged", [P, UNROLL, G, ROW])
                key_rows = tb("key_rows", [P, UNROLL, G * P], I32)
                equal = tb("equal", [P, UNROLL, G, G * P])
                junk = tb("junk", [P, UNROLL, G, G * P])
                repeats = tb("repeats", [P, UNROLL, G])
                shiftf = tb("shiftf", [P, UNROLL, G])
                factor = tb("factor", [P, UNROLL, G])
                put_idx = tb("put_idx", [P, UNROLL, G], I32)
                take_idx = tb("take_idx", [P, UNROLL, G], I32)
                cols = C if from_edges else ROW
                keys_in = [sm(f"keys_in{u}") for u in range(UNROLL)]
                gathered = [sm(f"gathered{u}") for u in range(UNROLL)]
                added = [sm(f"added{u}") for u in range(UNROLL)]
                take_ready = [sm(f"take_ready{u}") for u in range(UNROLL)]
                equal_ready, put_ready, products, evacuated, steps, cleared, offset = map(sm, (
                    "equal_ready", "put_ready", "products", "evacuated", "steps", "cleared", "offset"))
                with nc.Block() as block:
                    @block.sync
                    def _(sp):
                        n = count(sp, 0, BODIES)
                        with sp.Fori(0, n) as i:
                            for u in range(UNROLL):
                                g = i * UNROLL + u
                                sp.wait_ge(put_ready, g + 1)
                                sp.dma_start(key_rows[:, u, :],
                                             keys_dram[bass.ds(g * G, G), :].rearrange("g p -> (g p)")
                                             .rearrange("(a n) -> a n", a=1).to_broadcast([P, G * P]))\
                                  .then_inc(keys_in[u], 16)

                    @block.scalar
                    def _(act):
                        n = count(act, 0, BODIES)
                        act.sem_inc(evacuated, UNROLL)
                        for u in range(UNROLL):
                            nc.scalar.copy(take_idx[:, u, :], take[:, u * G:(u + 1) * G]).then_inc(take_ready[u], 1)
                        act.wait_ge(cleared, 2)
                        with act.Fori(0, n) as i:
                            for u in range(UNROLL):
                                g = i * UNROLL + u
                                act.wait_ge(gathered[u], (i + 1) * 16 * G)
                                nc.scalar.copy(take_idx[:, u, :], take[:, bass.ds((g + UNROLL) * G, G)])\
                                    .then_inc(take_ready[u], 1)
                                act.wait_ge(products, g + UNROLL + 1)
                                act.wait_ge(added[u], i * 16 * G)
                                for b in range(G):
                                    last = nc.scalar.copy(merged[:, u, b, 0:cols], psum[u * G + b][:, 0:cols])
                                last.then_inc(evacuated, 1)

                    @block.tensor
                    def _(pe):
                        n = count(pe, 0, BODIES)
                        pe.sem_inc(products, UNROLL)
                        with pe.Fori(0, n) as i:
                            for u in range(UNROLL):
                                g = i * UNROLL + u
                                pe.wait_ge(gathered[u], (i + 1) * 16 * G)
                                pe.wait_ge(equal_ready, g + 1)
                                pe.wait_ge(evacuated, g + 1)
                                for b in range(G):
                                    for f in range(G):
                                        last = nc.tensor.matmul(psum[u * G + b][:, 0:cols],
                                                                equal[:, u, f, b * P:(b + 1) * P],
                                                                taken[:, u, f, 0:cols],
                                                                start=(f == 0), stop=(f == G - 1))
                                last.then_inc(products, 1)

                    @block.vector
                    def _(dve):
                        v = nc.vector
                        n = count(dve, 0, BODIES)
                        dve.sem_inc(put_ready, UNROLL)
                        per_group = 4 if from_edges else 1
                        with dve.Fori(0, n) as i:
                            for u in range(UNROLL):
                                g = i * UNROLL + u
                                step = Chain(dve, steps, g * per_group)
                                pair = bass.ds(g * G, G)
                                if from_edges:
                                    dve.wait_ge(gathered[u], (i + 1) * 16 * G)
                                    step(v.tensor_scalar(factor[:, u, :], taken[:, u, :, C], 1.0, None, ALU.max))
                                    step(v.reciprocal(factor[:, u, :], factor[:, u, :]))
                                    step(v.tensor_tensor(factor[:, u, :], factor[:, u, :], is_live[:, pair], ALU.mult))
                                dve.wait_ge(keys_in[u], (i + 1) * 16)
                                dve.wait_ge(products, g + 1)
                                for f in range(G):
                                    k = key[:, bass.ds(g * G + f, 1)]
                                    if from_edges:
                                        last = v.tensor_scalar(equal[:, u, f, :], key_rows[:, u, :], k,
                                                               factor[:, u, f:f + 1], ALU.is_equal, ALU.mult)
                                    else:
                                        last = v.tensor_scalar(equal[:, u, f, :], key_rows[:, u, :], k, None,
                                                               ALU.is_equal)
                                last.then_inc(equal_ready, 1)
                                for b in range(G):
                                    w = (b + 1) * P
                                    last = v.scalar_tensor_tensor(
                                        junk[:, u, b, 0:w], key_rows[:, u, 0:w], key[:, bass.ds(g * G + b, 1)],
                                        before[:, b, :, :].rearrange("p a b -> p (a b)")[:, 0:w],
                                        ALU.is_equal, ALU.mult, accum_out=repeats[:, u, b:b + 1])
                                    if b == G - 1:
                                        step(last)
                                v.scalar_tensor_tensor(shiftf[:, u, :], repeats[:, u, :], 1.0, off[:, pair],
                                                       ALU.min, ALU.mult).then_inc(offset, 1)
                                dve.wait_ge(offset, g + 1)
                                dve.wait_ge(added[u], i * 16 * G)
                                v.tensor_tensor(put_idx[:, u, :], shiftf[:, u, :], row[:, pair], ALU.add)\
                                    .then_inc(put_ready, 1)

                    @block.gpsimd
                    def _(pool):
                        n = count(pool, 0, BODIES)
                        nc.gpsimd.memset(merged[:, :, :, :], 0.0).then_inc(cleared, 1)
                        nc.gpsimd.memset(taken[:, :, :, :], 0.0).then_inc(cleared, 1)
                        pool.wait_ge(cleared, 2)
                        if not from_edges:
                            nc.gpsimd.memset(taken[:, :, :, C:C + 1], 1.0).then_inc(cleared, 1)
                            pool.wait_ge(cleared, 3)

                        def gather(u, turn):
                            pool.wait_ge(take_ready[u], turn + 1)
                            for b in range(G):
                                pool.sem_inc(pool_passed, 1)
                                pool.indirect_dma_start(
                                    taken[:, u, b, 0:table.shape[1]], None, table,
                                    bass.IndirectOffsetOnAxis(take_idx[:, u, b:b + 1], 0)).then_inc(gathered[u], 16)

                        for u in range(UNROLL):
                            gather(u, 0)
                        with pool.Fori(0, n) as i:
                            for u in range(UNROLL):
                                g = i * UNROLL + u
                                pool.wait_ge(products, g + UNROLL + 1)
                                gather(u, i + 1)
                                pool.wait_ge(evacuated, g + UNROLL + 1)
                                pool.wait_ge(put_ready, g + UNROLL + 1)
                                if u:
                                    pool.wait_ge(added[u - 1], (i + 1) * 16 * G)
                                else:
                                    pool.wait_ge(added[UNROLL - 1], i * 16 * G)
                                for b in range(G):
                                    pool.sem_inc(pool_passed, 1)
                                    pool.indirect_dma_start(
                                        target, bass.IndirectOffsetOnAxis(put_idx[:, u, b:b + 1], 0),
                                        merged[:, u, b, :], None, compute_op=ALU.add).then_inc(added[u], 16)
                        for u in range(UNROLL):
                            pool.wait_ge(gathered[u], (n + 1) * 16 * G)
                            pool.wait_ge(added[u], n * 16 * G)
                            pool.sem_inc(pool_passed, 1)

        segment_sums("edges", dst_pad, dst_key, x, src_take, edge_row, edge_off, edge_sum, False)
        segment_sums("nodes", src_pad, src_key, edge_sum, dst_take, node_row, node_off, node_sum, True)

        rt = ExitStack()
        with rt:
            def tb(name, shape, dt=F32):
                return rt.enter_context(nc.sbuf_tensor(name, shape, dt))

            sums = tb("sums", [P, 2, ROW])
            q = tb("q", [P, 2, C])
            qT = tb("qT", [P, 2, K, P])
            aT = tb("aT", [P, 2, P])
            sq = tb("sq", [P, 2, NS * C])
            ssq = tb("ssq", [P, 2, NS])
            inv = tb("inv", [P, 2, NS])
            tr = tb("tr", [P, 2, NS * C])
            res = tb("res", [P, 2, NS * C])
            sidx = tb("sidx", [P, 2], I32)
            last_row = tb("last_row", [P, ROW])
            cfac = tb("cfac", [P, 1])
            sum_in = [sem("sum_in0"), sem("sum_in1")]
            res_out = [sem("res_out0"), sem("res_out1")]
            (t_idx, t_qa, t_q, t_tp, t_qT, t_h, t_aT, t_lg, t_lgc, t_ssq, t_std, t_inv, t_sc, t_sh, t_res, t_row,
             t_cq, t_at, t_clear) = map(sem, (
                "t_idx", "t_qa", "t_q", "t_tp", "t_qT", "t_h", "t_aT", "t_lg", "t_lgc", "t_ssq", "t_std", "t_inv",
                "t_sc", "t_sh", "t_res", "t_row", "t_cq", "t_at", "t_clear"))
            tiles_v = transformed.rearrange("(t p) c -> t p c", p=P)
            PAIRS = LIST // 2 + 1

            with nc.Block() as block:
                def pairs(eng):
                    return count(eng, 1, PAIRS) + 2

                @block.sync
                def _(sp):
                    n = pairs(sp)
                    sp.dma_start(last_row[:, :], edge_sum[LAST:LAST + 1, :].to_broadcast([P, ROW])).then_inc(t_row, 16)

                    def store(t, w):
                        sp.wait_ge(t_res, t + 1)
                        sp.dma_start(tiles_v[bass.ds(t, 1), :, :].rearrange("a p c -> (a p) c"), res[:, w, :])\
                          .then_inc(res_out[w], 16)

                    with sp.Fori(0, n) as i:
                        for u in range(2):
                            store(i * 2 + u, 1 - u)
                    store(n * 2, 1)
                    sp.wait_ge(res_out[0], n * 16)
                    sp.sem_inc(sp_passed, 1)
                    sp.wait_ge(res_out[1], n * 16 + 16)
                    sp.sem_inc(sp_passed, 1)

                @block.gpsimd
                def _(pool):
                    n = pairs(pool)
                    nc.gpsimd.memset(aT[:, :, :], 0.0).then_inc(t_clear, 1)
                    nc.gpsimd.memset(tr[:, :, :], 0.0).then_inc(t_clear, 1)

                    def gather(u, t):
                        pool.wait_ge(t_idx, t + 1)
                        pool.sem_inc(pool_passed, 1)
                        pool.indirect_dma_start(sums[:, u, :], None, node_sum,
                                                bass.IndirectOffsetOnAxis(sidx[:, u:u + 1], 0))\
                            .then_inc(sum_in[u], 16)

                    for u in range(2):
                        gather(u, u)
                    with pool.Fori(0, n) as i:
                        for u in range(2):
                            t = i * 2 + u
                            pool.wait_ge(t_q, t + 1)
                            gather(u, t + 2)
                    for u in range(2):
                        pool.wait_ge(sum_in[u], (n + 1) * 16)
                    pool.sem_inc(pool_passed, 1)

                @block.scalar
                def _(act):
                    n = pairs(act)
                    a = nc.scalar

                    def transposed(t, w):
                        act.wait_ge(t_tp, t + 1)
                        a.copy(qT[:, w, :, :], psum[w][:, 0:C].rearrange("p (k n) -> p k n", n=P)).then_inc(t_qT, 1)

                    def finish(t, w, i):
                        act.wait_ge(t_sh, t + 1)
                        act.wait_ge(res_out[w], i * 16)
                        a.activation(res[:, w, :], tr[:, w, :], ACT.Relu).then_inc(t_res, 1)

                    a.activation(ssq[:, 0, 0:1], eps_t[:, 0:1], ACT.Sqrt).then_inc(t_clear, 1)
                    for u in range(2):
                        a.copy(sidx[:, u:u + 1], sum_take[:, u:u + 1]).then_inc(t_idx, 1)
                    act.wait_ge(t_clear, 3)
                    transposed(0, 0)
                    with act.Fori(0, n) as i:
                        for u in range(2):
                            t = i * 2 + u
                            act.wait_ge(sum_in[u], (i + 1) * 16)
                            a.copy(sidx[:, u:u + 1], sum_take[:, bass.ds(t + 2, 1)]).then_inc(t_idx, 1)
                            act.wait_ge(t_h, t)
                            transposed(t + 1, 1 - u)
                            act.wait_ge(t_at, t + 1)
                            a.activation(aT[:, u, :], psum[4 + u][:, 0:P], ACT.Relu, bias=b_a[:, 0:1])\
                                .then_inc(t_aT, 1)
                            act.wait_ge(t_h, t + 1)
                            for s in range(NS):
                                last = a.activation(sq[:, u, s * C:(s + 1) * C], psum[2 + u][:, s * C:(s + 1) * C],
                                                    ACT.Square, accum_out=ssq[:, u, s:s + 1])
                            last.then_inc(t_ssq, 1)
                            act.wait_ge(t_ssq, t + 1)
                            a.activation(ssq[:, u, :], ssq[:, u, :], ACT.Sqrt, bias=eps_t[:, 0:1], scale=1.0 / C)\
                                .then_inc(t_std, 1)
                            finish(t, 1 - u, i)
                    finish(n * 2, 1, n)

                @block.vector
                def _(dve):
                    v = nc.vector
                    n = pairs(dve)
                    dve.sem_inc(t_sh, 1)
                    dve.sem_inc(t_lgc, 2)
                    step = Chain(dve, t_cq)
                    dve.wait_ge(t_row, 16)
                    step(v.tensor_scalar(cfac[:, :], last_row[:, C:C + 1], 1.0, None, ALU.max))
                    step(v.reciprocal(cfac[:, :], cfac[:, :]))
                    step(v.tensor_scalar(common_q[:, :], last_row[:, 0:C], cfac[:, 0:1], None, ALU.mult))

                    def means(t, u, i):
                        dve.wait_ge(sum_in[u], (i + 1) * 16)
                        v.scalar_tensor_tensor(q[:, u, :], common_q[:, :], sums[:, u, C + 1:C + 2],
                                               sums[:, u, 0:C], ALU.mult, ALU.add).then_inc(t_qa, 1)
                        dve.wait_ge(t_qa, t + 1)
                        v.tensor_scalar(q[:, u, :], q[:, u, :], sums[:, u, C:C + 1], None, ALU.mult)\
                            .then_inc(t_q, 1)

                    def take_logits(t, w):
                        dve.wait_ge(t_lg, t + 1)
                        v.tensor_copy(logits[:, bass.ds(t, 1), :].rearrange("p a s -> p (a s)"),
                                      psum[6 + w][:, 0:NS]).then_inc(t_lgc, 1)

                    for u in range(2):
                        means(u, u, 0)
                    with dve.Fori(0, n) as i:
                        for u in range(2):
                            t = i * 2 + u
                            dve.wait_ge(t_tp, t + 1)
                            means(t + 2, u, i + 1)
                            take_logits(t, 1 - u)
                            dve.wait_ge(t_std, t + 1)
                            v.reciprocal(inv[:, u, :], ssq[:, u, :]).then_inc(t_inv, 1)
                            dve.wait_ge(t_inv, t + 1)
                            dve.wait_ge(t_res, t)
                            for s in range(NS):
                                c = slice(s * C, (s + 1) * C)
                                last = v.scalar_tensor_tensor(tr[:, u, c], psum[2 + u][:, c], inv[:, u, s:s + 1],
                                                              gain[:, c], ALU.mult, ALU.mult)
                            last.then_inc(t_sc, 1)
                            dve.wait_ge(t_sc, t + 1)
                            v.tensor_tensor(tr[:, u, :], tr[:, u, :], shift[:, :], ALU.add).then_inc(t_sh, 1)
                    take_logits(n * 2, 1)

                @block.tensor
                def _(pe):
                    n = pairs(pe)
                    m = nc.tensor

                    def turn_rows(t, w):
                        pe.wait_ge(t_q, t + 1)
                        for k in range(K):
                            last = m.transpose(psum[w][:, k * P:(k + 1) * P], q[:, w, k * P:(k + 1) * P], ident[:, :])
                        last.then_inc(t_tp, 1)

                    def attend(t, w):
                        pe.wait_ge(t_aT, t)
                        pe.wait_ge(t_lgc, t + 1)
                        m.matmul(psum[6 + w][:, 0:NS], aT[:, w, :], w2[:, :], start=True, stop=True)\
                            .then_inc(t_lg, 1)

                    pe.wait_ge(t_clear, 3)
                    turn_rows(0, 0)
                    with pe.Fori(0, n) as i:
                        for u in range(2):
                            t = i * 2 + u
                            pe.wait_ge(t_qT, t)
                            turn_rows(t + 1, 1 - u)
                            attend(t, 1 - u)
                            pe.wait_ge(t_qT, t + 1)
                            for k in range(K):
                                last = m.matmul(psum[4 + u][:, 0:P], w_a[:, k, :], qT[:, u, k, :], start=(k == 0),
                                                stop=(k == K - 1))
                            last.then_inc(t_at, 1)
                            pe.wait_ge(t_sh, t)
                            m.matmul(psum[2 + u][:, :], ones3[:, :], bias3[:, :], start=True, stop=False)
                            for k in range(K):
                                last = m.matmul(psum[2 + u][:, :], qT[:, u, k, :], w_h[:, k, :], start=False,
                                                stop=(k == K - 1))
                            last.then_inc(t_h, 1)
                    attend(n * 2, 1)

        wt = ExitStack()
        with wt:
            def tb(name, shape, dt=F32):
                return wt.enter_context(nc.sbuf_tensor(name, shape, dt))

            l = tb("l", [P, NS, TILES])
            mx = tb("mx", [P, TILES])
            ex = tb("ex", [P, NS, TILES])
            tot = tb("tot", [P, TILES])
            acc = tb("acc", [P, NS])
            t0 = tb("t0", [P, NS * C])
            r_part = tb("r_part", [1, 3, 2 * C], BF16)
            w_d, w_a0, w_e, w_s, w_t, w_p = map(sem, ("w_d", "w_a0", "w_e", "w_s", "w_t", "w_p"))
            w_p3 = sem("w_p3")
            with nc.Block() as block:
                @block.sync
                def _(sp):
                    sp.dma_start(t0[:, :], transformed[P:2 * P, :]).then_inc(w_t, 16)
                    sp.wait_ge(w_p, 1)
                    for k in range(3):
                        sp.dma_start(common_r3[k:k + 1, :], r_part[0:1, k, :]).then_inc(w_p3, 16)
                    sp.wait_ge(w_p3, 48)

                @block.scalar
                def _(act):
                    act.wait_ge(w_a0, 1)
                    nc.scalar.activation(ex[:, :, :], l[:, :, :], ACT.Exp).then_inc(w_e, 1)

                @block.tensor
                def _(pe):
                    pe.wait_ge(w_s, 1)
                    nc.tensor.matmul(psum[0][:, 0:NS], ones[:, :], acc[:, :], start=True, stop=True).then_inc(w_s, 1)

                @block.vector
                def _(dve):
                    v = nc.vector
                    step = Chain(dve, w_d)
                    for s in range(NS):
                        step(v.tensor_scalar(l[:, s, :], logits[:, 1:, s], b2[:, s:s + 1], None, ALU.add))
                    step(v.tensor_tensor(mx[:, :], l[:, 0, :], l[:, 1, :], ALU.max))
                    for s in range(NS):
                        step(v.tensor_tensor(l[:, s, :], l[:, s, :], mx[:, :], ALU.subtract))
                    dve.sem_inc(w_a0, 1)
                    dve.wait_ge(w_e, 1)
                    step(v.tensor_tensor(tot[:, :], ex[:, 0, :], ex[:, 1, :], ALU.add))
                    step(v.reciprocal(tot[:, :], tot[:, :]))
                    step(v.tensor_tensor(tot[:, :], tot[:, :], tile_weight[:, :], ALU.mult))
                    for s in range(NS):
                        step(v.tensor_tensor(ex[:, s, :], ex[:, s, :], tot[:, :], ALU.mult))
                        step(v.reduce_sum(acc[:, s:s + 1], ex[:, s, :], AX))
                    dve.sem_inc(w_s, 1)
                    dve.wait_ge(w_s, 2)
                    step(v.scalar_tensor_tensor(mix[:, :], psum[0][:, 0:NS], 1.0 / N, static_w[:, :],
                                                ALU.mult, ALU.add))
                    step(v.tensor_scalar(mix[:, :], mix[:, :], 0.5, None, ALU.mult))
                    dve.wait_ge(w_t, 16)
                    step(v.tensor_scalar(common_r[:, :], t0[:, 0:C], mix[:, 0:1], None, ALU.mult))
                    step(v.scalar_tensor_tensor(common_r[:, :], t0[:, C:2 * C], mix[:, 1:2], common_r[:, :],
                                                ALU.mult, ALU.add))
                    for k in range(3):
                        for two in range(2):
                            step(v.tensor_copy(r_part[0:1, k, two * C:(two + 1) * C], common_r[0:1, :]))
                        step(v.tensor_tensor(common_r[0:1, :], common_r[0:1, :], r_part[0:1, k, 0:C], ALU.subtract))
                    dve.sem_inc(w_p, 1)

        ot = ExitStack()
        with ot:
            def tb(name, shape, dt=F32):
                return ot.enter_context(nc.sbuf_tensor(name, shape, dt))

            R = 8
            NB = 4
            xin = tb("xin", [P, NB, R, C])
            yout = tb("yout", [P, NB, R, C])
            stats = tb("stats", [P, NB, R, 6])
            mv = tb("mv", [P, NB, R, 2])
            std = tb("std", [P, NB, R])
            rs = tb("rs", [P, NB, R])
            nm = tb("nm", [P, NB, R])
            o_in = [sem(f"o_in{u}") for u in range(NB)]
            o_out = [sem(f"o_out{u}") for u in range(NB)]
            o_sum, o_st, o_mv, o_std, o_rs, o_nm, o_y = map(sem, (
                "o_sum", "o_st", "o_mv", "o_std", "o_rs", "o_nm", "o_y"))
            TURNS = FULL // NB
            xv = x[0:FULL * 8 * P, :].rearrange("(c p r) d -> c p (r d)", p=P, r=R)
            ov = out[0:FULL * 8 * P, :].rearrange("(c p r) d -> c p (r d)", p=P, r=R)
            xr = x[FULL * 8 * P:N, :].rearrange("(p r) d -> p (r d)", p=REST_P)
            orr = out[FULL * 8 * P:N, :].rearrange("(p r) d -> p (r d)", p=REST_P)
            peeled = [(c % NB, TURNS + (c // NB - TURNS), c, P, R) for c in range(TURNS * NB, FULL)]
            peeled.append((FULL % NB, FULL // NB, None, REST_P, REST_R))
            uses = [TURNS + sum(p[0] == u for p in peeled) for u in range(NB)]

            def every(eng, f):
                with eng.Fori(0, TURNS) as i:
                    for u in range(NB):
                        f(u, i, i * NB + u, P, R)
                for p in peeled:
                    f(*p)

            def position(u, i):
                return i * NB + u

            with nc.Block() as block:
                @block.sync
                def _(sp):
                    def load(u, i, c, pp, r):
                        sp.wait_ge(o_sum, position(u, i) + 1)
                        a = xr if c is None else xv[bass.ds(c, 1)].rearrange("a p c -> (a p) c")
                        sp.dma_start(xin[0:pp, u, 0:r, :].rearrange("p r c -> p (r c)"), a).then_inc(o_in[u], 16)
                    every(sp, load)

                @block.gpsimd
                def _(pool):
                    def store(u, i, c, pp, r):
                        pool.wait_ge(o_y, position(u, i) + 3)
                        a = orr if c is None else ov[bass.ds(c, 1)].rearrange("a p c -> (a p) c")
                        pool.sem_inc(pool_passed, 1)
                        pool.dma_start(a, yout[0:pp, u, 0:r, :].rearrange("p r c -> p (r c)")).then_inc(o_out[u], 16)
                    every(pool, store)
                    for u in range(NB):
                        pool.wait_ge(o_out[u], 16 * uses[u])

                def rows_of(u, pp, r):
                    return [(psum[(u % 2) * 4 + j // 2][0:pp, (j % 2) * C:(j % 2 + 1) * C], j) for j in range(r)]

                @block.tensor
                def _(pe):
                    pe.sem_inc(o_sum, NB)

                    def work(u, i, c, pp, r):
                        pe.wait_ge(o_in[u], (i + 1) * 16)
                        pe.wait_ge(o_y, position(u, i) + 1)
                        for j in range(0, r, 2):
                            bank = psum[(u % 2) * 4 + j // 2][0:pp, :]
                            nc.tensor.matmul(bank, ones3[:, 0:pp], common_r3[:, :], start=True, stop=False)
                            last = nc.tensor.matmul(bank, ident[0:pp, 0:pp],
                                                    xin[0:pp, u, j:j + 2, :].rearrange("p r c -> p (r c)"),
                                                    start=False, stop=True)
                        last.then_inc(o_sum, 1)
                    every(pe, work)

                @block.vector
                def _(dve):
                    v = nc.vector

                    def work(u, i, c, pp, r):
                        n = position(u, i)
                        dve.wait_ge(o_sum, n + NB + 1)
                        for y, j in rows_of(u, pp, r):
                            last = v.bn_stats(stats[0:pp, u, j, :], y)
                        last.then_inc(o_st, 1)
                        dve.wait_ge(o_st, n + 1)
                        dve.sem_inc(dve_passed, 1)
                        for j in range(r):
                            last = v.bn_aggr(mv[0:pp, u, j, :], stats[0:pp, u, j, :])
                        last.then_inc(o_mv, 1)
                        dve.wait_ge(o_std, n + 1)
                        v.reciprocal(rs[0:pp, u, 0:r], std[0:pp, u, 0:r]).then_inc(o_rs, 1)
                        dve.wait_ge(o_rs, n + 1)
                        v.scalar_tensor_tensor(nm[0:pp, u, 0:r], mv[0:pp, u, 0:r, 0], -1.0, rs[0:pp, u, 0:r],
                                               ALU.mult, ALU.mult).then_inc(o_nm, 1)
                    every(dve, work)

                @block.scalar
                def _(act):
                    act.sem_inc(o_y, 2)

                    def work(u, i, c, pp, r):
                        n = position(u, i)
                        act.wait_ge(o_mv, n + 1)
                        nc.scalar.activation(std[0:pp, u, 0:r], mv[0:pp, u, 0:r, 1], ACT.Sqrt, bias=eps_t[0:pp, 0:1])\
                            .then_inc(o_std, 1)
                        act.wait_ge(o_nm, n + 1)
                        act.wait_ge(o_out[u], i * 16)
                        for y, j in rows_of(u, pp, r):
                            last = nc.scalar.activation(yout[0:pp, u, j, :], y, ACT.Identity,
                                                        bias=nm[0:pp, u, j:j + 1], scale=rs[0:pp, u, j:j + 1])
                        last.then_inc(o_y, 1)
                    every(act, work)

        fo = ExitStack()
        with fo:
            def tb(name, shape, dt=F32):
                return fo.enter_context(nc.sbuf_tensor(name, shape, dt))

            U = 4
            xg = tb("xg", [P, U, C])
            tt = tb("tt", [P, U, 2 * C])
            ys = tb("ys", [P, U, C])
            yo = tb("yo", [P, U, C])
            st2 = tb("st2", [P, U, 6])
            mv2 = tb("mv2", [P, U, 2])
            sd2 = tb("sd2", [P, U])
            rs2 = tb("rs2", [P, U])
            nm2 = tb("nm2", [P, U])
            xi = tb("xi", [P, U], I32)
            yi = tb("yi", [P, U], I32)
            f_in = [sem(f"f_in{u}") for u in range(U)]
            f_t = [sem(f"f_t{u}") for u in range(U)]
            f_out = [sem(f"f_out{u}") for u in range(U)]
            f_idx, f_y1, f_y2, f_st, f_mv, f_sd, f_rs, f_nm, f_yo, f_yi = map(sem, (
                "f_idx", "f_y1", "f_y2", "f_st", "f_mv", "f_sd", "f_rs", "f_nm", "f_yo", "f_yi"))
            with nc.Block() as block:
                def turns(eng):
                    return (count(eng, 1, LIST // 2) + 1) // 2

                @block.sync
                def _(sp):
                    n = turns(sp)
                    with sp.Fori(0, n) as i:
                        for u in range(U):
                            sp.wait_ge(f_y2, i * U + u + 1)
                            sp.dma_start(tt[:, u, :], tiles_v[bass.ds(i * U + u + 2, 1)]
                                         .rearrange("a p c -> (a p) c")).then_inc(f_t[u], 16)

                @block.gpsimd
                def _(pool):
                    n = turns(pool)

                    def gather(u, turn):
                        pool.wait_ge(f_idx, turn * U + u + 1)
                        pool.wait_ge(f_y2, turn * U + u + 1)
                        pool.sem_inc(pool_passed, 1)
                        pool.indirect_dma_start(xg[:, u, :], None, x, bass.IndirectOffsetOnAxis(xi[:, u:u + 1], 0))\
                            .then_inc(f_in[u], 16)
                    for u in range(U):
                        gather(u, 0)
                    with pool.Fori(0, n) as i:
                        for u in range(U):
                            pool.wait_ge(f_yo, i * U + u + 1)
                            pool.wait_ge(f_yi, i * U + u + 1)
                            pool.sem_inc(pool_passed, 1)
                            pool.indirect_dma_start(out, bass.IndirectOffsetOnAxis(yi[:, u:u + 1], 0), yo[:, u, :],
                                                    None, bounds_check=N - 1, oob_is_err=False)\
                                .then_inc(f_out[u], 16)
                            gather(u, i + 1)
                    for u in range(U):
                        pool.wait_ge(f_out[u], n * 16)
                        pool.wait_ge(f_in[u], (n + 1) * 16)
                        pool.sem_inc(pool_passed, 1)

                @block.scalar
                def _(act):
                    n = turns(act)
                    a = nc.scalar
                    for u in range(U):
                        a.copy(xi[:, u:u + 1], x_take[:, u + 1:u + 2]).then_inc(f_idx, 1)
                    with act.Fori(0, n) as i:
                        for u in range(U):
                            t = i * U + u
                            act.wait_ge(f_in[u], (i + 1) * 16)
                            a.copy(xi[:, u:u + 1], x_take[:, bass.ds(t + U + 1, 1)]).then_inc(f_idx, 1)
                            act.wait_ge(f_out[u], i * 16)
                            a.copy(yi[:, u:u + 1], y_put[:, bass.ds(t + 1, 1)]).then_inc(f_yi, 1)
                            act.wait_ge(f_mv, t + 1)
                            a.activation(sd2[:, u:u + 1], mv2[:, u, 1:2], ACT.Sqrt, bias=eps_t[:, 0:1])\
                                .then_inc(f_sd, 1)
                            act.wait_ge(f_nm, t + 1)
                            a.activation(yo[:, u, :], ys[:, u, :], ACT.Identity, bias=nm2[:, u:u + 1],
                                         scale=rs2[:, u:u + 1]).then_inc(f_yo, 1)

                @block.vector
                def _(dve):
                    v = nc.vector
                    n = turns(dve)
                    dve.sem_inc(f_y2, U)
                    with dve.Fori(0, n) as i:
                        for u in range(U):
                            t = i * U + u
                            dve.wait_ge(f_in[u], (i + 1) * 16)
                            dve.wait_ge(f_t[u], (i + 1) * 16)
                            dve.wait_ge(f_yo, i * U)
                            v.scalar_tensor_tensor(ys[:, u, :], tt[:, u, 0:C], mix[:, 0:1], xg[:, u, :],
                                                   ALU.mult, ALU.add).then_inc(f_y1, 1)
                            dve.wait_ge(f_y1, t + 1)
                            v.scalar_tensor_tensor(ys[:, u, :], tt[:, u, C:2 * C], mix[:, 1:2], ys[:, u, :],
                                                   ALU.mult, ALU.add).then_inc(f_y2, 1)
                            dve.wait_ge(f_y2, t + U + 1)
                            v.bn_stats(st2[:, u, :], ys[:, u, :]).then_inc(f_st, 1)
                            dve.wait_ge(f_st, t + 1)
                            dve.sem_inc(dve_passed, 1)
                            v.bn_aggr(mv2[:, u, :], st2[:, u, :]).then_inc(f_mv, 1)
                            dve.wait_ge(f_sd, t + 1)
                            v.reciprocal(rs2[:, u:u + 1], sd2[:, u:u + 1]).then_inc(f_rs, 1)
                            dve.wait_ge(f_rs, t + 1)
                            v.scalar_tensor_tensor(nm2[:, u:u + 1], mv2[:, u, 0:1], -1.0, rs2[:, u:u + 1],
                                                   ALU.mult, ALU.mult).then_inc(f_nm, 1)


_INS = ["x", "src", "dst", "L0_gnn_conv_W", "L0_gnn_conv_b", "L0_gnn_tr_W", "L0_gnn_tr_b", "L0_gnn_ln_g",
        "L0_gnn_ln_b", "L0_gnn_scale_weights", "L0_gnn_attn_W1", "L0_gnn_attn_b1", "L0_gnn_attn_W2",
        "L0_gnn_attn_b2"]


def kernel(**inputs):
    import numpy as _np
    import concourse.bacc as _bacc
    from concourse import mybir as _mybir
    from concourse.bass_utils import run_bass_kernel_spmd as _run

    nc = _bacc.Bacc("TRN2", target_bir_lowering=False, num_devices=1)
    arrays, args = {}, []
    for name in _INS:
        a = _np.ascontiguousarray(inputs[name])
        arrays[f"in_{name}"] = a
        args.append(nc.dram_tensor(f"in_{name}", a.shape, _mybir.dt.from_np(a.dtype), kind="ExternalInput").ap())
    out = nc.dram_tensor("out", inputs["x"].shape, F32, kind="ExternalOutput").ap()
    gnn_kernel(nc, *args, out)
    r = _run(nc, [arrays], core_ids=[0])
    return r.results[0]["out"]
```

```python
from contextlib import ExitStack

import concourse.bass as bass
from concourse import mybir

P = 128
ALU = mybir.AluOpType
ACT = mybir.ActivationFunctionType
F32 = mybir.dt.float32
BF16 = mybir.dt.bfloat16
FP16 = mybir.dt.float16
I32 = mybir.dt.int32
AX = mybir.AxisListType.X

N_EDGES = 20000
EPS = 1e-5
ROW = 260
G = 2
UNROLL = 2
BODY = G * UNROLL


class Chain:

    def __init__(self, eng, sem, base=0):
        self.eng, self.sem, self.base, self.n = eng, sem, base, 0

    def __call__(self, instruction):
        instruction.then_inc(self.sem, 1)
        self.n += 1
        self.eng.wait_ge(self.sem, self.base + self.n)


def gnn_kernel(nc, x, src, dst, conv_W, conv_b, tr_W, tr_b, ln_g, ln_b, scale_w, attn_W1, attn_b1, attn_W2,
               attn_b2, out):
    N, C = x.shape
    E = src.shape[0]
    NS = conv_W.shape[0]
    H = attn_W1.shape[1]
    assert C == 2 * P and H == P and NS == 2
    K = C // P
    BATCHES = -(-E // P)
    TB = -(-BATCHES // P) * P
    HI = -(-N // P)
    LAST = N_EDGES - 1
    PAD = 1 << 17
    assert PAD > N and PAD // P > HI and TB >= BATCHES + 2 * BODY

    E_TRASH = N_EDGES
    E_COLS = -(-(N_EDGES + G * P) // P)
    S_TRASH = P * HI
    S_COMMON = S_TRASH + G * P
    S_ROWS = S_COMMON + P
    LIST = -(-HI // 8) * 8
    TILES = LIST + 16
    T_ROWS = (1 + TILES) * P

    FIXED = 48
    COUNTED = {"edges": 10, "nodes": 11}
    assert BATCHES <= FIXED * sum(COUNTED.values()) <= TB
    MOST = max(COUNTED["edges"] + BODY, COUNTED["nodes"])
    ZE, ZN = 23, 8
    assert S_ROWS % P == 0 and S_ROWS // P // ZN >= 2 * FIXED
    FULL = N // (8 * P)
    REST = N - FULL * 8 * P
    REST_P = 112
    assert REST % REST_P == 0
    REST_R = REST // REST_P

    ctx = ExitStack()
    with ctx:
        def sb(name, shape, dt=F32):
            return ctx.enter_context(nc.sbuf_tensor(name, shape, dt))

        def sem(name):
            return ctx.enter_context(nc.semaphore(name))

        def dram(name, shape, dt=F32):
            return nc.dram_tensor(name, shape, dt, kind="Internal").ap()

        src_pad = dram("src_pad", [TB, P], I32)
        dst_pad = dram("dst_pad", [TB, P], I32)
        edge_sum = dram("edge_sum", [E_COLS * P, ROW])
        node_sum = dram("node_sum", [S_ROWS, C])
        factors = dram("factors", [S_ROWS, 2])
        transformed = dram("transformed", [T_ROWS, 2 * C])

        psum = [ctx.enter_context(nc.psum_tensor(f"bank{i}", [P, 512], F32)) for i in range(8)]

        ident = sb("ident", [P, P])
        ones = sb("ones", [P, P])
        ones3 = sb("ones3", [3, P], BF16)
        zeros_bf = sb("zeros_bf", [P, 512], BF16)
        iota_h = sb("iota_h", [P, HI], FP16)
        earlier = sb("earlier", [P, P])
        before = sb("before", [P, G, G, P])
        key_init = sb("key_init", [P, HI])
        part = sb("part", [P, 1])
        eps_t = sb("eps_t", [P, 1])
        own_hi = sb("own_hi", [P, TB])
        own_lo = sb("own_lo", [P, TB])
        is_live = sb("is_live", [P, TB])
        edge_row = sb("edge_row", [P, TB])
        edge_off = sb("edge_off", [P, TB])
        node_row = sb("node_row", [P, TB])
        node_off = sb("node_off", [P, TB])
        dst_key = sb("dst_key", [P, TB])
        src_key = sb("src_key", [P, TB])
        src_take = sb("src_take", [P, TB], I32)
        dst_take = sb("dst_take", [P, TB], I32)
        w_h = sb("w_h", [P, K, NS * C])
        bias3 = sb("bias3", [3, NS * C], BF16)
        w_a = sb("w_a", [P, K, H])
        b_a = sb("b_a", [P, 1])
        w2 = sb("w2", [P, NS])
        gain = sb("gain", [P, NS * C])
        shift = sb("shift", [P, NS * C])
        b2 = sb("b2", [P, NS])
        static_w = sb("static_w", [P, NS])
        common_q = sb("common_q", [P, C])
        zero_rows = sb("zero_rows", [P, ZE * ROW])
        one_hi = sb("one_hi", [P, MOST, HI], BF16)
        one_lo = sb("one_lo", [P, MOST, P], BF16)
        BANKS = [(0, 0, 512), (1, 512, HI)]
        sum_take = sb("sum_take", [P, TILES], I32)
        x_take = sb("x_take", [P, TILES], I32)
        y_put = sb("y_put", [P, TILES], I32)
        tile_weight = sb("tile_weight", [P, TILES])
        logits = sb("logits", [P, 1 + TILES, NS])
        counts_i = sb("counts_i", [1, 4], I32)
        mix = sb("mix", [P, NS])
        common_r = sb("common_r", [P, C])
        common_r3 = sb("common_r3", [3, 2 * C], BF16)

        pool_passed, dve_passed, sp_passed = sem("pool_passed"), sem("dve_passed"), sem("sp_passed")

        setup = ExitStack()
        with setup:
            def tb(name, shape, dt=F32):
                return setup.enter_context(nc.sbuf_tensor(name, shape, dt))

            raw = [tb("src_raw", [P, TB // P, P], I32), tb("dst_raw", [P, TB // P, P], I32)]
            rawf = [tb("src_rawf", [P, TB // P, P]), tb("dst_rawf", [P, TB // P, P])]
            tmp_i = tb("tmp_i", [P, TB], I32)
            tmp_j = tb("tmp_j", [P, TB], I32)
            tmp_f = tb("tmp_f", [P, TB])
            trash_i = tb("trash_i", [P, TB // G, G], I32)
            trash = tb("trash", [P, TB])
            batch_i = tb("batch_i", [P, TB], I32)
            hi_i = tb("hi_i", [P, HI], I32)
            part_i = tb("part_i", [P, 1], I32)
            cw = tb("cw", [P, NS, K, C])
            cwT = tb("cwT", [P, NS, K, C])
            tw = tb("tw", [P, NS, K, C])
            aw = tb("aw", [P, K, H])
            cb = tb("cb", [P, NS, K])
            cbB = tb("cbB", [P, NS, K, P])
            cb_sum = tb("cb_sum", [P, K])
            hb = tb("hb", [P, NS * C])
            hb_row = tb("hb_row", [P, NS * C])
            hb_part = tb("hb_part", [1, 3, NS * C], BF16)
            ab1 = tb("ab1", [P, 1])
            small = tb("small", [P, 16])
            sw = tb("sw", [P, NS])

            s_cleared, s_raw, s_padded, s_rawf, s_tr, s_tab = map(sem, (
                "s_cleared", "s_raw", "s_padded", "s_rawf", "s_tr", "s_tab"))
            s_wl, s_iota, s_wT, s_wTc, s_prod, s_dve, s_last, s_b3 = map(sem, (
                "s_wl", "s_iota", "s_wT", "s_wTc", "s_prod", "s_dve", "s_last", "s_b3"))
            s_pool, s_exp, s_parts, s_lastT, s_zero, s_einit = map(sem, (
                "s_pool", "s_exp", "s_parts", "s_lastT", "s_zero", "s_einit"))
            WHOLE = BATCHES - 1
            TAIL = E - WHOLE * P
            with nc.Block() as block:
                @block.sync
                def _(sp):
                    sp.wait_ge(s_zero, 1)
                    edge_v = edge_sum.rearrange("(p r) c -> p r c", p=P)
                    spans = [(lo, min(E_COLS, lo + ZE)) for lo in range(0, E_COLS, ZE)]
                    for lo, hi in spans:
                        sp.dma_start(edge_v[:, lo:hi, :],
                                     zero_rows[:, 0:(hi - lo) * ROW].rearrange("p (r c) -> p r c", c=ROW))\
                          .then_inc(s_einit, 16)
                    sp.wait_ge(s_cleared, 2)
                    n = 0
                    for t, a in zip(raw, (src, dst)):
                        chunks = WHOLE // P
                        sp.dma_start(t[:, 0:chunks, :], a[0:chunks * P * P].rearrange("(c r e) -> r c e", r=P, e=P))\
                          .then_inc(s_raw, 16)
                        more = WHOLE - chunks * P
                        sp.dma_start(t[0:more, chunks, :],
                                     a[chunks * P * P:WHOLE * P].rearrange("(r e) -> r e", e=P)).then_inc(s_raw, 16)
                        sp.dma_start(t[more:more + 1, chunks, 0:TAIL],
                                     a[WHOLE * P:E].rearrange("(r e) -> r e", r=1)).then_inc(s_raw, 16)
                        n += 3
                    sp.wait_ge(s_raw, 16 * n)
                    for t, d in zip(raw, (src_pad, dst_pad)):
                        sp.dma_start(d.rearrange("(c r) e -> r c e", r=P), t[:, :, :]).then_inc(s_padded, 16)
                    sp.wait_ge(s_parts, 1)
                    for k in range(3):
                        sp.dma_start(bias3[k:k + 1, :], hb_part[0:1, k, :]).then_inc(s_b3, 16)
                    sp.wait_ge(s_b3, 48)
                    sp.wait_ge(s_padded, 32)
                    sp.wait_ge(s_einit, 16 * len(spans))

                @block.scalar
                def _(act):
                    act.dma_start(cw[:, :, :, :], conv_W.rearrange("s (k p) c -> p s k c", p=P)).then_inc(s_wl, 16)
                    act.dma_start(tw[:, :, :, :], tr_W.rearrange("s (k p) c -> p s k c", p=P)).then_inc(s_wl, 16)
                    act.dma_start(aw[:, :, :], attn_W1.rearrange("(k p) h -> p k h", p=P)).then_inc(s_wl, 16)
                    act.dma_start(w2[:, :], attn_W2).then_inc(s_wl, 16)
                    with nc.allow_non_contiguous_dma(reason="small bias columns"):
                        act.dma_start(cb[:, :, :], conv_b.rearrange("s (k p) -> p s k", p=P)).then_inc(s_wl, 16)
                        act.dma_start(ab1[:, :], attn_b1.rearrange("(p a) -> p a", a=1)).then_inc(s_wl, 16)

                    def rows(t, a):
                        act.dma_start(t[:, :], a.to_broadcast([P, a.shape[1]])).then_inc(s_wl, 16)

                    flat = "s c -> (s c)"
                    rows(hb, tr_b.rearrange(flat).rearrange("(a n) -> a n", a=1))
                    rows(gain, ln_g.rearrange(flat).rearrange("(a n) -> a n", a=1))
                    rows(shift, ln_b.rearrange(flat).rearrange("(a n) -> a n", a=1))
                    rows(b2, attn_b2.rearrange("(a n) -> a n", a=1))
                    rows(sw, scale_w.rearrange("(a n) -> a n", a=1))
                    act.wait_ge(s_exp, 1)
                    nc.scalar.activation(small[:, 8:8 + NS], small[:, 4:4 + NS], ACT.Exp).then_inc(s_exp, 1)

                WL = 16 * 11

                @block.gpsimd
                def _(pool):
                    step = Chain(pool, s_pool)
                    nc.gpsimd.memset(raw[0][:, :, :], PAD).then_inc(s_cleared, 1)
                    nc.gpsimd.memset(raw[1][:, :, :], PAD).then_inc(s_cleared, 1)
                    nc.gpsimd.memset(zero_rows[:, :], 0.0).then_inc(s_zero, 1)
                    step(nc.gpsimd.memset(ident[:, :], 0.0))
                    step(nc.gpsimd.affine_select(out=ident[:, :], in_=ident[:, :], compare_op=ALU.not_equal, fill=1.0,
                                                 base=0, pattern=[[-1, P]], channel_multiplier=1))
                    step(nc.gpsimd.memset(ones[:, :], 1.0))
                    step(nc.gpsimd.memset(ones3[:, :], 1.0))
                    step(nc.gpsimd.memset(zeros_bf[:, :], 0.0))
                    step(nc.gpsimd.affine_select(out=earlier[:, :], in_=ones[:, :], compare_op=ALU.is_gt, fill=0.0,
                                                 base=0, pattern=[[-1, P]], channel_multiplier=1))
                    step(nc.gpsimd.memset(before[:, :, :, :], 0.0))
                    for b in range(G):
                        for f in range(b + 1):
                            step(nc.gpsimd.tensor_copy(before[:, b, f, :], earlier[:, :] if f == b else ones[:, :]))
                    step(nc.gpsimd.iota(hi_i[:, :], pattern=[[1, HI]], base=0, channel_multiplier=0))
                    step(nc.gpsimd.tensor_copy(iota_h[:, :], hi_i[:, :]))
                    step(nc.gpsimd.iota(part_i[:, :], pattern=[[0, 1]], base=0, channel_multiplier=1))
                    step(nc.gpsimd.tensor_copy(part[:, :], part_i[:, :]))
                    step(nc.gpsimd.iota(batch_i[:, :], pattern=[[1, TB]], base=1, channel_multiplier=0))
                    step(nc.gpsimd.iota(trash_i[:, :, :], pattern=[[0, TB // G], [P, G]], base=0,
                                        channel_multiplier=1))
                    step(nc.gpsimd.memset(eps_t[:, :], EPS))
                    step(nc.gpsimd.memset(logits[:, :, :], 0.0))
                    nc.gpsimd.tensor_copy(trash[:, :], trash_i[:, :, :].rearrange("p a b -> p (a b)"))\
                        .then_inc(s_iota, 1)

                @block.tensor
                def _(pe):
                    pe.wait_ge(s_iota, 1)
                    for j in range(2):
                        pe.wait_ge(s_rawf, j + 1)
                        for c in range(TB // P):
                            last = nc.tensor.transpose(psum[2 * j + c // 4][:, (c % 4) * P:(c % 4 + 1) * P],
                                                       rawf[j][:, c, :], ident[:, :])
                        last.then_inc(s_tr, 1)
                    pe.wait_ge(s_wl, WL)
                    for s in range(NS):
                        for k in range(K):
                            for m in range(K):
                                last = nc.tensor.transpose(psum[4 + s][:, m * C + k * P:m * C + (k + 1) * P],
                                                           cw[:, s, k, m * P:(m + 1) * P], ident[:, :])
                    last.then_inc(s_wT, 1)
                    pe.wait_ge(s_wTc, 1)
                    pe.wait_ge(s_tab, 2)
                    for k in range(K):
                        for s in range(NS):
                            for m in range(K):
                                last = nc.tensor.matmul(psum[k][:, s * C:(s + 1) * C],
                                                        cwT[:, s, m, k * P:(k + 1) * P], tw[:, s, m, :],
                                                        start=(m == 0), stop=(m == K - 1))
                    for k in range(K):
                        for n in range(NS * K):
                            s, m = n // K, n % K
                            last = nc.tensor.matmul(psum[2][:, k * H:(k + 1) * H],
                                                    cwT[:, s, m, k * P:(k + 1) * P], aw[:, m, :],
                                                    start=(n == 0), stop=(n == NS * K - 1))
                    for s in range(NS):
                        for m in range(K):
                            last = nc.tensor.matmul(psum[3][:, s * C:(s + 1) * C], cbB[:, s, m, :], tw[:, s, m, :],
                                                    start=(m == 0), stop=(m == K - 1))
                    for m in range(K):
                        last = nc.tensor.matmul(psum[6][:, 0:1], aw[:, m, :], cb_sum[:, m:m + 1],
                                                start=(m == 0), stop=(m == K - 1))
                    last.then_inc(s_prod, 1)
                    pe.wait_ge(s_last, 1)
                    nc.tensor.matmul(psum[7][0:1, 0:P], small[:, 0:1], ident[:, :], start=True, stop=True)\
                        .then_inc(s_lastT, 1)

                @block.vector
                def _(dve):
                    v = nc.vector
                    step = Chain(dve, s_dve)
                    dve.wait_ge(s_raw, 96)
                    for j in range(2):
                        v.tensor_copy(rawf[j][:, :, :], raw[j][:, :, :]).then_inc(s_rawf, 1)
                    dve.wait_ge(s_iota, 1)
                    for j, t in enumerate((src_key, dst_key)):
                        dve.wait_ge(s_tr, j + 1)
                        for h in range(TB // 512):
                            step(v.tensor_copy(t[:, h * 512:(h + 1) * 512], psum[2 * j + h][:, :]))
                        dve.sem_inc(s_tab, 1)
                    dve.wait_ge(s_wT, 1)
                    for s in range(NS):
                        step(v.tensor_copy(cwT[:, s, :, :], psum[4 + s][:, :].rearrange("p (m c) -> p m c", c=C)))
                        for m in range(K):
                            step(v.tensor_scalar(cbB[:, s, m, :], ones[:, :], cb[:, s, m:m + 1], None, ALU.mult))
                    step(v.tensor_tensor(cb_sum[:, :], cb[:, 0, :], cb[:, 1, :], ALU.add))
                    dve.sem_inc(s_wTc, 1)
                    step(v.tensor_scalar(edge_off[:, :], trash[:, :], float(E_TRASH), None, ALU.add))
                    step(v.tensor_tensor(tmp_f[:, :], edge_off[:, :], dst_key[:, :], ALU.subtract))
                    step(v.tensor_scalar(is_live[:, :], dst_key[:, :], float(N_EDGES), None, ALU.is_lt))
                    step(v.tensor_tensor(tmp_f[:, :], tmp_f[:, :], is_live[:, :], ALU.mult))
                    step(v.tensor_tensor(edge_row[:, :], edge_off[:, :], tmp_f[:, :], ALU.subtract))
                    step(v.tensor_copy(edge_off[:, :], tmp_f[:, :]))
                    step(v.tensor_copy(tmp_f[:, :], batch_i[:, :]))
                    step(v.tensor_tensor(tmp_f[:, :], tmp_f[:, :], is_live[:, :], ALU.mult))
                    step(v.reduce_max(small[:, 0:1], tmp_f[:, :], AX))
                    dve.sem_inc(s_last, 1)
                    step(v.tensor_scalar(is_live[:, :], dst_key[:, :], float(LAST), None, ALU.is_lt))
                    step(v.tensor_copy(tmp_i[:, :], src_key[:, :]))
                    step(v.tensor_scalar(tmp_j[:, :], tmp_i[:, :], 7, None, ALU.arith_shift_right))
                    step(v.tensor_copy(own_hi[:, :], tmp_j[:, :]))
                    step(v.tensor_scalar(tmp_j[:, :], tmp_i[:, :], P - 1, None, ALU.bitwise_and))
                    step(v.tensor_copy(own_lo[:, :], tmp_j[:, :]))
                    step(v.scalar_tensor_tensor(node_row[:, :], own_lo[:, :], float(HI), own_hi[:, :],
                                                ALU.mult, ALU.add))
                    step(v.tensor_scalar(trash[:, :], trash[:, :], float(S_TRASH), None, ALU.add))
                    step(v.tensor_tensor(tmp_f[:, :], trash[:, :], node_row[:, :], ALU.subtract))
                    step(v.tensor_scalar(node_off[:, :], src_key[:, :], float(N), None, ALU.is_lt))
                    step(v.tensor_tensor(node_off[:, :], node_off[:, :], tmp_f[:, :], ALU.mult))
                    step(v.tensor_tensor(node_row[:, :], trash[:, :], node_off[:, :], ALU.subtract))
                    step(v.tensor_scalar(src_take[:, :], src_key[:, :], float(N - 1), None, ALU.min))
                    step(v.tensor_scalar(dst_take[:, :], dst_key[:, :], float(LAST), None, ALU.min))
                    dve.wait_ge(s_lastT, 1)
                    step(v.reduce_max(small[0:1, 1:2], psum[7][0:1, 0:P], AX))
                    step(v.tensor_scalar(small[0:1, 1:2], small[0:1, 1:2], float((FIXED + 1) * BODY),
                                         float(BODY - 1), ALU.max, ALU.add))
                    step(v.tensor_copy(counts_i[0:1, 1:2], small[0:1, 1:2]))
                    step(v.tensor_scalar(counts_i[0:1, 0:1], counts_i[0:1, 1:2], BODY.bit_length() - 1, None,
                                         ALU.arith_shift_right))
                    dve.wait_ge(s_prod, 1)
                    step(v.tensor_tensor(hb[:, :], hb[:, :], psum[3][:, :], ALU.add))
                    for s in range(NS):
                        cols = slice(s * C, (s + 1) * C)
                        for k in range(K + 1):
                            row = psum[k][:, cols] if k < K else hb[:, cols]
                            to = w_h[:, k, cols] if k < K else hb_row[:, cols]
                            step(v.reduce_sum(small[:, 2:3], row, AX))
                            step(v.tensor_scalar(small[:, 3:4], small[:, 2:3], 1.0 / C, None, ALU.mult))
                            step(v.tensor_scalar(to, row, small[:, 3:4], None, ALU.subtract))
                    for k in range(3):
                        step(v.tensor_copy(hb_part[0:1, k, :], hb_row[0:1, :]))
                        step(v.tensor_tensor(hb_row[0:1, :], hb_row[0:1, :], hb_part[0:1, k, :], ALU.subtract))
                    dve.sem_inc(s_parts, 1)
                    step(v.tensor_scalar(w_a[:, :, :], psum[2][:, 0:K * H].rearrange("p (k h) -> p k h", h=H),
                                         1.0 / NS, None, ALU.mult))
                    step(v.scalar_tensor_tensor(b_a[:, :], psum[6][:, 0:1], 1.0 / NS, ab1[:, :], ALU.mult, ALU.add))
                    step(v.reduce_max(small[:, 2:3], sw[:, :], AX))
                    step(v.tensor_scalar(small[:, 4:4 + NS], sw[:, :], small[:, 2:3], None, ALU.subtract))
                    dve.sem_inc(s_exp, 1)
                    dve.wait_ge(s_exp, 2)
                    step(v.reduce_sum(small[:, 2:3], small[:, 8:8 + NS], AX))
                    step(v.reciprocal(small[:, 3:4], small[:, 2:3]))
                    step(v.tensor_scalar(static_w[:, :], small[:, 8:8 + NS], small[:, 3:4], None, ALU.mult))

        def count(eng, j, most, least=1):
            return eng.value_load(counts_i[0:1, j:j + 1], min_val=least, max_val=most)

        BODIES = -(-BATCHES // BODY)

        def segment_sums(name, keys_dram, key, table, take, row, off, target, from_edges):
            st = ExitStack()
            with st:
                def tb(nm, shape, dt=F32):
                    return st.enter_context(nc.sbuf_tensor(f"{name}_{nm}", shape, dt))

                def sm(nm):
                    return sem(f"{name}_{nm}")

                taken = tb("taken", [P, UNROLL, G, ROW])
                merged = tb("merged", [P, UNROLL, G, ROW])
                key_rows = tb("key_rows", [P, UNROLL, G * P], I32)
                equal = tb("equal", [P, UNROLL, G, G * P])
                junk = tb("junk", [P, UNROLL, G, G * P])
                repeats = tb("repeats", [P, UNROLL, G])
                shiftf = tb("shiftf", [P, UNROLL, G])
                factor = tb("factor", [P, UNROLL, G])
                put_idx = tb("put_idx", [P, UNROLL, G], I32)
                take_idx = tb("take_idx", [P, UNROLL, G], I32)
                cols = C if from_edges else ROW
                counted = COUNTED[name]
                counted_from = COUNTED["edges"] * FIXED if from_edges else 0
                live_too = 0 if from_edges else BODY

                def one_hots(i, u, fixed):
                    lives = [(i * BODY + k, True) for k in range(live_too)]
                    alls = [(i * counted + counted_from + k, False) for k in range(counted)] if fixed else []
                    items = lives + alls
                    first = i * len(items) if fixed else (i - FIXED) * len(items) + FIXED * (live_too + counted)
                    half = -(-len(items) // 2)
                    return [(first + k, k, *items[k]) for k in range(len(items))
                            if (k >= half) == bool(u)]

                def both(eng, n, turn):
                    with eng.Fori(0, FIXED) as i:
                        turn(i, True)
                    with eng.Fori(FIXED, n) as i:
                        turn(i, False)

                def turns(eng):
                    return count(eng, 0, BODIES + 1, FIXED + 1)

                keys_in = [sm(f"keys_in{u}") for u in range(UNROLL)]
                gathered = [sm(f"gathered{u}") for u in range(UNROLL)]
                added = [sm(f"added{u}") for u in range(UNROLL)]
                take_ready = [sm(f"take_ready{u}") for u in range(UNROLL)]
                hot, hot_used, zeroed = sm("hot"), sm("hot_used"), sm("zeroed")
                equal_ready, put_ready, products, evacuated, steps, cleared, offset = map(sm, (
                    "equal_ready", "put_ready", "products", "evacuated", "steps", "cleared", "offset"))
                with nc.Block() as block:
                    @block.sync
                    def _(sp):
                        n = turns(sp)
                        node_v = node_sum.rearrange("(p r) c -> p (r c)", p=P)
                        zero_dmas = S_ROWS // P // ZN

                        def zero(at, rows):
                            sp.dma_start(node_v[:, bass.ds(at * C, rows * C)], zero_rows[:, 0:rows * C])\
                              .then_inc(zeroed, 16)

                        def turn(i, fixed):
                            for u in range(UNROLL):
                                g = i * UNROLL + u
                                sp.wait_ge(put_ready, g + 1)
                                sp.dma_start(key_rows[:, u, :],
                                             keys_dram[bass.ds(g * G, G), :].rearrange("g p -> (g p)")
                                             .rearrange("(a n) -> a n", a=1).to_broadcast([P, G * P]))\
                                  .then_inc(keys_in[u], 16)
                                if fixed and not from_edges:
                                    zero(g * ZN, ZN)

                        both(sp, n, turn)
                        if not from_edges:
                            for k in range(FIXED * UNROLL, zero_dmas):
                                zero(k * ZN, ZN)
                            zero(zero_dmas * ZN, S_ROWS // P - zero_dmas * ZN)
                            sp.wait_ge(zeroed, 16 * (zero_dmas + 1))

                    @block.scalar
                    def _(act):
                        n = turns(act)
                        act.sem_inc(evacuated, UNROLL)
                        for u in range(UNROLL):
                            nc.scalar.copy(take_idx[:, u, :], take[:, u * G:(u + 1) * G]).then_inc(take_ready[u], 1)
                        act.wait_ge(cleared, 2)
                        def turn(i, fixed):
                            for u in range(UNROLL):
                                g = i * UNROLL + u
                                act.wait_ge(gathered[u], (i + 1) * 16 * G)
                                nc.scalar.copy(take_idx[:, u, :], take[:, bass.ds((g + UNROLL) * G, G)])\
                                    .then_inc(take_ready[u], 1)
                                act.wait_ge(products, g + UNROLL + 1)
                                act.wait_ge(added[u], i * 16 * G)
                                for b in range(G):
                                    last = nc.scalar.copy(merged[:, u, b, 0:cols], psum[u * G + b][:, 0:cols])
                                last.then_inc(evacuated, 1)

                        both(act, n, turn)

                    @block.tensor
                    def _(pe):
                        n = turns(pe)
                        pe.sem_inc(products, UNROLL)
                        if not from_edges:
                            for b in range(4, 8):
                                nc.tensor.matmul(psum[b][:, :], zeros_bf[:, 0:P], zeros_bf[:, :], start=True,
                                                 stop=False, skip_group_check=True)
                        pe.sem_inc(hot_used, live_too + counted)

                        def turn(i, fixed):
                            for u in range(UNROLL):
                                g = i * UNROLL + u
                                pe.wait_ge(gathered[u], (i + 1) * 16 * G)
                                pe.wait_ge(equal_ready, g + 1)
                                pe.wait_ge(evacuated, g + 1)
                                for b in range(G):
                                    for f in range(G):
                                        last = nc.tensor.matmul(psum[u * G + b][:, 0:cols],
                                                                equal[:, u, f, b * P:(b + 1) * P],
                                                                taken[:, u, f, 0:cols],
                                                                start=(f == 0), stop=(f == G - 1))
                                last.then_inc(products, 1)
                                for o, k, _, live_only in one_hots(i, u, fixed):
                                    pe.wait_ge(hot, o + 1)
                                    for b, lo, hi in BANKS:
                                        last = nc.tensor.matmul(psum[(6 if live_only else 4) + b][:, 0:hi - lo],
                                                                one_lo[:, k, :], one_hi[:, k, lo:hi],
                                                                start=False, stop=False, skip_group_check=True)
                                    last.then_inc(hot_used, 1)

                        both(pe, n, turn)
                        if from_edges:
                            for b in range(4, 8):
                                nc.tensor.matmul(psum[b][:, :], zeros_bf[:, 0:P], zeros_bf[:, :], start=False,
                                                 stop=True, skip_group_check=True)

                    @block.vector
                    def _(dve):
                        v = nc.vector
                        n = turns(dve)
                        dve.sem_inc(put_ready, UNROLL)
                        per_group = 4 if from_edges else 1

                        def turn(i, fixed):
                            for u in range(UNROLL):
                                g = i * UNROLL + u
                                step = Chain(dve, steps, g * per_group)
                                pair = bass.ds(g * G, G)
                                if from_edges:
                                    dve.wait_ge(gathered[u], (i + 1) * 16 * G)
                                    step(v.tensor_scalar(factor[:, u, :], taken[:, u, :, C], 1.0, None, ALU.max))
                                    step(v.reciprocal(factor[:, u, :], factor[:, u, :]))
                                    step(v.tensor_tensor(factor[:, u, :], factor[:, u, :], is_live[:, pair], ALU.mult))
                                dve.wait_ge(keys_in[u], (i + 1) * 16)
                                dve.wait_ge(products, g + 1)
                                for f in range(G):
                                    k = key[:, bass.ds(g * G + f, 1)]
                                    if from_edges:
                                        last = v.tensor_scalar(equal[:, u, f, :], key_rows[:, u, :], k,
                                                               factor[:, u, f:f + 1], ALU.is_equal, ALU.mult)
                                    else:
                                        last = v.tensor_scalar(equal[:, u, f, :], key_rows[:, u, :], k, None,
                                                               ALU.is_equal)
                                last.then_inc(equal_ready, 1)
                                for b in range(G):
                                    w = (b + 1) * P
                                    last = v.scalar_tensor_tensor(
                                        junk[:, u, b, 0:w], key_rows[:, u, 0:w], key[:, bass.ds(g * G + b, 1)],
                                        before[:, b, :, :].rearrange("p a b -> p (a b)")[:, 0:w],
                                        ALU.is_equal, ALU.mult, accum_out=repeats[:, u, b:b + 1])
                                    if b == G - 1:
                                        step(last)
                                v.scalar_tensor_tensor(shiftf[:, u, :], repeats[:, u, :], 1.0, off[:, pair],
                                                       ALU.min, ALU.mult).then_inc(offset, 1)
                                dve.wait_ge(offset, g + 1)
                                dve.wait_ge(added[u], i * 16 * G)
                                v.tensor_tensor(put_idx[:, u, :], shiftf[:, u, :], row[:, pair], ALU.add)\
                                    .then_inc(put_ready, 1)
                                for o, k, b, live_only in one_hots(i, u, fixed):
                                    dve.wait_ge(hot_used, o + 1 + (0 if fixed else counted))
                                    if live_only:
                                        v.tensor_scalar(one_lo[:, k, :], iota_h[:, 0:P], own_lo[:, bass.ds(b, 1)],
                                                        is_live[:, bass.ds(b, 1)], ALU.is_equal, ALU.mult)
                                    else:
                                        v.tensor_scalar(one_lo[:, k, :], iota_h[:, 0:P], own_lo[:, bass.ds(b, 1)],
                                                        None, ALU.is_equal)
                                    v.tensor_scalar(one_hi[:, k, :], iota_h[:, :], own_hi[:, bass.ds(b, 1)], None,
                                                    ALU.is_equal).then_inc(hot, 1)

                        both(dve, n, turn)

                    @block.gpsimd
                    def _(pool):
                        n = turns(pool)
                        nc.gpsimd.memset(merged[:, :, :, :], 0.0).then_inc(cleared, 1)
                        nc.gpsimd.memset(taken[:, :, :, :], 0.0).then_inc(cleared, 1)
                        pool.wait_ge(cleared, 2)
                        if not from_edges:
                            nc.gpsimd.memset(taken[:, :, :, C:C + 1], 1.0).then_inc(cleared, 1)
                            pool.wait_ge(cleared, 3)

                        def gather(u, turn):
                            pool.wait_ge(take_ready[u], turn + 1)
                            for b in range(G):
                                pool.sem_inc(pool_passed, 1)
                                pool.indirect_dma_start(
                                    taken[:, u, b, 0:table.shape[1]], None, table,
                                    bass.IndirectOffsetOnAxis(take_idx[:, u, b:b + 1], 0)).then_inc(gathered[u], 16)

                        for u in range(UNROLL):
                            gather(u, 0)
                        def turn(i, fixed):
                            for u in range(UNROLL):
                                g = i * UNROLL + u
                                pool.wait_ge(products, g + UNROLL + 1)
                                gather(u, i + 1)
                                pool.wait_ge(evacuated, g + UNROLL + 1)
                                pool.wait_ge(put_ready, g + UNROLL + 1)
                                if u:
                                    pool.wait_ge(added[u - 1], (i + 1) * 16 * G)
                                else:
                                    pool.wait_ge(added[UNROLL - 1], i * 16 * G)
                                for b in range(G):
                                    pool.sem_inc(pool_passed, 1)
                                    pool.indirect_dma_start(
                                        target, bass.IndirectOffsetOnAxis(put_idx[:, u, b:b + 1], 0),
                                        merged[:, u, b, 0:cols], None, compute_op=ALU.add).then_inc(added[u], 16)

                        both(pool, n, turn)
                        for u in range(UNROLL):
                            pool.wait_ge(gathered[u], (n + 1) * 16 * G)
                            pool.wait_ge(added[u], n * 16 * G)
                            pool.sem_inc(pool_passed, 1)

        segment_sums("edges", dst_pad, dst_key, x, src_take, edge_row, edge_off, edge_sum, False)
        segment_sums("nodes", src_pad, src_key, edge_sum, dst_take, node_row, node_off, node_sum, True)

        ls = ExitStack()
        with ls:
            def tb(name, shape, dt=F32):
                return ls.enter_context(nc.sbuf_tensor(name, shape, dt))

            total = tb("total", [P, HI])
            live = tb("live", [P, HI])
            common_deg = tb("common_deg", [P, HI])
            pair = tb("pair", [P, HI, 2])
            flag = tb("flag", [P, HI])
            keys = tb("keys", [P, 2, HI])
            listed = tb("listed", [P, TILES])
            top = tb("top", [P, 8])
            dsm = tb("dsm", [P, 8])
            common_pair = tb("common_pair", [P, 2])
            valid = tb("valid", [P, TILES])
            l_step, l_top, l_count, l_sums, l_key, l_factors, l_pair = map(sem, (
                "l_step", "l_top", "l_count", "l_sums", "l_key", "l_factors", "l_pair"))
            with nc.Block() as block:
                @block.vector
                def _(dve):
                    v = nc.vector
                    step = Chain(dve, l_step)
                    for b, lo, hi in BANKS:
                        step(v.tensor_copy(total[:, lo:hi], psum[4 + b][:, 0:hi - lo]))
                        step(v.tensor_copy(live[:, lo:hi], psum[6 + b][:, 0:hi - lo]))
                    step(v.tensor_scalar(flag[:, :], total[:, :], 0.5, None, ALU.is_lt))
                    step(v.scalar_tensor_tensor(flag[:, :], live[:, :], 0.5, flag[:, :], ALU.is_gt, ALU.max))
                    dve.wait_ge(l_key, 2)
                    step(v.tensor_tensor(keys[:, 0, :], flag[:, :], key_init[:, :], ALU.mult))
                    step(v.tensor_scalar(flag[:, :], keys[:, 0, :], 0.5, None, ALU.is_gt))
                    step(v.reduce_sum(dsm[:, 0:1], flag[:, :], AX))
                    dve.sem_inc(l_count, 1)
                    step(v.tensor_tensor(pair[:, :, 1], total[:, :], live[:, :], ALU.subtract))
                    step(v.tensor_scalar(total[:, :], total[:, :], 1.0, None, ALU.max))
                    step(v.reciprocal(pair[:, :, 0], total[:, :]))
                    dve.sem_inc(l_pair, 1)
                    step(v.memset(listed[:, :], 0.0))
                    dve.wait_ge(l_sums, 1)
                    step(v.reduce_max(dsm[0:1, 1:2], psum[0][0:1, 0:P], AX))
                    step(v.tensor_scalar(dsm[0:1, 3:4], dsm[0:1, 1:2], 1.0, 7.0, ALU.max, ALU.add))
                    step(v.tensor_copy(counts_i[0:1, 3:4], dsm[0:1, 3:4]))
                    step(v.tensor_scalar(counts_i[0:1, 2:3], counts_i[0:1, 3:4], 3, None, ALU.arith_shift_right))
                    eights = count(dve, 2, LIST // 8)
                    with dve.Fori(0, eights) as i:
                        pick = Chain(dve, l_top, i * 4)
                        pick(v.max(top[:, :], keys[:, 0, :]))
                        dve.sem_inc(dve_passed, 1)
                        pick(v.match_replace(keys[:, 1, :], top[:, :], keys[:, 0, :], 0.0))
                        pick(v.tensor_copy(keys[:, 0, :], keys[:, 1, :]))
                        pick(v.tensor_copy(listed[:, bass.ds(i * 8 + 1, 8)], top[:, :]))
                    step(v.tensor_scalar(valid[:, :], listed[:, :], 0.5, None, ALU.is_gt))
                    step(v.tensor_scalar(listed[:, :], listed[:, :], 1.0, 0.0, ALU.subtract, ALU.max))
                    step(v.tensor_scalar(dsm[:, 4:5], part[:, :], float(HI), None, ALU.mult))
                    step(v.tensor_scalar(sum_take[:, :], listed[:, :], dsm[:, 4:5], None, ALU.add))
                    step(v.tensor_scalar(listed[:, :], listed[:, :], float(P), part[:, 0:1], ALU.mult, ALU.add))
                    step(v.tensor_copy(x_take[:, :], listed[:, :]))
                    step(v.tensor_scalar(tile_weight[:, :], valid[:, :], float(-PAD), float(PAD), ALU.mult, ALU.add))
                    step(v.tensor_tensor(y_put[:, :], listed[:, :], tile_weight[:, :], ALU.add))
                    step(v.tensor_copy(tile_weight[:, :], valid[:, :]))
                    step(v.memset(sum_take[:, 0:1], S_COMMON))
                    dve.wait_ge(l_sums, 2)
                    step(v.tensor_scalar(tile_weight[:, 0:1], psum[1][:, 0:1], -1.0 / P, float(N) / P,
                                         ALU.mult, ALU.add))

                @block.tensor
                def _(pe):
                    pe.wait_ge(l_count, 1)
                    nc.tensor.matmul(psum[0][0:1, 0:P], dsm[:, 0:1], ident[:, :], start=True, stop=True)\
                        .then_inc(l_sums, 1)
                    nc.tensor.matmul(psum[1][:, 0:1], ones[:, :], dsm[:, 0:1], start=True, stop=True)\
                        .then_inc(l_sums, 1)

                @block.gpsimd
                def _(pool):
                    nc.gpsimd.iota(key_init[:, :], pattern=[[1, HI]], base=1, channel_multiplier=0,
                                   allow_small_or_imprecise_dtypes=True).then_inc(l_key, 1)
                    pool.wait_ge(l_key, 1)
                    nc.gpsimd.affine_select(out=key_init[:, :], in_=key_init[:, :], compare_op=ALU.is_gt, fill=0.0,
                                            base=N, pattern=[[-P, HI]], channel_multiplier=-1).then_inc(l_key, 1)
                    nc.gpsimd.memset(common_pair[:, :], 1.0).then_inc(l_pair, 1)

                @block.sync
                def _(sp):
                    sp.wait_ge(l_pair, 2)
                    sp.dma_start(factors[0:S_TRASH, :].rearrange("(p r) c -> p (r c)", p=P),
                                 pair[:, :, :].rearrange("p r c -> p (r c)")).then_inc(l_factors, 16)
                    for r in range(S_TRASH, S_ROWS, P):
                        sp.dma_start(factors[r:r + P, :], common_pair[:, :]).then_inc(l_factors, 16)
                    sp.wait_ge(l_factors, 16 * (2 + G))

        rt = ExitStack()
        with rt:
            def tb(name, shape, dt=F32):
                return rt.enter_context(nc.sbuf_tensor(name, shape, dt))

            UT = 4
            sums = tb("sums", [P, UT, C])
            fac = tb("fac", [P, UT, 2])
            q = tb("q", [P, 2, C])
            qT = tb("qT", [P, 2, K, P])
            aT = tb("aT", [P, 2, P])
            sq = tb("sq", [P, 2, NS * C])
            ssq = tb("ssq", [P, 2, NS])
            inv = tb("inv", [P, 2, NS])
            tr = tb("tr", [P, 2, NS * C])
            res = tb("res", [P, 2, NS * C])
            sidx = tb("sidx", [P, UT], I32)
            last_row = tb("last_row", [P, ROW])
            cfac = tb("cfac", [P, 1])
            sum_in = [sem(f"sum_in{u}") for u in range(UT)]
            fac_in = [sem(f"fac_in{u}") for u in range(UT)]
            res_out = [sem("res_out0"), sem("res_out1")]
            (t_idx, t_qa, t_q, t_tp, t_qT, t_h, t_aT, t_lg, t_lgc, t_ssq, t_std, t_inv, t_sc, t_sh, t_res, t_row,
             t_cq, t_at, t_clear) = map(sem, (
                "t_idx", "t_qa", "t_q", "t_tp", "t_qT", "t_h", "t_aT", "t_lg", "t_lgc", "t_ssq", "t_std", "t_inv",
                "t_sc", "t_sh", "t_res", "t_row", "t_cq", "t_at", "t_clear"))
            tiles_v = transformed.rearrange("(t p) c -> t p c", p=P)

            with nc.Block() as block:
                def turns(eng):
                    return count(eng, 2, LIST // 8) * (8 // UT) + 1

                @block.sync
                def _(sp):
                    n = turns(sp)
                    sp.dma_start(last_row[:, :], edge_sum[LAST:LAST + 1, :].to_broadcast([P, ROW])).then_inc(t_row, 16)

                    def store(t, w):
                        sp.wait_ge(t_res, t + 1)
                        sp.dma_start(tiles_v[bass.ds(t, 1), :, :].rearrange("a p c -> (a p) c"), res[:, w, :])\
                          .then_inc(res_out[w], 16)

                    with sp.Fori(0, n) as i:
                        for u in range(UT):
                            store(i * UT + u, 1 - u % 2)
                    store(n * UT, 1)
                    sp.wait_ge(res_out[0], n * (UT // 2 * 16))
                    sp.sem_inc(sp_passed, 1)
                    sp.wait_ge(res_out[1], n * (UT // 2 * 16) + 16)
                    sp.sem_inc(sp_passed, 1)

                @block.gpsimd
                def _(pool):
                    n = turns(pool)
                    nc.gpsimd.memset(aT[:, :, :], 0.0).then_inc(t_clear, 1)
                    nc.gpsimd.memset(tr[:, :, :], 0.0).then_inc(t_clear, 1)

                    def gather(u, t):
                        pool.wait_ge(t_idx, t + 1)
                        pool.sem_inc(pool_passed, 1)
                        pool.indirect_dma_start(sums[:, u, :], None, node_sum,
                                                bass.IndirectOffsetOnAxis(sidx[:, u:u + 1], 0))\
                            .then_inc(sum_in[u], 16)
                        pool.indirect_dma_start(fac[:, u, :], None, factors,
                                                bass.IndirectOffsetOnAxis(sidx[:, u:u + 1], 0))\
                            .then_inc(fac_in[u], 16)

                    for u in range(UT):
                        gather(u, u)
                    with pool.Fori(0, n) as i:
                        for u in range(UT):
                            t = i * UT + u
                            pool.wait_ge(t_q, t + 1)
                            gather(u, t + UT)
                    for u in range(UT):
                        pool.wait_ge(sum_in[u], (n + 1) * 16)
                        pool.wait_ge(fac_in[u], (n + 1) * 16)
                    pool.sem_inc(pool_passed, 1)

                @block.scalar
                def _(act):
                    n = turns(act)
                    a = nc.scalar

                    def transposed(t, w):
                        act.wait_ge(t_tp, t + 1)
                        a.copy(qT[:, w, :, :], psum[w][:, 0:C].rearrange("p (k n) -> p k n", n=P)).then_inc(t_qT, 1)

                    def finish(t, w, used):
                        act.wait_ge(t_sh, t + 1)
                        act.wait_ge(res_out[w], used * 16)
                        a.activation(res[:, w, :], tr[:, w, :], ACT.Relu).then_inc(t_res, 1)

                    a.activation(ssq[:, 0, 0:1], eps_t[:, 0:1], ACT.Sqrt).then_inc(t_clear, 1)
                    for u in range(UT):
                        a.copy(sidx[:, u:u + 1], sum_take[:, u:u + 1]).then_inc(t_idx, 1)
                    act.wait_ge(t_clear, 3)
                    transposed(0, 0)
                    with act.Fori(0, n) as i:
                        for b in range(UT):
                            t = i * UT + b
                            u = b % 2
                            act.wait_ge(sum_in[b], (i + 1) * 16)
                            act.wait_ge(fac_in[b], (i + 1) * 16)
                            a.copy(sidx[:, b:b + 1], sum_take[:, bass.ds(t + UT, 1)]).then_inc(t_idx, 1)
                            act.wait_ge(t_h, t)
                            transposed(t + 1, 1 - u)
                            act.wait_ge(t_at, t + 1)
                            a.activation(aT[:, u, :], psum[4 + u][:, 0:P], ACT.Relu, bias=b_a[:, 0:1])\
                                .then_inc(t_aT, 1)
                            act.wait_ge(t_h, t + 1)
                            for s in range(NS):
                                last = a.activation(sq[:, u, s * C:(s + 1) * C], psum[2 + u][:, s * C:(s + 1) * C],
                                                    ACT.Square, accum_out=ssq[:, u, s:s + 1])
                            last.then_inc(t_ssq, 1)
                            act.wait_ge(t_ssq, t + 1)
                            a.activation(ssq[:, u, :], ssq[:, u, :], ACT.Sqrt, bias=eps_t[:, 0:1], scale=1.0 / C)\
                                .then_inc(t_std, 1)
                            finish(t, 1 - u, i * (UT // 2) + b // 2)
                    finish(n * UT, 1, n * (UT // 2))

                @block.vector
                def _(dve):
                    v = nc.vector
                    n = turns(dve)
                    dve.sem_inc(t_sh, 1)
                    dve.sem_inc(t_lgc, 2)
                    step = Chain(dve, t_cq)
                    dve.wait_ge(t_row, 16)
                    step(v.tensor_scalar(cfac[:, :], last_row[:, C:C + 1], 1.0, None, ALU.max))
                    step(v.reciprocal(cfac[:, :], cfac[:, :]))
                    step(v.tensor_scalar(common_q[:, :], last_row[:, 0:C], cfac[:, 0:1], None, ALU.mult))

                    def means(t, b, i):
                        u = b % 2
                        dve.wait_ge(sum_in[b], (i + 1) * 16)
                        dve.wait_ge(fac_in[b], (i + 1) * 16)
                        v.scalar_tensor_tensor(q[:, u, :], common_q[:, :], fac[:, b, 1:2],
                                               sums[:, b, :], ALU.mult, ALU.add).then_inc(t_qa, 1)
                        dve.wait_ge(t_qa, t + 1)
                        v.tensor_scalar(q[:, u, :], q[:, u, :], fac[:, b, 0:1], None, ALU.mult)\
                            .then_inc(t_q, 1)

                    def take_logits(t, w):
                        dve.wait_ge(t_lg, t + 1)
                        v.tensor_copy(logits[:, bass.ds(t, 1), :].rearrange("p a s -> p (a s)"),
                                      psum[6 + w][:, 0:NS]).then_inc(t_lgc, 1)

                    for u in range(2):
                        means(u, u, 0)
                    with dve.Fori(0, n) as i:
                        for b in range(UT):
                            t = i * UT + b
                            u = b % 2
                            dve.wait_ge(t_tp, t + 1)
                            means(t + 2, (b + 2) % UT, i + (b + 2) // UT)
                            take_logits(t, 1 - u)
                            dve.wait_ge(t_std, t + 1)
                            v.reciprocal(inv[:, u, :], ssq[:, u, :]).then_inc(t_inv, 1)
                            dve.wait_ge(t_inv, t + 1)
                            dve.wait_ge(t_res, t)
                            for s in range(NS):
                                c = slice(s * C, (s + 1) * C)
                                last = v.scalar_tensor_tensor(tr[:, u, c], psum[2 + u][:, c], inv[:, u, s:s + 1],
                                                              gain[:, c], ALU.mult, ALU.mult)
                            last.then_inc(t_sc, 1)
                            dve.wait_ge(t_sc, t + 1)
                            v.tensor_tensor(tr[:, u, :], tr[:, u, :], shift[:, :], ALU.add).then_inc(t_sh, 1)
                    take_logits(n * UT, 1)

                @block.tensor
                def _(pe):
                    n = turns(pe)
                    m = nc.tensor

                    def turn_rows(t, w):
                        pe.wait_ge(t_q, t + 1)
                        for k in range(K):
                            last = m.transpose(psum[w][:, k * P:(k + 1) * P], q[:, w, k * P:(k + 1) * P], ident[:, :])
                        last.then_inc(t_tp, 1)

                    def attend(t, w):
                        pe.wait_ge(t_aT, t)
                        pe.wait_ge(t_lgc, t + 1)
                        m.matmul(psum[6 + w][:, 0:NS], aT[:, w, :], w2[:, :], start=True, stop=True)\
                            .then_inc(t_lg, 1)

                    pe.wait_ge(t_clear, 3)
                    turn_rows(0, 0)
                    with pe.Fori(0, n) as i:
                        for b in range(UT):
                            t = i * UT + b
                            u = b % 2
                            pe.wait_ge(t_qT, t)
                            turn_rows(t + 1, 1 - u)
                            attend(t, 1 - u)
                            pe.wait_ge(t_qT, t + 1)
                            for k in range(K):
                                last = m.matmul(psum[4 + u][:, 0:P], w_a[:, k, :], qT[:, u, k, :], start=(k == 0),
                                                stop=(k == K - 1))
                            last.then_inc(t_at, 1)
                            pe.wait_ge(t_sh, t)
                            m.matmul(psum[2 + u][:, :], ones3[:, :], bias3[:, :], start=True, stop=False)
                            for k in range(K):
                                last = m.matmul(psum[2 + u][:, :], qT[:, u, k, :], w_h[:, k, :], start=False,
                                                stop=(k == K - 1))
                            last.then_inc(t_h, 1)
                    attend(n * UT, 1)

        wt = ExitStack()
        with wt:
            def tb(name, shape, dt=F32):
                return wt.enter_context(nc.sbuf_tensor(name, shape, dt))

            l = tb("l", [P, NS, TILES])
            mx = tb("mx", [P, TILES])
            ex = tb("ex", [P, NS, TILES])
            tot = tb("tot", [P, TILES])
            acc = tb("acc", [P, NS])
            t0 = tb("t0", [P, NS * C])
            r_part = tb("r_part", [1, 3, 2 * C], BF16)
            w_d, w_a0, w_e, w_s, w_t, w_p = map(sem, ("w_d", "w_a0", "w_e", "w_s", "w_t", "w_p"))
            w_p3 = sem("w_p3")
            with nc.Block() as block:
                @block.sync
                def _(sp):
                    sp.dma_start(t0[:, :], transformed[P:2 * P, :]).then_inc(w_t, 16)
                    sp.wait_ge(w_p, 1)
                    for k in range(3):
                        sp.dma_start(common_r3[k:k + 1, :], r_part[0:1, k, :]).then_inc(w_p3, 16)
                    sp.wait_ge(w_p3, 48)

                @block.scalar
                def _(act):
                    act.wait_ge(w_a0, 1)
                    nc.scalar.activation(ex[:, :, :], l[:, :, :], ACT.Exp).then_inc(w_e, 1)

                @block.tensor
                def _(pe):
                    pe.wait_ge(w_s, 1)
                    nc.tensor.matmul(psum[0][:, 0:NS], ones[:, :], acc[:, :], start=True, stop=True).then_inc(w_s, 1)

                @block.vector
                def _(dve):
                    v = nc.vector
                    step = Chain(dve, w_d)
                    for s in range(NS):
                        step(v.tensor_scalar(l[:, s, :], logits[:, 1:, s], b2[:, s:s + 1], None, ALU.add))
                    step(v.tensor_tensor(mx[:, :], l[:, 0, :], l[:, 1, :], ALU.max))
                    for s in range(NS):
                        step(v.tensor_tensor(l[:, s, :], l[:, s, :], mx[:, :], ALU.subtract))
                    dve.sem_inc(w_a0, 1)
                    dve.wait_ge(w_e, 1)
                    step(v.tensor_tensor(tot[:, :], ex[:, 0, :], ex[:, 1, :], ALU.add))
                    step(v.reciprocal(tot[:, :], tot[:, :]))
                    step(v.tensor_tensor(tot[:, :], tot[:, :], tile_weight[:, :], ALU.mult))
                    for s in range(NS):
                        step(v.tensor_tensor(ex[:, s, :], ex[:, s, :], tot[:, :], ALU.mult))
                        step(v.reduce_sum(acc[:, s:s + 1], ex[:, s, :], AX))
                    dve.sem_inc(w_s, 1)
                    dve.wait_ge(w_s, 2)
                    step(v.scalar_tensor_tensor(mix[:, :], psum[0][:, 0:NS], 1.0 / N, static_w[:, :],
                                                ALU.mult, ALU.add))
                    step(v.tensor_scalar(mix[:, :], mix[:, :], 0.5, None, ALU.mult))
                    dve.wait_ge(w_t, 16)
                    step(v.tensor_scalar(common_r[:, :], t0[:, 0:C], mix[:, 0:1], None, ALU.mult))
                    step(v.scalar_tensor_tensor(common_r[:, :], t0[:, C:2 * C], mix[:, 1:2], common_r[:, :],
                                                ALU.mult, ALU.add))
                    for k in range(3):
                        for two in range(2):
                            step(v.tensor_copy(r_part[0:1, k, two * C:(two + 1) * C], common_r[0:1, :]))
                        step(v.tensor_tensor(common_r[0:1, :], common_r[0:1, :], r_part[0:1, k, 0:C], ALU.subtract))
                    dve.sem_inc(w_p, 1)

        ot = ExitStack()
        with ot:
            def tb(name, shape, dt=F32):
                return ot.enter_context(nc.sbuf_tensor(name, shape, dt))

            R = 8
            NB = 4
            xin = tb("xin", [P, NB, R, C])
            yout = tb("yout", [P, NB, R, C])
            stats = tb("stats", [P, NB, R, 6])
            mv = tb("mv", [P, NB, R, 2])
            std = tb("std", [P, NB, R])
            rs = tb("rs", [P, NB, R])
            nm = tb("nm", [P, NB, R])
            o_in = [sem(f"o_in{u}") for u in range(NB)]
            o_out = [sem(f"o_out{u}") for u in range(NB)]
            o_sum, o_st, o_mv, o_std, o_rs, o_nm, o_y = map(sem, (
                "o_sum", "o_st", "o_mv", "o_std", "o_rs", "o_nm", "o_y"))
            TURNS = FULL // NB
            xv = x[0:FULL * 8 * P, :].rearrange("(c p r) d -> c p (r d)", p=P, r=R)
            ov = out[0:FULL * 8 * P, :].rearrange("(c p r) d -> c p (r d)", p=P, r=R)
            xr = x[FULL * 8 * P:N, :].rearrange("(p r) d -> p (r d)", p=REST_P)
            orr = out[FULL * 8 * P:N, :].rearrange("(p r) d -> p (r d)", p=REST_P)
            peeled = [(c % NB, TURNS + (c // NB - TURNS), c, P, R) for c in range(TURNS * NB, FULL)]
            peeled.append((FULL % NB, FULL // NB, None, REST_P, REST_R))
            uses = [TURNS + sum(p[0] == u for p in peeled) for u in range(NB)]

            def every(eng, f):
                with eng.Fori(0, TURNS) as i:
                    for u in range(NB):
                        f(u, i, i * NB + u, P, R)
                for p in peeled:
                    f(*p)

            def position(u, i):
                return i * NB + u

            with nc.Block() as block:
                @block.sync
                def _(sp):
                    def load(u, i, c, pp, r):
                        sp.wait_ge(o_sum, position(u, i) + 1)
                        a = xr if c is None else xv[bass.ds(c, 1)].rearrange("a p c -> (a p) c")
                        sp.dma_start(xin[0:pp, u, 0:r, :].rearrange("p r c -> p (r c)"), a).then_inc(o_in[u], 16)
                    every(sp, load)

                @block.gpsimd
                def _(pool):
                    def store(u, i, c, pp, r):
                        pool.wait_ge(o_y, position(u, i) + 3)
                        a = orr if c is None else ov[bass.ds(c, 1)].rearrange("a p c -> (a p) c")
                        pool.sem_inc(pool_passed, 1)
                        pool.dma_start(a, yout[0:pp, u, 0:r, :].rearrange("p r c -> p (r c)")).then_inc(o_out[u], 16)
                    every(pool, store)
                    for u in range(NB):
                        pool.wait_ge(o_out[u], 16 * uses[u])

                def rows_of(u, pp, r):
                    return [(psum[(u % 2) * 4 + j // 2][0:pp, (j % 2) * C:(j % 2 + 1) * C], j) for j in range(r)]

                @block.tensor
                def _(pe):
                    pe.sem_inc(o_sum, NB)

                    def work(u, i, c, pp, r):
                        pe.wait_ge(o_in[u], (i + 1) * 16)
                        pe.wait_ge(o_y, position(u, i) + 1)
                        for j in range(0, r, 2):
                            bank = psum[(u % 2) * 4 + j // 2][0:pp, :]
                            nc.tensor.matmul(bank, ones3[:, 0:pp], common_r3[:, :], start=True, stop=False)
                            last = nc.tensor.matmul(bank, ident[0:pp, 0:pp],
                                                    xin[0:pp, u, j:j + 2, :].rearrange("p r c -> p (r c)"),
                                                    start=False, stop=True)
                        last.then_inc(o_sum, 1)
                    every(pe, work)

                @block.vector
                def _(dve):
                    v = nc.vector

                    def work(u, i, c, pp, r):
                        n = position(u, i)
                        dve.wait_ge(o_sum, n + NB + 1)
                        for y, j in rows_of(u, pp, r):
                            last = v.bn_stats(stats[0:pp, u, j, :], y)
                        last.then_inc(o_st, 1)
                        dve.wait_ge(o_st, n + 1)
                        dve.sem_inc(dve_passed, 1)
                        for j in range(r):
                            last = v.bn_aggr(mv[0:pp, u, j, :], stats[0:pp, u, j, :])
                        last.then_inc(o_mv, 1)
                        dve.wait_ge(o_std, n + 1)
                        v.reciprocal(rs[0:pp, u, 0:r], std[0:pp, u, 0:r]).then_inc(o_rs, 1)
                        dve.wait_ge(o_rs, n + 1)
                        v.scalar_tensor_tensor(nm[0:pp, u, 0:r], mv[0:pp, u, 0:r, 0], -1.0, rs[0:pp, u, 0:r],
                                               ALU.mult, ALU.mult).then_inc(o_nm, 1)
                    every(dve, work)

                @block.scalar
                def _(act):
                    act.sem_inc(o_y, 2)

                    def work(u, i, c, pp, r):
                        n = position(u, i)
                        act.wait_ge(o_mv, n + 1)
                        nc.scalar.activation(std[0:pp, u, 0:r], mv[0:pp, u, 0:r, 1], ACT.Sqrt, bias=eps_t[0:pp, 0:1])\
                            .then_inc(o_std, 1)
                        act.wait_ge(o_nm, n + 1)
                        act.wait_ge(o_out[u], i * 16)
                        for y, j in rows_of(u, pp, r):
                            last = nc.scalar.activation(yout[0:pp, u, j, :], y, ACT.Identity,
                                                        bias=nm[0:pp, u, j:j + 1], scale=rs[0:pp, u, j:j + 1])
                        last.then_inc(o_y, 1)
                    every(act, work)

        fo = ExitStack()
        with fo:
            def tb(name, shape, dt=F32):
                return fo.enter_context(nc.sbuf_tensor(name, shape, dt))

            U = 8
            xg = tb("xg", [P, U, C])
            tt = tb("tt", [P, U, 2 * C])
            ys = tb("ys", [P, U, C])
            yo = tb("yo", [P, U, C])
            st2 = tb("st2", [P, U, 6])
            mv2 = tb("mv2", [P, U, 2])
            sd2 = tb("sd2", [P, U])
            rs2 = tb("rs2", [P, U])
            nm2 = tb("nm2", [P, U])
            xi = tb("xi", [P, U], I32)
            yi = tb("yi", [P, U], I32)
            f_in = [sem(f"f_in{u}") for u in range(U)]
            f_t = [sem(f"f_t{u}") for u in range(U)]
            f_out = [sem(f"f_out{u}") for u in range(U)]
            f_idx, f_y1, f_y2, f_st, f_mv, f_sd, f_rs, f_nm, f_yo, f_yi = map(sem, (
                "f_idx", "f_y1", "f_y2", "f_st", "f_mv", "f_sd", "f_rs", "f_nm", "f_yo", "f_yi"))
            with nc.Block() as block:
                def turns(eng):
                    return count(eng, 2, LIST // 8)

                @block.sync
                def _(sp):
                    n = turns(sp)
                    with sp.Fori(0, n) as i:
                        for u in range(U):
                            sp.wait_ge(f_y2, i * U + u + 1)
                            sp.dma_start(tt[:, u, :], tiles_v[bass.ds(i * U + u + 2, 1)]
                                         .rearrange("a p c -> (a p) c")).then_inc(f_t[u], 16)

                @block.gpsimd
                def _(pool):
                    n = turns(pool)

                    def gather(u, turn):
                        pool.wait_ge(f_idx, turn * U + u + 1)
                        pool.wait_ge(f_y2, turn * U + u + 1)
                        pool.sem_inc(pool_passed, 1)
                        pool.indirect_dma_start(xg[:, u, :], None, x, bass.IndirectOffsetOnAxis(xi[:, u:u + 1], 0))\
                            .then_inc(f_in[u], 16)
                    for u in range(U):
                        gather(u, 0)
                    with pool.Fori(0, n) as i:
                        for u in range(U):
                            pool.wait_ge(f_yo, i * U + u + 1)
                            pool.wait_ge(f_yi, i * U + u + 1)
                            pool.sem_inc(pool_passed, 1)
                            pool.indirect_dma_start(out, bass.IndirectOffsetOnAxis(yi[:, u:u + 1], 0), yo[:, u, :],
                                                    None, bounds_check=N - 1, oob_is_err=False)\
                                .then_inc(f_out[u], 16)
                            gather(u, i + 1)
                    for u in range(U):
                        pool.wait_ge(f_out[u], n * 16)
                        pool.wait_ge(f_in[u], (n + 1) * 16)
                        pool.sem_inc(pool_passed, 1)

                @block.scalar
                def _(act):
                    n = turns(act)
                    a = nc.scalar
                    for u in range(U):
                        a.copy(xi[:, u:u + 1], x_take[:, u + 1:u + 2]).then_inc(f_idx, 1)
                    with act.Fori(0, n) as i:
                        for u in range(U):
                            t = i * U + u
                            act.wait_ge(f_in[u], (i + 1) * 16)
                            a.copy(xi[:, u:u + 1], x_take[:, bass.ds(t + U + 1, 1)]).then_inc(f_idx, 1)
                            act.wait_ge(f_out[u], i * 16)
                            a.copy(yi[:, u:u + 1], y_put[:, bass.ds(t + 1, 1)]).then_inc(f_yi, 1)
                            act.wait_ge(f_mv, t + 1)
                            a.activation(sd2[:, u:u + 1], mv2[:, u, 1:2], ACT.Sqrt, bias=eps_t[:, 0:1])\
                                .then_inc(f_sd, 1)
                            act.wait_ge(f_nm, t + 1)
                            a.activation(yo[:, u, :], ys[:, u, :], ACT.Identity, bias=nm2[:, u:u + 1],
                                         scale=rs2[:, u:u + 1]).then_inc(f_yo, 1)

                @block.vector
                def _(dve):
                    v = nc.vector
                    n = turns(dve)
                    dve.sem_inc(f_y2, U)
                    with dve.Fori(0, n) as i:
                        for u in range(U):
                            t = i * U + u
                            dve.wait_ge(f_in[u], (i + 1) * 16)
                            dve.wait_ge(f_t[u], (i + 1) * 16)
                            dve.wait_ge(f_yo, i * U)
                            v.scalar_tensor_tensor(ys[:, u, :], tt[:, u, 0:C], mix[:, 0:1], xg[:, u, :],
                                                   ALU.mult, ALU.add).then_inc(f_y1, 1)
                            dve.wait_ge(f_y1, t + 1)
                            v.scalar_tensor_tensor(ys[:, u, :], tt[:, u, C:2 * C], mix[:, 1:2], ys[:, u, :],
                                                   ALU.mult, ALU.add).then_inc(f_y2, 1)
                            dve.wait_ge(f_y2, t + U + 1)
                            v.bn_stats(st2[:, u, :], ys[:, u, :]).then_inc(f_st, 1)
                            dve.wait_ge(f_st, t + 1)
                            dve.sem_inc(dve_passed, 1)
                            v.bn_aggr(mv2[:, u, :], st2[:, u, :]).then_inc(f_mv, 1)
                            dve.wait_ge(f_sd, t + 1)
                            v.reciprocal(rs2[:, u:u + 1], sd2[:, u:u + 1]).then_inc(f_rs, 1)
                            dve.wait_ge(f_rs, t + 1)
                            v.scalar_tensor_tensor(nm2[:, u:u + 1], mv2[:, u, 0:1], -1.0, rs2[:, u:u + 1],
                                                   ALU.mult, ALU.mult).then_inc(f_nm, 1)


_INS = ["x", "src", "dst", "L0_gnn_conv_W", "L0_gnn_conv_b", "L0_gnn_tr_W", "L0_gnn_tr_b", "L0_gnn_ln_g",
        "L0_gnn_ln_b", "L0_gnn_scale_weights", "L0_gnn_attn_W1", "L0_gnn_attn_b1", "L0_gnn_attn_W2",
        "L0_gnn_attn_b2"]


def kernel(**inputs):
    import numpy as _np
    import concourse.bacc as _bacc
    from concourse import mybir as _mybir
    from concourse.bass_utils import run_bass_kernel_spmd as _run

    nc = _bacc.Bacc("TRN2", target_bir_lowering=False, num_devices=1)
    arrays, args = {}, []
    for name in _INS:
        a = _np.ascontiguousarray(inputs[name])
        arrays[f"in_{name}"] = a
        args.append(nc.dram_tensor(f"in_{name}", a.shape, _mybir.dt.from_np(a.dtype), kind="ExternalInput").ap())
    out = nc.dram_tensor("out", inputs["x"].shape, F32, kind="ExternalOutput").ap()
    gnn_kernel(nc, *args, out)
    r = _run(nc, [arrays], core_ids=[0])
    return r.results[0]["out"]
```

```python
from contextlib import ExitStack

import concourse.bass as bass
from concourse import mybir

P = 128
ALU = mybir.AluOpType
ACT = mybir.ActivationFunctionType
F32 = mybir.dt.float32
BF16 = mybir.dt.bfloat16
FP16 = mybir.dt.float16
I32 = mybir.dt.int32
AX = mybir.AxisListType.X

N_EDGES = 20000
EPS = 1e-5
ROW = 260
G = 2
UNROLL = 2
BODY = G * UNROLL


class Chain:

    def __init__(self, eng, sem, base=0):
        self.eng, self.sem, self.base, self.n = eng, sem, base, 0

    def __call__(self, instruction):
        instruction.then_inc(self.sem, 1)
        self.n += 1
        self.eng.wait_ge(self.sem, self.base + self.n)


def gnn_kernel(nc, x, src, dst, conv_W, conv_b, tr_W, tr_b, ln_g, ln_b, scale_w, attn_W1, attn_b1, attn_W2,
               attn_b2, out):
    N, C = x.shape
    E = src.shape[0]
    NS = conv_W.shape[0]
    H = attn_W1.shape[1]
    assert C == 2 * P and H == P and NS == 2
    K = C // P
    BATCHES = -(-E // P)
    TB = -(-BATCHES // P) * P
    HI = -(-N // P)
    LAST = N_EDGES - 1
    PAD = 1 << 17
    assert PAD > N and PAD // P > HI and TB >= BATCHES + 2 * BODY

    E_TRASH = N_EDGES
    E_COLS = -(-(N_EDGES + G * P) // P)
    S_TRASH = P * HI
    S_COMMON = S_TRASH + G * P
    S_ROWS = S_COMMON + P
    LIST = -(-HI // 8) * 8
    TILES = LIST + 16
    T_ROWS = (1 + TILES) * P

    FIXED = 48
    COUNTED = {"edges": 6, "nodes": 11}
    assert BATCHES <= FIXED * (BODY + sum(COUNTED.values())) <= TB
    MOST = max(COUNTED["edges"] + BODY, COUNTED["nodes"])
    ZE, ZN = 23, 4
    ZD = UNROLL * 2
    assert S_ROWS % P == 0 and S_ROWS // P // ZN >= ZD * FIXED
    FULL = N // (8 * P)
    EARLY_X = FULL + 1
    REST = N - FULL * 8 * P
    REST_P = 112
    assert REST % REST_P == 0
    REST_R = REST // REST_P

    ctx = ExitStack()
    with ctx:
        def sb(name, shape, dt=F32):
            return ctx.enter_context(nc.sbuf_tensor(name, shape, dt))

        def sem(name):
            return ctx.enter_context(nc.semaphore(name))

        def dram(name, shape, dt=F32):
            return nc.dram_tensor(name, shape, dt, kind="Internal").ap()

        src_pad = dram("src_pad", [TB, P], I32)
        dst_pad = dram("dst_pad", [TB, P], I32)
        edge_sum = dram("edge_sum", [E_COLS * P, ROW])
        node_sum = dram("node_sum", [S_ROWS, C])
        factors = dram("factors", [S_ROWS, 2])
        spare = dram("spare", [8, 1])
        transformed = dram("transformed", [T_ROWS, 2 * C])

        psum = [ctx.enter_context(nc.psum_tensor(f"bank{i}", [P, 512], F32)) for i in range(8)]

        ident = sb("ident", [P, P])
        ones = sb("ones", [P, P])
        ones3 = sb("ones3", [3, P], BF16)
        zeros_bf = sb("zeros_bf", [P, 512], BF16)
        iota_h = sb("iota_h", [P, HI], FP16)
        key_init = sb("key_init", [P, HI])
        part = sb("part", [P, 1])
        eps_t = sb("eps_t", [P, 1])
        b_a = sb("b_a", [P, 1])
        w2 = sb("w2", [P, NS])
        b2 = sb("b2", [P, NS])
        static_w = sb("static_w", [P, NS])
        common_q = sb("common_q", [P, C])
        BANKS = [(0, 0, 512), (1, 512, HI)]
        sum_take = sb("sum_take", [P, TILES], I32)
        x_take = sb("x_take", [P, TILES], I32)
        y_put = sb("y_put", [P, TILES], I32)
        tile_weight = sb("tile_weight", [P, TILES])
        logits = sb("logits", [P, 1 + TILES, NS])
        counts_i = sb("counts_i", [1, 5], I32)
        mix = sb("mix", [P, NS])
        common_r = sb("common_r", [P, C])
        common_r3 = sb("common_r3", [3, 2 * C], BF16)

        rows_scope = ctx.enter_context(ExitStack())

        def rows_only(name, shape, dt=F32):
            return rows_scope.enter_context(nc.sbuf_tensor(name, shape, dt))

        w_h = rows_only("w_h", [P, K, NS * C])
        bias3 = rows_only("bias3", [3, NS * C], BF16)
        w_a = rows_only("w_a", [P, K, H])
        gain = rows_only("gain", [P, NS * C])
        shift = rows_only("shift", [P, NS * C])
        before = rows_only("before", [P, G, G, P])
        earlier = rows_only("earlier", [P, P])

        sums_only = ctx.enter_context(ExitStack())

        def early(name, shape, dt=F32):
            return sums_only.enter_context(nc.sbuf_tensor(name, shape, dt))

        own_hi = early("own_hi", [P, TB])
        own_lo = early("own_lo", [P, TB])
        is_live = early("is_live", [P, TB])
        edge_row = early("edge_row", [P, TB])
        edge_off = early("edge_off", [P, TB])
        node_row = early("node_row", [P, TB])
        node_off = early("node_off", [P, TB])
        dst_key = early("dst_key", [P, TB])
        src_key = early("src_key", [P, TB])
        src_take = early("src_take", [P, TB], I32)
        dst_take = early("dst_take", [P, TB], I32)
        zero_rows = early("zero_rows", [P, ZE * ROW])
        one_hi = early("one_hi", [P, MOST, HI], BF16)
        one_lo = early("one_lo", [P, MOST, P], BF16)
        live_lo = early("live_lo", [P, BODY, P], BF16)

        passed = sem("passed")

        setup = ExitStack()
        with setup:
            def tb(name, shape, dt=F32):
                return setup.enter_context(nc.sbuf_tensor(name, shape, dt))

            raw = [tb("src_raw", [P, TB // P, P], I32), tb("dst_raw", [P, TB // P, P], I32)]
            rawf = [tb("src_rawf", [P, TB // P, P]), tb("dst_rawf", [P, TB // P, P])]
            tmp_i = tb("tmp_i", [P, TB], I32)
            tmp_j = tb("tmp_j", [P, TB], I32)
            tmp_f = tb("tmp_f", [P, TB])
            trash_i = tb("trash_i", [P, TB // G, G], I32)
            trash = tb("trash", [P, TB])
            batch_i = tb("batch_i", [P, TB], I32)
            hi_i = tb("hi_i", [P, HI], I32)
            part_i = tb("part_i", [P, 1], I32)
            cw = tb("cw", [P, NS, K, C])
            cwT = tb("cwT", [P, NS, K, C])
            tw = tb("tw", [P, NS, K, C])
            aw = tb("aw", [P, K, H])
            cb = tb("cb", [P, NS, K])
            cbB = tb("cbB", [P, NS, K, P])
            cb_sum = tb("cb_sum", [P, K])
            hb = tb("hb", [P, NS * C])
            hb_row = tb("hb_row", [P, NS * C])
            hb_part = tb("hb_part", [1, 3, NS * C], BF16)
            ab1 = tb("ab1", [P, 1])
            small = tb("small", [P, 16])
            sw = tb("sw", [P, NS])

            s_cleared, s_raw, s_padded, s_rawf, s_tr, s_tab = map(sem, (
                "s_cleared", "s_raw", "s_padded", "s_rawf", "s_tr", "s_tab"))
            s_wl, s_iota, s_wT, s_wTc, s_prod, s_dve, s_last, s_b3 = map(sem, (
                "s_wl", "s_iota", "s_wT", "s_wTc", "s_prod", "s_dve", "s_last", "s_b3"))
            s_pool, s_exp, s_parts, s_lastT, s_zero, s_einit = map(sem, (
                "s_pool", "s_exp", "s_parts", "s_lastT", "s_zero", "s_einit"))
            WHOLE = BATCHES - 1
            TAIL = E - WHOLE * P
            with nc.Block() as block:
                @block.sync
                def _(sp):
                    sp.wait_ge(s_cleared, 2)
                    n = 0
                    for t, a in zip(raw, (src, dst)):
                        chunks = WHOLE // P
                        sp.dma_start(t[:, 0:chunks, :], a[0:chunks * P * P].rearrange("(c r e) -> r c e", r=P, e=P))\
                          .then_inc(s_raw, 16)
                        more = WHOLE - chunks * P
                        sp.dma_start(t[0:more, chunks, :],
                                     a[chunks * P * P:WHOLE * P].rearrange("(r e) -> r e", e=P)).then_inc(s_raw, 16)
                        sp.dma_start(t[more:more + 1, chunks, 0:TAIL],
                                     a[WHOLE * P:E].rearrange("(r e) -> r e", r=1)).then_inc(s_raw, 16)
                        n += 3
                    sp.wait_ge(s_raw, 16 * n)
                    for t, d in zip(raw, (src_pad, dst_pad)):
                        sp.dma_start(d.rearrange("(c r) e -> r c e", r=P), t[:, :, :]).then_inc(s_padded, 16)
                    sp.wait_ge(s_zero, 1)
                    edge_v = edge_sum.rearrange("(p r) c -> p r c", p=P)
                    spans = [(lo, min(E_COLS, lo + ZE)) for lo in range(0, E_COLS, ZE)]
                    for lo, hi in spans:
                        sp.dma_start(edge_v[:, lo:hi, :],
                                     zero_rows[:, 0:(hi - lo) * ROW].rearrange("p (r c) -> p r c", c=ROW))\
                          .then_inc(s_einit, 16)
                    sp.wait_ge(s_parts, 1)
                    for k in range(3):
                        sp.dma_start(bias3[k:k + 1, :], hb_part[0:1, k, :]).then_inc(s_b3, 16)
                    sp.wait_ge(s_b3, 48)
                    sp.wait_ge(s_padded, 32)
                    sp.wait_ge(s_einit, 16 * len(spans))

                @block.scalar
                def _(act):
                    act.dma_start(cw[:, :, :, :], conv_W.rearrange("s (k p) c -> p s k c", p=P)).then_inc(s_wl, 16)
                    act.dma_start(tw[:, :, :, :], tr_W.rearrange("s (k p) c -> p s k c", p=P)).then_inc(s_wl, 16)
                    act.dma_start(aw[:, :, :], attn_W1.rearrange("(k p) h -> p k h", p=P)).then_inc(s_wl, 16)
                    act.dma_start(w2[:, :], attn_W2).then_inc(s_wl, 16)
                    with nc.allow_non_contiguous_dma(reason="small bias columns"):
                        act.dma_start(cb[:, :, :], conv_b.rearrange("s (k p) -> p s k", p=P)).then_inc(s_wl, 16)
                        act.dma_start(ab1[:, :], attn_b1.rearrange("(p a) -> p a", a=1)).then_inc(s_wl, 16)

                    def rows(t, a):
                        act.dma_start(t[:, :], a.to_broadcast([P, a.shape[1]])).then_inc(s_wl, 16)

                    flat = "s c -> (s c)"
                    rows(hb, tr_b.rearrange(flat).rearrange("(a n) -> a n", a=1))
                    rows(gain, ln_g.rearrange(flat).rearrange("(a n) -> a n", a=1))
                    rows(shift, ln_b.rearrange(flat).rearrange("(a n) -> a n", a=1))
                    rows(b2, attn_b2.rearrange("(a n) -> a n", a=1))
                    rows(sw, scale_w.rearrange("(a n) -> a n", a=1))
                    act.wait_ge(s_exp, 1)
                    nc.scalar.activation(small[:, 8:8 + NS], small[:, 4:4 + NS], ACT.Exp).then_inc(s_exp, 1)

                WL = 16 * 11

                @block.gpsimd
                def _(pool):
                    step = Chain(pool, s_pool)
                    nc.gpsimd.memset(raw[0][:, :, :], PAD).then_inc(s_cleared, 1)
                    nc.gpsimd.memset(raw[1][:, :, :], PAD).then_inc(s_cleared, 1)
                    nc.gpsimd.memset(zero_rows[:, :], 0.0).then_inc(s_zero, 1)
                    step(nc.gpsimd.memset(ident[:, :], 0.0))
                    step(nc.gpsimd.affine_select(out=ident[:, :], in_=ident[:, :], compare_op=ALU.not_equal, fill=1.0,
                                                 base=0, pattern=[[-1, P]], channel_multiplier=1))
                    step(nc.gpsimd.memset(ones[:, :], 1.0))
                    step(nc.gpsimd.memset(ones3[:, :], 1.0))
                    step(nc.gpsimd.memset(zeros_bf[:, :], 0.0))
                    step(nc.gpsimd.affine_select(out=earlier[:, :], in_=ones[:, :], compare_op=ALU.is_gt, fill=0.0,
                                                 base=0, pattern=[[-1, P]], channel_multiplier=1))
                    step(nc.gpsimd.memset(before[:, :, :, :], 0.0))
                    for b in range(G):
                        for f in range(b + 1):
                            step(nc.gpsimd.tensor_copy(before[:, b, f, :], earlier[:, :] if f == b else ones[:, :]))
                    step(nc.gpsimd.iota(hi_i[:, :], pattern=[[1, HI]], base=0, channel_multiplier=0))
                    step(nc.gpsimd.tensor_copy(iota_h[:, :], hi_i[:, :]))
                    step(nc.gpsimd.iota(part_i[:, :], pattern=[[0, 1]], base=0, channel_multiplier=1))
                    step(nc.gpsimd.tensor_copy(part[:, :], part_i[:, :]))
                    step(nc.gpsimd.iota(batch_i[:, :], pattern=[[1, TB]], base=1, channel_multiplier=0))
                    step(nc.gpsimd.iota(trash_i[:, :, :], pattern=[[0, TB // G], [P, G]], base=0,
                                        channel_multiplier=1))
                    step(nc.gpsimd.memset(eps_t[:, :], EPS))
                    step(nc.gpsimd.memset(logits[:, :, :], 0.0))
                    nc.gpsimd.tensor_copy(trash[:, :], trash_i[:, :, :].rearrange("p a b -> p (a b)"))\
                        .then_inc(s_iota, 1)

                @block.tensor
                def _(pe):
                    pe.wait_ge(s_iota, 1)
                    for j in range(2):
                        pe.wait_ge(s_rawf, j + 1)
                        for c in range(TB // P):
                            last = nc.tensor.transpose(psum[2 * j + c // 4][:, (c % 4) * P:(c % 4 + 1) * P],
                                                       rawf[j][:, c, :], ident[:, :])
                        last.then_inc(s_tr, 1)
                    pe.wait_ge(s_wl, WL)
                    for s in range(NS):
                        for k in range(K):
                            for m in range(K):
                                last = nc.tensor.transpose(psum[4 + s][:, m * C + k * P:m * C + (k + 1) * P],
                                                           cw[:, s, k, m * P:(m + 1) * P], ident[:, :])
                    last.then_inc(s_wT, 1)
                    pe.wait_ge(s_wTc, 1)
                    pe.wait_ge(s_tab, 2)
                    for k in range(K):
                        for s in range(NS):
                            for m in range(K):
                                last = nc.tensor.matmul(psum[k][:, s * C:(s + 1) * C],
                                                        cwT[:, s, m, k * P:(k + 1) * P], tw[:, s, m, :],
                                                        start=(m == 0), stop=(m == K - 1))
                    for k in range(K):
                        for n in range(NS * K):
                            s, m = n // K, n % K
                            last = nc.tensor.matmul(psum[2][:, k * H:(k + 1) * H],
                                                    cwT[:, s, m, k * P:(k + 1) * P], aw[:, m, :],
                                                    start=(n == 0), stop=(n == NS * K - 1))
                    for s in range(NS):
                        for m in range(K):
                            last = nc.tensor.matmul(psum[3][:, s * C:(s + 1) * C], cbB[:, s, m, :], tw[:, s, m, :],
                                                    start=(m == 0), stop=(m == K - 1))
                    for m in range(K):
                        last = nc.tensor.matmul(psum[6][:, 0:1], aw[:, m, :], cb_sum[:, m:m + 1],
                                                start=(m == 0), stop=(m == K - 1))
                    last.then_inc(s_prod, 1)
                    pe.wait_ge(s_last, 1)
                    nc.tensor.matmul(psum[7][0:1, 0:P], small[:, 0:1], ident[:, :], start=True, stop=True)\
                        .then_inc(s_lastT, 1)

                @block.vector
                def _(dve):
                    v = nc.vector
                    step = Chain(dve, s_dve)
                    dve.wait_ge(s_raw, 96)
                    for j in range(2):
                        v.tensor_copy(rawf[j][:, :, :], raw[j][:, :, :]).then_inc(s_rawf, 1)
                    dve.wait_ge(s_iota, 1)
                    for j, t in enumerate((src_key, dst_key)):
                        dve.wait_ge(s_tr, j + 1)
                        for h in range(TB // 512):
                            step(v.tensor_copy(t[:, h * 512:(h + 1) * 512], psum[2 * j + h][:, :]))
                        dve.sem_inc(s_tab, 1)
                    dve.wait_ge(s_wT, 1)
                    for s in range(NS):
                        step(v.tensor_copy(cwT[:, s, :, :], psum[4 + s][:, :].rearrange("p (m c) -> p m c", c=C)))
                        for m in range(K):
                            step(v.tensor_scalar(cbB[:, s, m, :], ones[:, :], cb[:, s, m:m + 1], None, ALU.mult))
                    step(v.tensor_tensor(cb_sum[:, :], cb[:, 0, :], cb[:, 1, :], ALU.add))
                    dve.sem_inc(s_wTc, 1)
                    step(v.tensor_scalar(edge_off[:, :], trash[:, :], float(E_TRASH), None, ALU.add))
                    step(v.tensor_tensor(tmp_f[:, :], edge_off[:, :], dst_key[:, :], ALU.subtract))
                    step(v.tensor_scalar(is_live[:, :], dst_key[:, :], float(N_EDGES), None, ALU.is_lt))
                    step(v.tensor_tensor(tmp_f[:, :], tmp_f[:, :], is_live[:, :], ALU.mult))
                    step(v.tensor_tensor(edge_row[:, :], edge_off[:, :], tmp_f[:, :], ALU.subtract))
                    step(v.tensor_copy(edge_off[:, :], tmp_f[:, :]))
                    step(v.tensor_copy(tmp_f[:, :], batch_i[:, :]))
                    step(v.tensor_tensor(tmp_f[:, :], tmp_f[:, :], is_live[:, :], ALU.mult))
                    step(v.reduce_max(small[:, 0:1], tmp_f[:, :], AX))
                    dve.sem_inc(s_last, 1)
                    step(v.tensor_scalar(is_live[:, :], dst_key[:, :], float(LAST), None, ALU.is_lt))
                    step(v.tensor_copy(tmp_i[:, :], src_key[:, :]))
                    step(v.tensor_scalar(tmp_j[:, :], tmp_i[:, :], 7, None, ALU.arith_shift_right))
                    step(v.tensor_copy(own_hi[:, :], tmp_j[:, :]))
                    step(v.tensor_scalar(tmp_j[:, :], tmp_i[:, :], P - 1, None, ALU.bitwise_and))
                    step(v.tensor_copy(own_lo[:, :], tmp_j[:, :]))
                    step(v.scalar_tensor_tensor(node_row[:, :], own_lo[:, :], float(HI), own_hi[:, :],
                                                ALU.mult, ALU.add))
                    step(v.tensor_scalar(trash[:, :], trash[:, :], float(S_TRASH), None, ALU.add))
                    step(v.tensor_tensor(tmp_f[:, :], trash[:, :], node_row[:, :], ALU.subtract))
                    step(v.tensor_scalar(node_off[:, :], src_key[:, :], float(N), None, ALU.is_lt))
                    step(v.tensor_tensor(node_off[:, :], node_off[:, :], tmp_f[:, :], ALU.mult))
                    step(v.tensor_tensor(node_row[:, :], trash[:, :], node_off[:, :], ALU.subtract))
                    step(v.tensor_scalar(src_take[:, :], src_key[:, :], float(N - 1), None, ALU.min))
                    step(v.tensor_scalar(dst_take[:, :], dst_key[:, :], float(LAST), None, ALU.min))
                    dve.wait_ge(s_lastT, 1)
                    step(v.reduce_max(small[0:1, 1:2], psum[7][0:1, 0:P], AX))
                    step(v.tensor_scalar(small[0:1, 1:2], small[0:1, 1:2], float((FIXED + 1) * BODY),
                                         float(BODY - 1), ALU.max, ALU.add))
                    step(v.tensor_copy(counts_i[0:1, 1:2], small[0:1, 1:2]))
                    step(v.tensor_scalar(counts_i[0:1, 0:1], counts_i[0:1, 1:2], BODY.bit_length() - 1, None,
                                         ALU.arith_shift_right))
                    dve.wait_ge(s_prod, 1)
                    step(v.tensor_tensor(hb[:, :], hb[:, :], psum[3][:, :], ALU.add))
                    for s in range(NS):
                        cols = slice(s * C, (s + 1) * C)
                        for k in range(K + 1):
                            row = psum[k][:, cols] if k < K else hb[:, cols]
                            to = w_h[:, k, cols] if k < K else hb_row[:, cols]
                            step(v.reduce_sum(small[:, 2:3], row, AX))
                            step(v.tensor_scalar(small[:, 3:4], small[:, 2:3], 1.0 / C, None, ALU.mult))
                            step(v.tensor_scalar(to, row, small[:, 3:4], None, ALU.subtract))
                    for k in range(3):
                        step(v.tensor_copy(hb_part[0:1, k, :], hb_row[0:1, :]))
                        step(v.tensor_tensor(hb_row[0:1, :], hb_row[0:1, :], hb_part[0:1, k, :], ALU.subtract))
                    dve.sem_inc(s_parts, 1)
                    step(v.tensor_scalar(w_a[:, :, :], psum[2][:, 0:K * H].rearrange("p (k h) -> p k h", h=H),
                                         1.0 / NS, None, ALU.mult))
                    step(v.scalar_tensor_tensor(b_a[:, :], psum[6][:, 0:1], 1.0 / NS, ab1[:, :], ALU.mult, ALU.add))
                    step(v.reduce_max(small[:, 2:3], sw[:, :], AX))
                    step(v.tensor_scalar(small[:, 4:4 + NS], sw[:, :], small[:, 2:3], None, ALU.subtract))
                    dve.sem_inc(s_exp, 1)
                    dve.wait_ge(s_exp, 2)
                    step(v.reduce_sum(small[:, 2:3], small[:, 8:8 + NS], AX))
                    step(v.reciprocal(small[:, 3:4], small[:, 2:3]))
                    step(v.tensor_scalar(static_w[:, :], small[:, 8:8 + NS], small[:, 3:4], None, ALU.mult))

        def count(eng, j, most, least=1):
            return eng.value_load(counts_i[0:1, j:j + 1], min_val=least, max_val=most)

        def start_at_16(pool, sems):
            for k, s in enumerate(sems):
                pool.dma_start(spare[k:k + 1, :], eps_t[0:1, 0:1]).then_inc(s, 16)
            for s in sems:
                pool.wait_ge(s, 16)

        BODIES = -(-BATCHES // BODY)

        def segment_sums(name, keys_dram, key, table, take, row, off, target, from_edges):
            st = ExitStack()
            with st:
                def tb(nm, shape, dt=F32):
                    return st.enter_context(nc.sbuf_tensor(f"{name}_{nm}", shape, dt))

                def sm(nm):
                    return sem(f"{name}_{nm}")

                taken = tb("taken", [P, UNROLL, G, ROW])
                merged = tb("merged", [P, UNROLL, G, ROW])
                key_rows = tb("key_rows", [P, UNROLL, G * P], I32)
                equal = tb("equal", [P, UNROLL, G, G * P])
                junk = tb("junk", [P, UNROLL, G, G * P])
                repeats = tb("repeats", [P, UNROLL, G])
                shiftf = tb("shiftf", [P, UNROLL, G])
                factor = tb("factor", [P, UNROLL, G])
                put_idx = tb("put_idx", [P, UNROLL, G], I32)
                take_idx = tb("take_idx", [P, UNROLL, G], I32)
                cols = C if from_edges else ROW
                counted = COUNTED[name]
                counted_from = FIXED * (BODY + (COUNTED["edges"] if from_edges else 0))
                own = 0 if from_edges else BODY

                def one_hots(i, u, fixed):
                    items = [(i * BODY + k, True, fixed) for k in range(own)]
                    items += [(i * counted + counted_from + k, False, True) for k in range(counted)] if fixed else []
                    first = i * len(items) if fixed else (i - FIXED) * len(items) + FIXED * (own + counted)
                    return [(first + k, k, *items[k]) for k in range(len(items))
                            if (k >= -(-len(items) // 2)) == bool(u)]

                def both(eng, n, turn):
                    with eng.Fori(0, FIXED) as i:
                        turn(i, True)
                    with eng.Fori(FIXED, n) as i:
                        turn(i, False)

                def turns(eng):
                    return count(eng, 0, BODIES + 1, FIXED + 1)

                keys_in = [sm(f"keys_in{u}") for u in range(UNROLL)]
                gathered = [sm(f"gathered{u}") for u in range(UNROLL)]
                added = [sm(f"added{u}") for u in range(UNROLL)]
                take_ready = [sm(f"take_ready{u}") for u in range(UNROLL)]
                hot, hot_used, zeroed, adding = sm("hot"), sm("hot_used"), sm("zeroed"), sm("adding")
                equal_ready, put_ready, products, evacuated, steps, cleared, offset = map(sm, (
                    "equal_ready", "put_ready", "products", "evacuated", "steps", "cleared", "offset"))
                with nc.Block() as block:
                    @block.sync
                    def _(sp):
                        n = turns(sp)
                        node_v = node_sum.rearrange("(p r) c -> p (r c)", p=P)
                        zero_dmas = S_ROWS // P // ZN

                        def zero(at, rows):
                            sp.dma_start(node_v[:, bass.ds(at * C, rows * C)], zero_rows[:, 0:rows * C])\
                              .then_inc(zeroed, 16)

                        def turn(i, fixed):
                            for u in range(UNROLL):
                                g = i * UNROLL + u
                                sp.wait_ge(put_ready, g + 1)
                                sp.dma_start(key_rows[:, u, :],
                                             keys_dram[bass.ds(g * G, G), :].rearrange("g p -> (g p)")
                                             .rearrange("(a n) -> a n", a=1).to_broadcast([P, G * P]))\
                                  .then_inc(keys_in[u], 16)
                                if fixed and not from_edges:
                                    sp.wait_ge(adding, g + 1)
                                for z in range(ZD // UNROLL if fixed and not from_edges else 0):
                                    zero((g * (ZD // UNROLL) + z) * ZN, ZN)

                        both(sp, n, turn)
                        if not from_edges:
                            for k in range(FIXED * ZD, zero_dmas):
                                zero(k * ZN, ZN)
                            if S_ROWS // P % ZN:
                                zero(zero_dmas * ZN, S_ROWS // P % ZN)
                            sp.wait_ge(zeroed, 16 * -(-S_ROWS // P // ZN))

                    @block.scalar
                    def _(act):
                        n = turns(act)
                        act.sem_inc(evacuated, UNROLL)
                        for u in range(UNROLL):
                            nc.scalar.copy(take_idx[:, u, :], take[:, u * G:(u + 1) * G]).then_inc(take_ready[u], 1)
                        act.wait_ge(cleared, 2)
                        def turn(i, fixed):
                            for u in range(UNROLL):
                                g = i * UNROLL + u
                                act.wait_ge(gathered[u], (i + 1) * 16 * G)
                                nc.scalar.copy(take_idx[:, u, :], take[:, bass.ds((g + UNROLL) * G, G)])\
                                    .then_inc(take_ready[u], 1)
                                act.wait_ge(products, g + UNROLL + 1)
                                act.wait_ge(added[u], i * 16 * G + 16)
                                for b in range(G):
                                    last = nc.scalar.copy(merged[:, u, b, 0:cols], psum[u * G + b][:, 0:cols])
                                last.then_inc(evacuated, 1)

                        both(act, n, turn)

                    @block.tensor
                    def _(pe):
                        n = turns(pe)
                        pe.sem_inc(products, UNROLL)
                        if not from_edges:
                            for b in range(4, 8):
                                nc.tensor.matmul(psum[b][:, :], zeros_bf[:, 0:P], zeros_bf[:, :], start=True,
                                                 stop=False, skip_group_check=True)
                        pe.sem_inc(hot_used, own + counted)

                        def turn(i, fixed):
                            for u in range(UNROLL):
                                g = i * UNROLL + u
                                pe.wait_ge(gathered[u], (i + 1) * 16 * G)
                                pe.wait_ge(equal_ready, g + 1)
                                pe.wait_ge(evacuated, g + 1)
                                for b in range(G):
                                    for f in range(G):
                                        last = nc.tensor.matmul(psum[u * G + b][:, 0:cols],
                                                                equal[:, u, f, b * P:(b + 1) * P],
                                                                taken[:, u, f, 0:cols],
                                                                start=(f == 0), stop=(f == G - 1))
                                last.then_inc(products, 1)
                                for o, k, _, live, every in one_hots(i, u, fixed):
                                    pe.wait_ge(hot, o + 1)
                                    for lo_part, bank in [(one_lo, 4)] * every + [(live_lo, 6)] * live:
                                        for b, lo, hi in BANKS:
                                            last = nc.tensor.matmul(psum[bank + b][:, 0:hi - lo], lo_part[:, k, :],
                                                                    one_hi[:, k, lo:hi], start=False, stop=False,
                                                                    skip_group_check=True)
                                    last.then_inc(hot_used, 1)

                        both(pe, n, turn)
                        if from_edges:
                            for b in range(4, 8):
                                nc.tensor.matmul(psum[b][:, :], zeros_bf[:, 0:P], zeros_bf[:, :], start=False,
                                                 stop=True, skip_group_check=True)

                    @block.vector
                    def _(dve):
                        v = nc.vector
                        n = turns(dve)
                        dve.sem_inc(put_ready, UNROLL)
                        per_group = 4 if from_edges else 1

                        def one_hot(item, fixed):
                            if item is None:
                                return
                            o, k, b, live, every = item
                            dve.wait_ge(hot_used, o + 1 + (0 if fixed else counted))
                            lo = own_lo[:, bass.ds(b, 1)]
                            if live:
                                v.tensor_scalar(live_lo[:, k, :], iota_h[:, 0:P], lo, is_live[:, bass.ds(b, 1)],
                                                ALU.is_equal, ALU.mult)
                            if every:
                                v.tensor_scalar(one_lo[:, k, :], iota_h[:, 0:P], lo, None, ALU.is_equal)
                            v.tensor_scalar(one_hi[:, k, :], iota_h[:, :], own_hi[:, bass.ds(b, 1)], None,
                                            ALU.is_equal).then_inc(hot, 1)

                        def turn(i, fixed):
                            for u in range(UNROLL):
                                g = i * UNROLL + u
                                pair = bass.ds(g * G, G)
                                items = one_hots(i, u, fixed)

                                def between(n=1):
                                    for _ in range(n):
                                        one_hot(items.pop(0) if items else None, fixed)

                                if from_edges:
                                    dve.wait_ge(gathered[u], (i + 1) * 16 * G)
                                    v.tensor_scalar(factor[:, u, :], taken[:, u, :, C], 1.0, None, ALU.max)\
                                        .then_inc(steps, 1)
                                    between()
                                    dve.wait_ge(steps, g * 4 + 1)
                                    v.reciprocal(factor[:, u, :], factor[:, u, :]).then_inc(steps, 1)
                                    between()
                                    dve.wait_ge(steps, g * 4 + 2)
                                    v.tensor_tensor(factor[:, u, :], factor[:, u, :], is_live[:, pair], ALU.mult)\
                                        .then_inc(steps, 1)
                                dve.wait_ge(keys_in[u], (i + 1) * 16)
                                for b in range(G):
                                    w = (b + 1) * P
                                    last = v.scalar_tensor_tensor(
                                        junk[:, u, b, 0:w], key_rows[:, u, 0:w], key[:, bass.ds(g * G + b, 1)],
                                        before[:, b, :, :].rearrange("p a b -> p (a b)")[:, 0:w],
                                        ALU.is_equal, ALU.mult, accum_out=repeats[:, u, b:b + 1])
                                last.then_inc(steps, 1)
                                if from_edges:
                                    dve.wait_ge(steps, g * 4 + 3)
                                dve.wait_ge(products, g + 1)
                                for f in range(G):
                                    k = key[:, bass.ds(g * G + f, 1)]
                                    if from_edges:
                                        last = v.tensor_scalar(equal[:, u, f, :], key_rows[:, u, :], k,
                                                               factor[:, u, f:f + 1], ALU.is_equal, ALU.mult)
                                    else:
                                        last = v.tensor_scalar(equal[:, u, f, :], key_rows[:, u, :], k, None,
                                                               ALU.is_equal)
                                last.then_inc(equal_ready, 1)
                                dve.wait_ge(steps, (g + 1) * per_group)
                                v.scalar_tensor_tensor(shiftf[:, u, :], repeats[:, u, :], 1.0, off[:, pair],
                                                       ALU.min, ALU.mult).then_inc(offset, 1)
                                between()
                                dve.wait_ge(offset, g + 1)
                                dve.wait_ge(added[u], i * 16 * G + 16)
                                v.tensor_tensor(put_idx[:, u, :], shiftf[:, u, :], row[:, pair], ALU.add)\
                                    .then_inc(put_ready, 1)
                                between(len(items))

                        both(dve, n, turn)

                    @block.gpsimd
                    def _(pool):
                        n = turns(pool)
                        pool.sem_inc(adding, 2)
                        nc.gpsimd.memset(merged[:, :, :, :], 0.0).then_inc(cleared, 1)
                        nc.gpsimd.memset(taken[:, :, :, :], 0.0).then_inc(cleared, 1)
                        pool.wait_ge(cleared, 2)
                        if not from_edges:
                            nc.gpsimd.memset(taken[:, :, :, C:C + 1], 1.0).then_inc(cleared, 1)
                            pool.wait_ge(cleared, 3)

                        def gather(u, turn):
                            pool.wait_ge(take_ready[u], turn + 1)
                            for b in range(G):
                                pool.sem_inc(passed, 1)
                                pool.indirect_dma_start(
                                    taken[:, u, b, 0:table.shape[1]], None, table,
                                    bass.IndirectOffsetOnAxis(take_idx[:, u, b:b + 1], 0)).then_inc(gathered[u], 16)

                        for u in range(UNROLL):
                            gather(u, 0)
                        start_at_16(pool, added)
                        def turn(i, fixed):
                            for u in range(UNROLL):
                                g = i * UNROLL + u
                                pool.wait_ge(products, g + UNROLL + 1)
                                gather(u, i + 1)
                                pool.wait_ge(evacuated, g + UNROLL + 1)
                                pool.wait_ge(put_ready, g + UNROLL + 1)
                                if fixed and not from_edges:
                                    pool.sem_inc(adding, 1)
                                if u:
                                    pool.wait_ge(added[u - 1], (i + 1) * 16 * G + 16)
                                else:
                                    pool.wait_ge(added[UNROLL - 1], i * 16 * G + 16)
                                for b in range(G):
                                    pool.sem_inc(passed, 1)
                                    pool.indirect_dma_start(
                                        target, bass.IndirectOffsetOnAxis(put_idx[:, u, b:b + 1], 0),
                                        merged[:, u, b, 0:cols], None, compute_op=ALU.add).then_inc(added[u], 16)

                        both(pool, n, turn)
                        for u in range(UNROLL):
                            pool.wait_ge(gathered[u], (n + 1) * 16 * G)
                            pool.wait_ge(added[u], n * 16 * G + 16)
                            pool.sem_inc(passed, 1)

        segment_sums("edges", dst_pad, dst_key, x, src_take, edge_row, edge_off, edge_sum, False)
        segment_sums("nodes", src_pad, src_key, edge_sum, dst_take, node_row, node_off, node_sum, True)

        sums_only.close()

        ls = ExitStack()
        with ls:
            def tb(name, shape, dt=F32):
                return ls.enter_context(nc.sbuf_tensor(name, shape, dt))

            total = tb("total", [P, HI])
            live = tb("live", [P, HI])
            common_deg = tb("common_deg", [P, HI])
            pair = tb("pair", [P, HI, 2])
            flag = tb("flag", [P, HI])
            keys = tb("keys", [P, 2, HI])
            listed = tb("listed", [P, TILES])
            top = tb("top", [P, 2, 8])
            dsm = tb("dsm", [P, 8])
            common_pair = tb("common_pair", [P, 2])
            valid = tb("valid", [P, TILES])
            l_step, l_top, l_count, l_sums, l_key, l_factors, l_pair = map(sem, (
                "l_step", "l_top", "l_count", "l_sums", "l_key", "l_factors", "l_pair"))
            with nc.Block() as block:
                @block.vector
                def _(dve):
                    v = nc.vector
                    step = Chain(dve, l_step)
                    for b, lo, hi in BANKS:
                        step(v.tensor_copy(total[:, lo:hi], psum[4 + b][:, 0:hi - lo]))
                        step(v.tensor_copy(live[:, lo:hi], psum[6 + b][:, 0:hi - lo]))
                    step(v.tensor_scalar(flag[:, :], total[:, :], 0.5, None, ALU.is_lt))
                    step(v.scalar_tensor_tensor(flag[:, :], live[:, :], 0.5, flag[:, :], ALU.is_gt, ALU.max))
                    dve.wait_ge(l_key, 2)
                    step(v.tensor_tensor(keys[:, 0, :], flag[:, :], key_init[:, :], ALU.mult))
                    step(v.tensor_scalar(flag[:, :], keys[:, 0, :], 0.5, None, ALU.is_gt))
                    step(v.reduce_sum(dsm[:, 0:1], flag[:, :], AX))
                    dve.sem_inc(l_count, 1)
                    step(v.tensor_tensor(pair[:, :, 1], total[:, :], live[:, :], ALU.subtract))
                    step(v.tensor_scalar(total[:, :], total[:, :], 1.0, None, ALU.max))
                    step(v.reciprocal(pair[:, :, 0], total[:, :]))
                    dve.sem_inc(l_pair, 1)
                    step(v.memset(listed[:, :], 0.0))
                    dve.wait_ge(l_sums, 1)
                    step(v.reduce_max(dsm[0:1, 1:2], psum[0][0:1, 0:P], AX))
                    step(v.tensor_scalar(dsm[0:1, 3:4], dsm[0:1, 1:2], float(EARLY_X), 7.0, ALU.max, ALU.add))
                    step(v.tensor_copy(counts_i[0:1, 3:4], dsm[0:1, 3:4]))
                    step(v.tensor_scalar(counts_i[0:1, 2:3], counts_i[0:1, 3:4], 3, None, ALU.arith_shift_right))
                    step(v.tensor_scalar(counts_i[0:1, 4:5], counts_i[0:1, 2:3], EARLY_X // 8, None, ALU.subtract))
                    step(v.tensor_scalar(dsm[0:1, 3:4], dsm[0:1, 1:2], 1.0, 15.0, ALU.max, ALU.add))
                    step(v.tensor_copy(counts_i[0:1, 3:4], dsm[0:1, 3:4]))
                    step(v.tensor_scalar(counts_i[0:1, 1:2], counts_i[0:1, 3:4], 4, None, ALU.arith_shift_right))
                    sixteens = count(dve, 1, LIST // 16)
                    with dve.Fori(0, sixteens) as i:
                        pick = Chain(dve, l_top, i * 4)
                        for h in range(2):
                            dve.sem_inc(passed, 1)
                            pick(v.max(top[:, h, :], keys[:, h, :]))
                            v.tensor_copy(listed[:, bass.ds(i * 16 + h * 8 + 1, 8)], top[:, h, :])
                            dve.sem_inc(passed, 1)
                            pick(v.match_replace(keys[:, 1 - h, :], top[:, h, :], keys[:, h, :], 0.0))
                    step(v.tensor_scalar(valid[:, :], listed[:, :], 0.5, None, ALU.is_gt))
                    step(v.tensor_scalar(listed[:, :], listed[:, :], 1.0, 0.0, ALU.subtract, ALU.max))
                    step(v.tensor_scalar(dsm[:, 4:5], part[:, :], float(HI), None, ALU.mult))
                    step(v.tensor_scalar(sum_take[:, :], listed[:, :], dsm[:, 4:5], None, ALU.add))
                    step(v.tensor_scalar(listed[:, :], listed[:, :], float(P), part[:, 0:1], ALU.mult, ALU.add))
                    step(v.tensor_copy(x_take[:, :], listed[:, :]))
                    step(v.tensor_scalar(tile_weight[:, :], valid[:, :], float(-PAD), float(PAD), ALU.mult, ALU.add))
                    step(v.tensor_tensor(y_put[:, :], listed[:, :], tile_weight[:, :], ALU.add))
                    step(v.tensor_copy(tile_weight[:, :], valid[:, :]))
                    step(v.memset(sum_take[:, 0:1], S_COMMON))
                    dve.wait_ge(l_sums, 2)
                    step(v.tensor_scalar(tile_weight[:, 0:1], psum[1][:, 0:1], -1.0 / P, float(N) / P,
                                         ALU.mult, ALU.add))

                @block.tensor
                def _(pe):
                    pe.wait_ge(l_count, 1)
                    nc.tensor.matmul(psum[0][0:1, 0:P], dsm[:, 0:1], ident[:, :], start=True, stop=True)\
                        .then_inc(l_sums, 1)
                    nc.tensor.matmul(psum[1][:, 0:1], ones[:, :], dsm[:, 0:1], start=True, stop=True)\
                        .then_inc(l_sums, 1)

                @block.gpsimd
                def _(pool):
                    nc.gpsimd.iota(key_init[:, :], pattern=[[1, HI]], base=1, channel_multiplier=0,
                                   allow_small_or_imprecise_dtypes=True).then_inc(l_key, 1)
                    pool.wait_ge(l_key, 1)
                    nc.gpsimd.affine_select(out=key_init[:, :], in_=key_init[:, :], compare_op=ALU.is_gt, fill=0.0,
                                            base=N, pattern=[[-P, HI]], channel_multiplier=-1).then_inc(l_key, 1)
                    nc.gpsimd.memset(common_pair[:, :], 1.0).then_inc(l_pair, 1)

                @block.sync
                def _(sp):
                    sp.wait_ge(l_pair, 2)
                    sp.dma_start(factors[0:S_TRASH, :].rearrange("(p r) c -> p (r c)", p=P),
                                 pair[:, :, :].rearrange("p r c -> p (r c)")).then_inc(l_factors, 16)
                    for r in range(S_TRASH, S_ROWS, P):
                        sp.dma_start(factors[r:r + P, :], common_pair[:, :]).then_inc(l_factors, 16)
                    sp.wait_ge(l_factors, 16 * (2 + G))

        rt = ExitStack()
        with rt:
            def tb(name, shape, dt=F32):
                return rt.enter_context(nc.sbuf_tensor(name, shape, dt))

            UT = 4
            sums = tb("sums", [P, UT, C])
            fac = tb("fac", [P, UT, 2])
            q = tb("q", [P, UT, C])
            qT = tb("qT", [P, 2, K, P])
            aT = tb("aT", [P, 2, P])
            sq = tb("sq", [P, 2, NS * C])
            ssq = tb("ssq", [P, 2, NS])
            inv = tb("inv", [P, 2, NS])
            tr = tb("tr", [P, 2, NS * C])
            res = tb("res", [P, 2, NS * C])
            sidx = tb("sidx", [P, UT], I32)
            last_row = tb("last_row", [P, ROW])
            cfac = tb("cfac", [P, 1])
            sum_in = [sem(f"sum_in{u}") for u in range(UT)]
            fac_in = [sem(f"fac_in{u}") for u in range(UT)]
            res_out = [sem("res_out0"), sem("res_out1")]
            (t_idx, t_qa, t_q, t_tp, t_qT, t_h, t_aT, t_lg, t_lgc, t_ssq, t_std, t_inv, t_sc, t_sh, t_res, t_row,
             t_cq, t_at, t_clear) = map(sem, (
                "t_idx", "t_qa", "t_q", "t_tp", "t_qT", "t_h", "t_aT", "t_lg", "t_lgc", "t_ssq", "t_std", "t_inv",
                "t_sc", "t_sh", "t_res", "t_row", "t_cq", "t_at", "t_clear"))
            tiles_v = transformed.rearrange("(t p) c -> t p c", p=P)

            with nc.Block() as block:
                def turns(eng):
                    return count(eng, 2, LIST // 8, -(-EARLY_X // 8)) * (8 // UT) + 1

                @block.sync
                def _(sp):
                    n = turns(sp)
                    sp.dma_start(last_row[:, :], edge_sum[LAST:LAST + 1, :].to_broadcast([P, ROW])).then_inc(t_row, 16)

                    def store(t, w):
                        sp.wait_ge(t_res, t + 2)
                        sp.dma_start(tiles_v[bass.ds(t, 1), :, :].rearrange("a p c -> (a p) c"), res[:, w, :])\
                          .then_inc(res_out[w], 16)

                    with sp.Fori(0, n) as i:
                        for u in range(UT):
                            store(i * UT + u, 1 - u % 2)
                    store(n * UT, 1)
                    sp.wait_ge(res_out[0], n * (UT // 2 * 16) + 1)
                    sp.sem_inc(passed, 1)
                    sp.wait_ge(res_out[1], n * (UT // 2 * 16) + 17)
                    sp.sem_inc(passed, 1)

                @block.gpsimd
                def _(pool):
                    n = turns(pool)
                    nc.gpsimd.memset(aT[:, :, :], 0.0).then_inc(t_clear, 1)
                    nc.gpsimd.memset(tr[:, :, :], 0.0).then_inc(t_clear, 1)

                    def gather(u, t):
                        pool.wait_ge(t_idx, t + 1)
                        pool.sem_inc(passed, 1)
                        pool.indirect_dma_start(sums[:, u, :], None, node_sum,
                                                bass.IndirectOffsetOnAxis(sidx[:, u:u + 1], 0))\
                            .then_inc(sum_in[u], 16)
                        pool.indirect_dma_start(fac[:, u, :], None, factors,
                                                bass.IndirectOffsetOnAxis(sidx[:, u:u + 1], 0))\
                            .then_inc(fac_in[u], 16)

                    for u in range(UT):
                        gather(u, u)
                    with pool.Fori(0, n) as i:
                        for u in range(UT):
                            t = i * UT + u
                            pool.wait_ge(t_q, t + 1)
                            gather(u, t + UT)
                    for u in range(UT):
                        pool.wait_ge(sum_in[u], (n + 1) * 16)
                        pool.wait_ge(fac_in[u], (n + 1) * 16)
                    pool.sem_inc(passed, 1)

                @block.scalar
                def _(act):
                    n = turns(act)
                    a = nc.scalar

                    def transposed(t, w):
                        act.wait_ge(t_tp, t + 2)
                        a.copy(qT[:, w, :, :], psum[w][:, 0:C].rearrange("p (k n) -> p k n", n=P)).then_inc(t_qT, 1)

                    def finish(t, w, used):
                        act.wait_ge(t_sh, t + 2)
                        act.wait_ge(res_out[w], used * 16 + 1)
                        a.activation(res[:, w, :], tr[:, w, :], ACT.Relu).then_inc(t_res, 1)

                    for s in [t_res, t_qT, t_aT, *res_out]:
                        act.sem_inc(s, 1)
                    a.activation(ssq[:, 0, 0:1], eps_t[:, 0:1], ACT.Sqrt).then_inc(t_clear, 1)
                    for u in range(UT):
                        a.copy(sidx[:, u:u + 1], sum_take[:, u:u + 1]).then_inc(t_idx, 1)
                    act.wait_ge(t_clear, 3)
                    transposed(0, 0)
                    with act.Fori(0, n) as i:
                        for b in range(UT):
                            t = i * UT + b
                            u = b % 2
                            act.wait_ge(sum_in[b], (i + 1) * 16)
                            act.wait_ge(fac_in[b], (i + 1) * 16)
                            a.copy(sidx[:, b:b + 1], sum_take[:, bass.ds(t + UT, 1)]).then_inc(t_idx, 1)
                            act.wait_ge(t_h, t + 1)
                            transposed(t + 1, 1 - u)
                            act.wait_ge(t_at, t + 1)
                            a.activation(aT[:, u, :], psum[4 + u][:, 0:P], ACT.Relu, bias=b_a[:, 0:1])\
                                .then_inc(t_aT, 1)
                            act.wait_ge(t_h, t + 2)
                            for s in range(NS):
                                last = a.activation(sq[:, u, s * C:(s + 1) * C], psum[2 + u][:, s * C:(s + 1) * C],
                                                    ACT.Square, accum_out=ssq[:, u, s:s + 1])
                            last.then_inc(t_ssq, 1)
                            act.wait_ge(t_ssq, t + 1)
                            a.activation(ssq[:, u, :], ssq[:, u, :], ACT.Sqrt, bias=eps_t[:, 0:1], scale=1.0 / C)\
                                .then_inc(t_std, 1)
                            finish(t, 1 - u, i * (UT // 2) + b // 2)
                    finish(n * UT, 1, n * (UT // 2))

                @block.vector
                def _(dve):
                    v = nc.vector
                    n = turns(dve)
                    dve.sem_inc(t_sh, 2)
                    dve.sem_inc(t_lgc, 2)
                    step = Chain(dve, t_cq)
                    dve.wait_ge(t_row, 16)
                    step(v.tensor_scalar(cfac[:, :], last_row[:, C:C + 1], 1.0, None, ALU.max))
                    step(v.reciprocal(cfac[:, :], cfac[:, :]))
                    step(v.tensor_scalar(common_q[:, :], last_row[:, 0:C], cfac[:, 0:1], None, ALU.mult))

                    def sum_all(t, b, i):
                        dve.wait_ge(sum_in[b], (i + 1) * 16)
                        dve.wait_ge(fac_in[b], (i + 1) * 16)
                        v.scalar_tensor_tensor(q[:, b, :], common_q[:, :], fac[:, b, 1:2],
                                               sums[:, b, :], ALU.mult, ALU.add).then_inc(t_qa, 1)

                    def divide(t, b):
                        dve.wait_ge(t_qa, t + 1)
                        v.tensor_scalar(q[:, b, :], q[:, b, :], fac[:, b, 0:1], None, ALU.mult)\
                            .then_inc(t_q, 1)

                    def take_logits(t, w):
                        dve.wait_ge(t_lg, t + 1)
                        v.tensor_copy(logits[:, bass.ds(t, 1), :].rearrange("p a s -> p (a s)"),
                                      psum[6 + w][:, 0:NS]).then_inc(t_lgc, 1)

                    for b in range(3):
                        sum_all(b, b, 0)
                        divide(b, b)
                    with dve.Fori(0, n) as i:
                        for b in range(UT):
                            t = i * UT + b
                            u = b % 2
                            ahead = (t + 3, (b + 3) % UT)
                            take_logits(t, 1 - u)
                            dve.wait_ge(t_std, t + 1)
                            v.reciprocal(inv[:, u, :], ssq[:, u, :]).then_inc(t_inv, 1)
                            dve.wait_ge(t_tp, t + 1)
                            sum_all(*ahead, i + (b + 3) // UT)
                            dve.wait_ge(t_inv, t + 1)
                            dve.wait_ge(t_res, t + 1)
                            for s in range(NS):
                                c = slice(s * C, (s + 1) * C)
                                last = v.scalar_tensor_tensor(tr[:, u, c], psum[2 + u][:, c], inv[:, u, s:s + 1],
                                                              gain[:, c], ALU.mult, ALU.mult)
                            last.then_inc(t_sc, 1)
                            divide(*ahead)
                            dve.wait_ge(t_sc, t + 1)
                            v.tensor_tensor(tr[:, u, :], tr[:, u, :], shift[:, :], ALU.add).then_inc(t_sh, 1)
                    take_logits(n * UT, 1)

                @block.tensor
                def _(pe):
                    n = turns(pe)
                    m = nc.tensor

                    def turn_rows(t, b):
                        w = b % 2
                        pe.wait_ge(t_q, t + 1)
                        for k in range(K):
                            last = m.transpose(psum[w][:, k * P:(k + 1) * P], q[:, b, k * P:(k + 1) * P], ident[:, :])
                        last.then_inc(t_tp, 1)

                    def attend(t, w):
                        pe.wait_ge(t_aT, t + 1)
                        pe.wait_ge(t_lgc, t + 1)
                        m.matmul(psum[6 + w][:, 0:NS], aT[:, w, :], w2[:, :], start=True, stop=True)\
                            .then_inc(t_lg, 1)

                    for s in [t_h, t_tp]:
                        pe.sem_inc(s, 1)
                    pe.wait_ge(t_clear, 3)
                    turn_rows(0, 0)
                    with pe.Fori(0, n) as i:
                        for b in range(UT):
                            t = i * UT + b
                            u = b % 2
                            pe.wait_ge(t_qT, t + 1)
                            turn_rows(t + 1, (b + 1) % UT)
                            attend(t, 1 - u)
                            pe.wait_ge(t_qT, t + 2)
                            for k in range(K):
                                last = m.matmul(psum[4 + u][:, 0:P], w_a[:, k, :], qT[:, u, k, :], start=(k == 0),
                                                stop=(k == K - 1))
                            last.then_inc(t_at, 1)
                            pe.wait_ge(t_sh, t + 1)
                            m.matmul(psum[2 + u][:, :], ones3[:, :], bias3[:, :], start=True, stop=False)
                            for k in range(K):
                                last = m.matmul(psum[2 + u][:, :], qT[:, u, k, :], w_h[:, k, :], start=False,
                                                stop=(k == K - 1))
                            last.then_inc(t_h, 1)
                    attend(n * UT, 1)

        wt = ExitStack()
        with wt:
            def tb(name, shape, dt=F32):
                return wt.enter_context(nc.sbuf_tensor(name, shape, dt))

            l = tb("l", [P, NS, TILES])
            mx = tb("mx", [P, TILES])
            ex = tb("ex", [P, NS, TILES])
            tot = tb("tot", [P, TILES])
            acc = tb("acc", [P, NS])
            t0 = tb("t0", [P, NS * C])
            r_part = tb("r_part", [1, 3, 2 * C], BF16)
            w_d, w_a0, w_e, w_s, w_t, w_p = map(sem, ("w_d", "w_a0", "w_e", "w_s", "w_t", "w_p"))
            w_p3 = sem("w_p3")
            with nc.Block() as block:
                @block.sync
                def _(sp):
                    sp.dma_start(t0[:, :], transformed[P:2 * P, :]).then_inc(w_t, 16)
                    sp.wait_ge(w_p, 1)
                    for k in range(3):
                        sp.dma_start(common_r3[k:k + 1, :], r_part[0:1, k, :]).then_inc(w_p3, 16)
                    sp.wait_ge(w_p3, 48)

                @block.scalar
                def _(act):
                    act.wait_ge(w_a0, 1)
                    nc.scalar.activation(ex[:, :, :], l[:, :, :], ACT.Exp).then_inc(w_e, 1)

                @block.tensor
                def _(pe):
                    pe.wait_ge(w_s, 1)
                    nc.tensor.matmul(psum[0][:, 0:NS], ones[:, :], acc[:, :], start=True, stop=True).then_inc(w_s, 1)

                @block.vector
                def _(dve):
                    v = nc.vector
                    step = Chain(dve, w_d)
                    for s in range(NS):
                        step(v.tensor_scalar(l[:, s, :], logits[:, 1:, s], b2[:, s:s + 1], None, ALU.add))
                    step(v.tensor_tensor(mx[:, :], l[:, 0, :], l[:, 1, :], ALU.max))
                    for s in range(NS):
                        step(v.tensor_tensor(l[:, s, :], l[:, s, :], mx[:, :], ALU.subtract))
                    dve.sem_inc(w_a0, 1)
                    dve.wait_ge(w_e, 1)
                    step(v.tensor_tensor(tot[:, :], ex[:, 0, :], ex[:, 1, :], ALU.add))
                    step(v.reciprocal(tot[:, :], tot[:, :]))
                    step(v.tensor_tensor(tot[:, :], tot[:, :], tile_weight[:, :], ALU.mult))
                    for s in range(NS):
                        step(v.tensor_tensor(ex[:, s, :], ex[:, s, :], tot[:, :], ALU.mult))
                        step(v.reduce_sum(acc[:, s:s + 1], ex[:, s, :], AX))
                    dve.sem_inc(w_s, 1)
                    dve.wait_ge(w_s, 2)
                    step(v.scalar_tensor_tensor(mix[:, :], psum[0][:, 0:NS], 1.0 / N, static_w[:, :],
                                                ALU.mult, ALU.add))
                    step(v.tensor_scalar(mix[:, :], mix[:, :], 0.5, None, ALU.mult))
                    dve.wait_ge(w_t, 16)
                    step(v.tensor_scalar(common_r[:, :], t0[:, 0:C], mix[:, 0:1], None, ALU.mult))
                    step(v.scalar_tensor_tensor(common_r[:, :], t0[:, C:2 * C], mix[:, 1:2], common_r[:, :],
                                                ALU.mult, ALU.add))
                    for k in range(3):
                        for two in range(2):
                            step(v.tensor_copy(r_part[0:1, k, two * C:(two + 1) * C], common_r[0:1, :]))
                        step(v.tensor_tensor(common_r[0:1, :], common_r[0:1, :], r_part[0:1, k, 0:C], ALU.subtract))
                    dve.sem_inc(w_p, 1)

        rows_scope.close()

        late = ctx.enter_context(ExitStack())
        NB = 4
        x_early = late.enter_context(nc.sbuf_tensor("x_early", [P, NB + EARLY_X, C], F32))
        ot = ExitStack()
        with ot:
            def tb(name, shape, dt=F32):
                return ot.enter_context(nc.sbuf_tensor(name, shape, dt))

            R = 8
            xin = tb("xin", [P, NB, R, C])
            yout = tb("yout", [P, NB, R, C])
            stats = tb("stats", [P, 4, R // 2, 6])
            mv = tb("mv", [P, 4, R // 2, 2])
            std = tb("std", [P, 4, R // 2])
            rs = tb("rs", [P, 4, R // 2])
            nm = tb("nm", [P, 4, R // 2])
            o_table = sem("o_table")
            xe = tb("xe", [P, NB], I32)
            xs = tb("xs", [P, NB, C])
            o_x = [sem(f"o_x{u}") for u in range(NB)]
            o_xe = sem("o_xe")
            o_in = [sem(f"o_in{u}") for u in range(NB)]
            o_out = [sem(f"o_out{u}") for u in range(NB)]
            o_sum, o_st, o_mv, o_std, o_rs, o_nm, o_y = map(sem, (
                "o_sum", "o_st", "o_mv", "o_std", "o_rs", "o_nm", "o_y"))
            TURNS = FULL // NB
            xv = x[0:FULL * 8 * P, :].rearrange("(c p r) d -> c p (r d)", p=P, r=R)
            ov = out[0:FULL * 8 * P, :].rearrange("(c p r) d -> c p (r d)", p=P, r=R)
            xr = x[FULL * 8 * P:N, :].rearrange("(p r) d -> p (r d)", p=REST_P)
            orr = out[FULL * 8 * P:N, :].rearrange("(p r) d -> p (r d)", p=REST_P)
            peeled = [(c % NB, TURNS + (c // NB - TURNS), c, P, R) for c in range(TURNS * NB, FULL)]
            peeled.append((FULL % NB, FULL // NB, None, REST_P, REST_R))
            uses = [TURNS + sum(p[0] == u for p in peeled) for u in range(NB)]

            def every(eng, f):
                with eng.Fori(0, TURNS) as i:
                    for u in range(NB):
                        f(u, i, i * NB + u, P, R)
                for p in peeled:
                    f(*p)

            HR = R // 2

            def halves(u, i, pp, r):
                return [(u, i, h, pp, min(HR, r - h * HR)) for h in range(2)]

            def number(u, i, h):
                return (i * NB + u) * 2 + h

            def slot(u, h):
                return (2 * u + h) % 4

            def banks(half):
                u, _, h, pp, r = half
                return [psum[slot(u, h) * 2 + j // 2][0:pp, (j % 2) * C:(j % 2 + 1) * C] for j in range(r)]

            def each_half(eng, work):
                before = None
                for u in range(NB):
                    for half in halves(u, 0, P, R):
                        work(half, before)
                        before = half
                with eng.Fori(1, TURNS) as i:
                    before = (NB - 1, i - 1, 1, P, HR)
                    for u in range(NB):
                        for half in halves(u, i, P, R):
                            work(half, before)
                            before = half
                before = (NB - 1, TURNS - 1, 1, P, HR)
                for u, i, _, pp, r in peeled:
                    for half in halves(u, i, pp, r):
                        work(half, before)
                        before = half
                work(None, before)

            with nc.Block() as block:
                @block.sync
                def _(sp):
                    def load(u, i, c, pp, r):
                        sp.wait_ge(o_sum, number(u, i, 0) + 2)
                        a = xr if c is None else xv[bass.ds(c, 1)].rearrange("a p c -> (a p) c")
                        sp.dma_start(xin[0:pp, u, 0:r, :].rearrange("p r c -> p (r c)"), a).then_inc(o_in[u], 16)
                    every(sp, load)

                @block.gpsimd
                def _(pool):
                    def store(u, i, c, pp, r):
                        pool.wait_ge(o_y, number(u, i, 0) + 2 + 4)
                        a = orr if c is None else ov[bass.ds(c, 1)].rearrange("a p c -> (a p) c")
                        pool.sem_inc(passed, 1)
                        pool.dma_start(a, yout[0:pp, u, 0:r, :].rearrange("p r c -> p (r c)")).then_inc(o_out[u], 16)
                        c = FULL if c is None else c
                        pool.wait_ge(o_x[u], i * 16 + 16)
                        nc.gpsimd.tensor_copy(x_early[:, bass.ds(c, 1), :].rearrange("p a c -> p (a c)"),
                                              xs[:, u, :])
                        nc.gpsimd.tensor_copy(xe[:, u:u + 1], x_take[:, bass.ds(c + 1, 1)]).then_inc(o_xe, 1)
                        pool.wait_ge(o_xe, i * NB + u + 2)
                        pool.sem_inc(passed, 1)
                        pool.indirect_dma_start(xs[:, u, :], None, x,
                                                bass.IndirectOffsetOnAxis(xe[:, u:u + 1], 0)).then_inc(o_x[u], 16)
                    nc.gpsimd.memset(xs[:, :, :], 0.0).then_inc(o_xe, 1)
                    start_at_16(pool, o_out + o_x)
                    pool.wait_ge(o_xe, 1)
                    every(pool, store)
                    for t in range(EARLY_X - NB, EARLY_X):
                        u = t % NB
                        pool.wait_ge(o_x[u], 16 * len(range(u, EARLY_X, NB)) + 16)
                        nc.gpsimd.tensor_copy(x_early[:, t + NB, :], xs[:, u, :])
                    for u in range(NB):
                        pool.wait_ge(o_out[u], 16 * uses[u] + 16)

                @block.tensor
                def _(pe):
                    pe.sem_inc(o_sum, 2 * NB)

                    def work(half, before):
                        if half is None:
                            return
                        u, i, h, pp, r = half
                        pe.wait_ge(o_in[u], (i + 1) * 16)
                        pe.wait_ge(o_y, number(u, i, h) + 1)
                        for j in range(0, r, 2):
                            bank = psum[slot(u, h) * 2 + j // 2][0:pp, :]
                            nc.tensor.matmul(bank, ones3[:, 0:pp], common_r3[:, :], start=True, stop=False)
                            last = nc.tensor.matmul(bank, ident[0:pp, 0:pp],
                                                    xin[0:pp, u, h * HR + j:h * HR + j + 2, :]
                                                    .rearrange("p r c -> p (r c)"), start=False, stop=True)
                        last.then_inc(o_sum, 1)
                    each_half(pe, work)

                @block.vector
                def _(dve):
                    v = nc.vector

                    def work(half, before):
                        if half is not None:
                            u, i, h, pp, r = half
                            n, q = number(u, i, h), slot(u, h)
                            dve.wait_ge(o_sum, n + 2 * NB + 1)
                            for j, y in enumerate(banks(half)):
                                last = v.bn_stats(stats[0:pp, q, j, :], y)
                            last.then_inc(o_st, 1)
                        if before is not None:
                            bu, bi, bh, bp, br = before
                            bn, bq = number(bu, bi, bh), slot(bu, bh)
                            dve.wait_ge(o_std, bn + 1)
                            v.reciprocal(rs[0:bp, bq, 0:br], std[0:bp, bq, 0:br]).then_inc(o_rs, 1)
                        if half is not None:
                            dve.wait_ge(o_st, n + 1)
                            dve.sem_inc(passed, 1)
                            for j in range(r):
                                last = v.bn_aggr(mv[0:pp, q, j, :], stats[0:pp, q, j, :])
                            last.then_inc(o_mv, 1)
                        if before is not None:
                            dve.wait_ge(o_rs, bn + 1)
                            v.scalar_tensor_tensor(nm[0:bp, bq, 0:br], mv[0:bp, bq, 0:br, 0], -1.0,
                                                   rs[0:bp, bq, 0:br], ALU.mult, ALU.mult).then_inc(o_nm, 1)
                    each_half(dve, work)

                @block.scalar
                def _(act):
                    act.sem_inc(o_y, 4)
                    nc.scalar.activation(std[:, 0, 0:1], eps_t[:, 0:1], ACT.Sqrt).then_inc(o_table, 1)
                    act.wait_ge(o_table, 1)

                    def work(half, before):
                        if half is not None:
                            u, i, h, pp, r = half
                            q = slot(u, h)
                            act.wait_ge(o_mv, number(u, i, h) + 1)
                            nc.scalar.activation(std[0:pp, q, 0:r], mv[0:pp, q, 0:r, 1], ACT.Sqrt,
                                                 bias=eps_t[0:pp, 0:1]).then_inc(o_std, 1)
                        if before is not None:
                            u, i, h, pp, r = before
                            q = slot(u, h)
                            act.wait_ge(o_nm, number(u, i, h) + 1)
                            act.wait_ge(o_out[u], i * 16 + 16)
                            for j, y in enumerate(banks(before)):
                                last = nc.scalar.activation(yout[0:pp, u, h * HR + j, :], y, ACT.Identity,
                                                            bias=nm[0:pp, q, j:j + 1], scale=rs[0:pp, q, j:j + 1])
                            last.then_inc(o_y, 1)
                    each_half(act, work)

        fo = ExitStack()
        with fo:
            def tb(name, shape, dt=F32):
                return fo.enter_context(nc.sbuf_tensor(name, shape, dt))

            U = 8
            xg = tb("xg", [P, U, C])
            tt = tb("tt", [P, U, 2 * C])
            ys = tb("ys", [P, U, C])
            yo = tb("yo", [P, U, C])
            st2 = tb("st2", [P, U, 6])
            mv2 = tb("mv2", [P, U, 2])
            sd2 = tb("sd2", [P, U])
            rs2 = tb("rs2", [P, U])
            nm2 = tb("nm2", [P, U])
            xi = tb("xi", [P, U], I32)
            yi = tb("yi", [P, U], I32)
            f_in = [sem(f"f_in{u}") for u in range(U)]
            f_t = [sem(f"f_t{u}") for u in range(U)]
            f_out = [sem(f"f_out{u}") for u in range(U)]
            f_idx, f_y1, f_y2, f_st, f_mv, f_sd, f_rs, f_nm, f_yo = map(sem, (
                "f_idx", "f_y1", "f_y2", "f_st", "f_mv", "f_sd", "f_rs", "f_nm", "f_yo"))
            FIRST = EARLY_X // U
            assert FIRST * U + 2 == EARLY_X
            with nc.Block() as block:
                def turns(eng):
                    return count(eng, 4, LIST // 8 - FIRST)

                @block.sync
                def _(sp):
                    n = turns(sp) + FIRST

                    def load(u, i):
                        sp.wait_ge(f_y2, i * U + u + 1)
                        sp.dma_start(tt[:, u, :], tiles_v[bass.ds(i * U + u + 2, 1)]
                                     .rearrange("a p c -> (a p) c")).then_inc(f_t[u], 16)
                    with sp.Fori(0, n) as i:
                        for u in range(U):
                            load(u, i)
                    load(0, n)
                    load(1, n)

                @block.gpsimd
                def _(pool):
                    more = turns(pool)

                    def gather(u, k):
                        pool.wait_ge(f_idx, k * U + u + 1)
                        if k is not 0:
                            pool.wait_ge(f_y2, (k + FIRST) * U + u + 1)
                        pool.sem_inc(passed, 1)
                        pool.indirect_dma_start(xg[:, u, :], None, x, bass.IndirectOffsetOnAxis(xi[:, u:u + 1], 0))\
                            .then_inc(f_in[u], 16)
                    def scatter(u, i):
                        pool.wait_ge(f_yo, (i + 1) * U + u + 1)
                        pool.sem_inc(passed, 1)
                        pool.indirect_dma_start(out, bass.IndirectOffsetOnAxis(yi[:, u:u + 1], 0), yo[:, u, :],
                                                None, bounds_check=N - 1, oob_is_err=False)\
                            .then_inc(f_out[u], 16)

                    start_at_16(pool, f_out)
                    for u in range(U):
                        gather(u, 0)
                    with pool.Fori(0, FIRST) as i:
                        for u in range(U):
                            scatter(u, i)
                    with pool.Fori(0, more) as k:
                        for u in range(U):
                            scatter(u, k + FIRST)
                            gather(u, k + 1)
                    for u in range(U):
                        pool.wait_ge(f_out[u], (more + FIRST) * 16 + 16)
                        pool.wait_ge(f_in[u], (more + 1) * 16)
                        pool.sem_inc(passed, 1)

                @block.scalar
                def _(act):
                    more = turns(act)
                    a = nc.scalar

                    def deviation(p, u):
                        act.wait_ge(f_mv, p + 1)
                        a.activation(sd2[:, u:u + 2], mv2[:, u:u + 2, 1], ACT.Sqrt, bias=eps_t[:, 0:1])\
                            .then_inc(f_sd, 1)

                    for u in range(U):
                        a.copy(xi[:, u:u + 1], x_take[:, FIRST * U + u + 1:FIRST * U + u + 2]).then_inc(f_idx, 1)
                    act.sem_inc(f_yo, U)
                    deviation(0, 0)

                    def turn(i, k):
                        for h in range(0, U, 2):
                            p = i * (U // 2) + h // 2
                            for u in (h, h + 1):
                                t = i * U + u
                                if k is not None:
                                    act.wait_ge(f_in[u], (k + 1) * 16)
                                    a.copy(xi[:, u:u + 1], x_take[:, bass.ds(t + U + 1, 1)]).then_inc(f_idx, 1)
                                act.wait_ge(f_out[u], i * 16 + 16)
                                a.copy(yi[:, u:u + 1], y_put[:, bass.ds(t + 1, 1)])
                            act.wait_ge(f_nm, p + 1)
                            for u in (h, h + 1):
                                a.activation(yo[:, u, :], ys[:, u, :], ACT.Identity, bias=nm2[:, u:u + 1],
                                             scale=rs2[:, u:u + 1]).then_inc(f_yo, 1)
                            deviation(p + 1, (h + 2) % U)

                    with act.Fori(0, FIRST) as i:
                        turn(i, None)
                    with act.Fori(0, more) as k:
                        turn(k + FIRST, k)

                @block.vector
                def _(dve):
                    v = nc.vector
                    more = turns(dve)
                    dve.sem_inc(f_y2, U)

                    def mix_first(t, u, i, k):
                        if k is not None:
                            dve.wait_ge(f_in[u], (k + 1) * 16)
                            x_rows = xg[:, u, :]
                        else:
                            x_rows = x_early[:, bass.ds(t + NB, 1), :].rearrange("p a c -> p (a c)")
                        dve.wait_ge(f_t[u], (i + 1) * 16)
                        dve.wait_ge(f_yo, t + 1)
                        v.scalar_tensor_tensor(ys[:, u, :], tt[:, u, 0:C], mix[:, 0:1], x_rows,
                                               ALU.mult, ALU.add).then_inc(f_y1, 1)

                    def mix_second(t, u):
                        dve.wait_ge(f_y1, t + 1)
                        v.scalar_tensor_tensor(ys[:, u, :], tt[:, u, C:2 * C], mix[:, 1:2], ys[:, u, :],
                                               ALU.mult, ALU.add).then_inc(f_y2, 1)

                    def statistics(p, h):
                        dve.wait_ge(f_y2, p * 2 + U + 2)
                        for u in (h, h + 1):
                            last = v.bn_stats(st2[:, u, :], ys[:, u, :])
                        last.then_inc(f_st, 1)

                    def aggregate(p, h):
                        dve.wait_ge(f_st, p + 1)
                        dve.sem_inc(passed, 1)
                        for u in (h, h + 1):
                            last = v.bn_aggr(mv2[:, u, :], st2[:, u, :])
                        last.then_inc(f_mv, 1)

                    for u in range(2):
                        mix_first(u, u, 0, None)
                    for u in range(2):
                        mix_second(u, u)
                    statistics(0, 0)
                    aggregate(0, 0)

                    def turn(i, k):
                        for h in range(0, U, 2):
                            p = i * (U // 2) + h // 2
                            wrap, b = (h + 2) // U, (h + 2) % U
                            for u in range(2):
                                mix_first(p * 2 + 2 + u, b + u, i + wrap, k if k is None else k + wrap)
                            dve.wait_ge(f_sd, p + 1)
                            v.reciprocal(rs2[:, h:h + 2], sd2[:, h:h + 2]).then_inc(f_rs, 1)
                            for u in range(2):
                                mix_second(p * 2 + 2 + u, b + u)
                            dve.wait_ge(f_rs, p + 1)
                            v.scalar_tensor_tensor(nm2[:, h:h + 2], mv2[:, h:h + 2, 0], -1.0, rs2[:, h:h + 2],
                                                   ALU.mult, ALU.mult).then_inc(f_nm, 1)
                            statistics(p + 1, b)
                            aggregate(p + 1, b)

                    with dve.Fori(0, FIRST) as i:
                        turn(i, None)
                    with dve.Fori(0, more) as k:
                        turn(k + FIRST, k)


_INS = ["x", "src", "dst", "L0_gnn_conv_W", "L0_gnn_conv_b", "L0_gnn_tr_W", "L0_gnn_tr_b", "L0_gnn_ln_g",
        "L0_gnn_ln_b", "L0_gnn_scale_weights", "L0_gnn_attn_W1", "L0_gnn_attn_b1", "L0_gnn_attn_W2",
        "L0_gnn_attn_b2"]


def kernel(**inputs):
    import numpy as _np
    import concourse.bacc as _bacc
    from concourse import mybir as _mybir
    from concourse.bass_utils import run_bass_kernel_spmd as _run

    nc = _bacc.Bacc("TRN2", target_bir_lowering=False, num_devices=1)
    arrays, args = {}, []
    for name in _INS:
        a = _np.ascontiguousarray(inputs[name])
        arrays[f"in_{name}"] = a
        args.append(nc.dram_tensor(f"in_{name}", a.shape, _mybir.dt.from_np(a.dtype), kind="ExternalInput").ap())
    out = nc.dram_tensor("out", inputs["x"].shape, F32, kind="ExternalOutput").ap()
    gnn_kernel(nc, *args, out)
    r = _run(nc, [arrays], core_ids=[0])
    return r.results[0]["out"]
```
